# Optimizing a Trainium2 kernel written in Bass

```python
import numpy as np
import jax
import jax.numpy as jnp

def _softmax(x, axis=-1):
    return jax.nn.softmax(x, axis=axis)

def _gelu(x):
    return jax.nn.gelu(x, approximate=True)

def _silu(x):
    return jax.nn.silu(x)

def _sigmoid(x):
    return jax.nn.sigmoid(x)

def _layernorm(x, axis=-1, eps=1e-05):
    m = jnp.mean(x, axis=axis, keepdims=True)
    v = jnp.var(x, axis=axis, keepdims=True)
    return (x - m) / jnp.sqrt(v + eps)

def _scatter_add(tgt, idx, src, axis=0):
    return tgt.at[idx].add(src)

def _segment_sum(src, seg, n):
    return jax.ops.segment_sum(src, seg, n)
kernel_name = 'mk_adaln_d2_jaxref_r8_5ba522'

def setup_inputs(seed: int=0):
    np.random.seed(seed)
    _w = jnp.asarray

    def _L0_attn_setup():
        import jax, jax.numpy as jnp
        import numpy as np
        B, N, C = (32, 64, 128)
        H = 16
        D = C // H
        MAX_SEQ = 64
        BASE = 10000.0

        def _rope_tables(n, d):
            position = jnp.arange(n, dtype=jnp.float32)[:, None]
            div_term = jnp.exp(jnp.arange(0, d, 2, dtype=jnp.float32) * (-np.log(BASE) / d))
            ang = position * div_term
            return (jnp.sin(ang), jnp.cos(ang))

        def _apply_rope(x, sin, cos):
            x1 = x[..., ::2]
            x2 = x[..., 1::2]
            out = jnp.stack([x1 * cos - x2 * sin, x1 * sin + x2 * cos], axis=-1)
            return out.reshape(*x.shape[:-1], -1)
        key = jax.random.key(seed)
        k1, k2, k3, k4, k5 = jax.random.split(key, 5)
        s = 0.02
        return {'x': jax.random.normal(k1, (B, N, C), dtype=jnp.float32), 'w_qkv': jax.random.normal(k2, (3 * C, C), dtype=jnp.float32) * s, 'b_qkv': jax.random.normal(k3, (3 * C,), dtype=jnp.float32) * s, 'w_lepe': jax.random.normal(k4, (C, 1, 3), dtype=jnp.float32) * s, 'b_lepe': jax.random.normal(k5, (C,), dtype=jnp.float32) * s}
    _L0_attn_in = _L0_attn_setup()

    def _L0_ffn_setup():
        import jax, jax.numpy as jnp
        import numpy as np
        DIM = 128
        DEPTH = 2
        HEADS = 8
        DIM_HEAD = 64
        WINDOW = 64
        INNER = HEADS * DIM_HEAD
        HID = int(DIM * 4 * 2 / 3)
        B, N = (2, 1024)
        QK_SCALE = 8.0

        def shift_token(t):
            t1, t2 = jnp.split(t, 2, axis=-1)
            t2 = jnp.pad(t2, ((0, 0), (1, 0), (0, 0)))[:, :-1]
            return jnp.concatenate([t1, t2], axis=-1)

        def l2norm(t):
            return t / jnp.clip(jnp.linalg.norm(t, axis=-1, keepdims=True), 1e-12)

        def rotate_half(x):
            x1, x2 = jnp.split(x, 2, axis=-1)
            return jnp.concatenate([-x2, x1], axis=-1)

        def rotary_xpos(q, k):
            n = q.shape[-2]
            half_idx = jnp.arange(0, DIM_HEAD, 2, dtype=jnp.float32)
            inv_freq = 1.0 / 10000.0 ** (half_idx / DIM_HEAD)
            t = jnp.arange(n, dtype=jnp.float32)
            freqs = t[:, None] * inv_freq[None, :]
            freqs = jnp.concatenate([freqs, freqs], axis=-1)
            base = (half_idx + 0.4 * DIM_HEAD) / (1.4 * DIM_HEAD)
            power = (t - n // 2) / float(WINDOW // 2)
            scale = base[None, :] ** power[:, None]
            scale = jnp.concatenate([scale, scale], axis=-1)
            cos, sin = (jnp.cos(freqs), jnp.sin(freqs))
            q = q * cos * scale + rotate_half(q) * sin * scale
            k = k * cos / scale + rotate_half(k) * sin / scale
            return (q, k)

        def local_attention(q, k, v):
            b, h, n, d = q.shape
            w = n // WINDOW
            bq = q.reshape(b, h, w, WINDOW, d) * QK_SCALE
            bk = k.reshape(b, h, w, WINDOW, d)
            bv = v.reshape(b, h, w, WINDOW, d)

            def look_around(t):
                p = jnp.pad(t, ((0, 0), (0, 0), (1, 0), (0, 0), (0, 0)))
                return jnp.concatenate([p[:, :, :w], p[:, :, 1:]], axis=3)
            bk, bv = (look_around(bk), look_around(bv))
            bt = jnp.arange(n).reshape(w, WINDOW)
            btp = jnp.pad(bt, ((1, 0), (0, 0)), constant_values=-1)
            btk = jnp.concatenate([btp[:w], btp[1:]], axis=1)
            sim = jnp.einsum('bhwid,bhwjd->bhwij', bq, bk)
            i = bt[:, :, None]
            j = btk[:, None, :]
            mask = (i < j) | (i > j + WINDOW) | (j == -1)
            sim = jnp.where(mask, -jnp.finfo(sim.dtype).max, sim)
            attn = jax.nn.softmax(sim, axis=-1)
            out = jnp.einsum('bhwij,bhwjd->bhwid', attn, bv)
            return out.reshape(b, h, n, d)

        def _layer(x, wqkv, qs, ksc, wo, lg, lb, w1, b1, w2, b2):
            b, n, _ = x.shape
            h = shift_token(x)
            qkv = h @ wqkv
            q, k, v = jnp.split(qkv, 3, axis=-1)
            to_heads = lambda t: t.reshape(b, n, HEADS, DIM_HEAD).transpose(0, 2, 1, 3)
            q, k, v = (to_heads(q), to_heads(k), to_heads(v))
            q = l2norm(q) * qs
            k = l2norm(k) * ksc
            q, k = rotary_xpos(q, k)
            o = local_attention(q, k, v)
            o = o.transpose(0, 2, 1, 3).reshape(b, n, INNER)
            x = x + o @ wo
            h = shift_token(x)
            mu = h.mean(-1, keepdims=True)
            var = h.var(-1, keepdims=True)
            h = (h - mu) / jnp.sqrt(var + 1e-05) * lg + lb
            h = h @ w1 + b1
            a, g = jnp.split(h, 2, axis=-1)
            h = a * jax.nn.gelu(g, approximate=False)
            x = x + h @ w2 + b2
            return x
        key = jax.random.key(seed)
        ks = jax.random.split(key, 6)
        return {'x': jax.random.normal(ks[0], (B, N, DIM), jnp.float32), 'wqkv': jax.random.normal(ks[1], (DEPTH, DIM, 3 * INNER), jnp.float32) * 0.02, 'q_scale': jnp.ones((DEPTH, DIM_HEAD), jnp.float32), 'k_scale': jnp.ones((DEPTH, DIM_HEAD), jnp.float32), 'wo': jax.random.normal(ks[2], (DEPTH, INNER, DIM), jnp.float32) * 0.02, 'ln_g': jnp.ones((DEPTH, DIM), jnp.float32), 'ln_b': jnp.zeros((DEPTH, DIM), jnp.float32), 'w1': jax.random.normal(ks[3], (DEPTH, DIM, 2 * HID), jnp.float32) * 0.02, 'b1': jnp.zeros((DEPTH, 2 * HID), jnp.float32), 'w2': jax.random.normal(ks[4], (DEPTH, HID, DIM), jnp.float32) * 0.02, 'b2': jnp.zeros((DEPTH, DIM), jnp.float32)}
    _L0_ffn_in = _L0_ffn_setup()
    _L0_c = _w((lambda *s: np.random.randn(*s).astype(np.float32) * 0.05)(2, 128))
    _L0_wmod = _w((lambda *s: np.random.randn(*s).astype(np.float32) * 0.05)(128, 6 * 128) * 128 ** (-0.5))

    def _L1_attn_setup():
        import jax, jax.numpy as jnp
        import numpy as np
        B, S, D, H = (2, 256, 128, 16)
        HD = D // H
        LN_EPS = 1e-05
        key = jax.random.key(seed)
        ks = jax.random.split(key, 8)
        inv = 1.0 / np.sqrt(D)
        return {'embedded': jax.random.normal(ks[0], (B, S, D), dtype=jnp.float32), 'Wq': jax.random.normal(ks[1], (D, D), dtype=jnp.float32) * inv, 'bq': jax.random.normal(ks[2], (D,), dtype=jnp.float32) * 0.01, 'Wk': jax.random.normal(ks[3], (D, D), dtype=jnp.float32) * inv, 'bk': jax.random.normal(ks[4], (D,), dtype=jnp.float32) * 0.01, 'Wv': jax.random.normal(ks[5], (D, D), dtype=jnp.float32) * inv, 'bv': jax.random.normal(ks[6], (D,), dtype=jnp.float32) * 0.01, 'gamma': jnp.ones((D,), dtype=jnp.float32), 'beta': jnp.zeros((D,), dtype=jnp.float32)}
    _L1_attn_in = _L1_attn_setup()

    def _L1_ffn_setup():
        import jax, jax.numpy as jnp
        import numpy as np
        B, S, H, F, E, R, TOPK = (4, 256, 128, 512, 4, 4, 2)

        def _more_forward(x, Wg, bg, W1, b1, W2, b2):
            b, s, h = x.shape
            cur = x
            for r in range(R):
                flat = cur.reshape(-1, h)
                logits = flat @ Wg[r] + bg[r]
                vals, idx = jax.lax.top_k(logits, TOPK)
                w = jax.nn.softmax(vals, axis=-1)
                cw = jnp.sum(jax.nn.one_hot(idx, E, dtype=flat.dtype) * w[..., None], axis=1)
                hmid = jax.nn.gelu(jnp.einsum('nh,ehf->enf', flat, W1) + b1[:, None, :])
                y = jnp.einsum('enf,efh->enh', hmid, W2) + b2[:, None, :]
                out = jnp.einsum('ne,enh->nh', cw, y)
                cur = cur + out.reshape(b, s, h)
            return cur
        key = jax.random.key(seed)
        ks = jax.random.split(key, 8)
        scale = 0.02
        return {'x': jax.random.normal(ks[0], (B, S, H), dtype=jnp.float32), 'Wg': jax.random.normal(ks[1], (R, H, E), dtype=jnp.float32) * scale, 'bg': jnp.zeros((R, E), dtype=jnp.float32), 'W1': jax.random.normal(ks[2], (E, H, F), dtype=jnp.float32) * scale, 'b1': jnp.zeros((E, F), dtype=jnp.float32), 'W2': jax.random.normal(ks[3], (E, F, H), dtype=jnp.float32) * scale, 'b2': jnp.zeros((E, H), dtype=jnp.float32)}
    _L1_ffn_in = _L1_ffn_setup()
    _L1_c = _w((lambda *s: np.random.randn(*s).astype(np.float32) * 0.05)(2, 128))
    _L1_wmod = _w((lambda *s: np.random.randn(*s).astype(np.float32) * 0.05)(128, 6 * 128) * 128 ** (-0.5))
    _d = {'L0_attn_x': _L0_attn_in['x'], 'L0_attn_w_qkv': _L0_attn_in['w_qkv'], 'L0_attn_b_qkv': _L0_attn_in['b_qkv'], 'L0_attn_w_lepe': _L0_attn_in['w_lepe'], 'L0_attn_b_lepe': _L0_attn_in['b_lepe'], 'L0_ffn_wqkv': _L0_ffn_in['wqkv'], 'L0_ffn_q_scale': _L0_ffn_in['q_scale'], 'L0_ffn_k_scale': _L0_ffn_in['k_scale'], 'L0_ffn_wo': _L0_ffn_in['wo'], 'L0_ffn_ln_g': _L0_ffn_in['ln_g'], 'L0_ffn_ln_b': _L0_ffn_in['ln_b'], 'L0_ffn_w1': _L0_ffn_in['w1'], 'L0_ffn_b1': _L0_ffn_in['b1'], 'L0_ffn_w2': _L0_ffn_in['w2'], 'L0_ffn_b2': _L0_ffn_in['b2'], 'L0_c': _L0_c, 'L0_wmod': _L0_wmod, 'L1_attn_Wq': _L1_attn_in['Wq'], 'L1_attn_bq': _L1_attn_in['bq'], 'L1_attn_Wk': _L1_attn_in['Wk'], 'L1_attn_bk': _L1_attn_in['bk'], 'L1_attn_Wv': _L1_attn_in['Wv'], 'L1_attn_bv': _L1_attn_in['bv'], 'L1_attn_gamma': _L1_attn_in['gamma'], 'L1_attn_beta': _L1_attn_in['beta'], 'L1_ffn_Wg': _L1_ffn_in['Wg'], 'L1_ffn_bg': _L1_ffn_in['bg'], 'L1_ffn_W1': _L1_ffn_in['W1'], 'L1_ffn_b1': _L1_ffn_in['b1'], 'L1_ffn_W2': _L1_ffn_in['W2'], 'L1_ffn_b2': _L1_ffn_in['b2'], 'L1_c': _L1_c, 'L1_wmod': _L1_wmod}
    _x0 = _d['L0_attn_x']
    _d['L0_attn_x'] = jax.random.normal(jax.random.fold_in(jax.random.key(seed), 1), (2, 1024, 128), dtype=_x0.dtype)
    del _x0
    return _d

def reference(L0_attn_x, L0_attn_w_qkv, L0_attn_b_qkv, L0_attn_w_lepe, L0_attn_b_lepe, L0_ffn_wqkv, L0_ffn_q_scale, L0_ffn_k_scale, L0_ffn_wo, L0_ffn_ln_g, L0_ffn_ln_b, L0_ffn_w1, L0_ffn_b1, L0_ffn_w2, L0_ffn_b2, L0_c, L0_wmod, L1_attn_Wq, L1_attn_bq, L1_attn_Wk, L1_attn_bk, L1_attn_Wv, L1_attn_bv, L1_attn_gamma, L1_attn_beta, L1_ffn_Wg, L1_ffn_bg, L1_ffn_W1, L1_ffn_b1, L1_ffn_W2, L1_ffn_b2, L1_c, L1_wmod):

    def _L0_attn_ref(x, w_qkv, b_qkv, w_lepe, b_lepe):
        import jax, jax.numpy as jnp
        import numpy as np
        B, N, C = (32, 64, 128)
        H = 16
        D = C // H
        MAX_SEQ = 64
        BASE = 10000.0

        def _rope_tables(n, d):
            position = jnp.arange(n, dtype=jnp.float32)[:, None]
            div_term = jnp.exp(jnp.arange(0, d, 2, dtype=jnp.float32) * (-np.log(BASE) / d))
            ang = position * div_term
            return (jnp.sin(ang), jnp.cos(ang))

        def _apply_rope(x, sin, cos):
            x1 = x[..., ::2]
            x2 = x[..., 1::2]
            out = jnp.stack([x1 * cos - x2 * sin, x1 * sin + x2 * cos], axis=-1)
            return out.reshape(*x.shape[:-1], -1)
        b, n, c = x.shape
        scale = 1.0 / np.sqrt(D)
        sin, cos = _rope_tables(n, D)
        qkv = (x @ w_qkv.T + b_qkv).reshape(b, n, 3, H, D).transpose(2, 0, 3, 1, 4)
        q, k, v = (qkv[0], qkv[1], qkv[2])
        q = jax.nn.elu(q) + 1.0
        k = jax.nn.elu(k) + 1.0
        q = _apply_rope(q, sin, cos)
        k = _apply_rope(k, sin, cos)
        attn = jnp.einsum('bhnd,bhmd->bhnm', q, k) * scale
        attn = jax.nn.softmax(attn, axis=-1)
        attn_out = jnp.einsum('bhnm,bhmd->bhnd', attn, v)
        attn_out = attn_out.transpose(0, 2, 1, 3).reshape(b, n, c)
        v_conv = v.transpose(0, 2, 1, 3).reshape(b, n, c).transpose(0, 2, 1)
        lepe = jax.lax.conv_general_dilated(v_conv, w_lepe, window_strides=(1,), padding=((1, 1),), dimension_numbers=('NCH', 'OIH', 'NCH'), feature_group_count=c) + b_lepe[None, :, None]
        lepe = lepe.transpose(0, 2, 1)
        return attn_out + lepe

    def _L0_ffn_ref(x, wqkv, q_scale, k_scale, wo, ln_g, ln_b, w1, b1, w2, b2):
        import jax, jax.numpy as jnp
        import numpy as np
        DIM = 128
        DEPTH = 2
        HEADS = 8
        DIM_HEAD = 64
        WINDOW = 64
        INNER = HEADS * DIM_HEAD
        HID = int(DIM * 4 * 2 / 3)
        B, N = (2, 1024)
        QK_SCALE = 8.0

        def shift_token(t):
            t1, t2 = jnp.split(t, 2, axis=-1)
            t2 = jnp.pad(t2, ((0, 0), (1, 0), (0, 0)))[:, :-1]
            return jnp.concatenate([t1, t2], axis=-1)

        def l2norm(t):
            return t / jnp.clip(jnp.linalg.norm(t, axis=-1, keepdims=True), 1e-12)

        def rotate_half(x):
            x1, x2 = jnp.split(x, 2, axis=-1)
            return jnp.concatenate([-x2, x1], axis=-1)

        def rotary_xpos(q, k):
            n = q.shape[-2]
            half_idx = jnp.arange(0, DIM_HEAD, 2, dtype=jnp.float32)
            inv_freq = 1.0 / 10000.0 ** (half_idx / DIM_HEAD)
            t = jnp.arange(n, dtype=jnp.float32)
            freqs = t[:, None] * inv_freq[None, :]
            freqs = jnp.concatenate([freqs, freqs], axis=-1)
            base = (half_idx + 0.4 * DIM_HEAD) / (1.4 * DIM_HEAD)
            power = (t - n // 2) / float(WINDOW // 2)
            scale = base[None, :] ** power[:, None]
            scale = jnp.concatenate([scale, scale], axis=-1)
            cos, sin = (jnp.cos(freqs), jnp.sin(freqs))
            q = q * cos * scale + rotate_half(q) * sin * scale
            k = k * cos / scale + rotate_half(k) * sin / scale
            return (q, k)

        def local_attention(q, k, v):
            b, h, n, d = q.shape
            w = n // WINDOW
            bq = q.reshape(b, h, w, WINDOW, d) * QK_SCALE
            bk = k.reshape(b, h, w, WINDOW, d)
            bv = v.reshape(b, h, w, WINDOW, d)

            def look_around(t):
                p = jnp.pad(t, ((0, 0), (0, 0), (1, 0), (0, 0), (0, 0)))
                return jnp.concatenate([p[:, :, :w], p[:, :, 1:]], axis=3)
            bk, bv = (look_around(bk), look_around(bv))
            bt = jnp.arange(n).reshape(w, WINDOW)
            btp = jnp.pad(bt, ((1, 0), (0, 0)), constant_values=-1)
            btk = jnp.concatenate([btp[:w], btp[1:]], axis=1)
            sim = jnp.einsum('bhwid,bhwjd->bhwij', bq, bk)
            i = bt[:, :, None]
            j = btk[:, None, :]
            mask = (i < j) | (i > j + WINDOW) | (j == -1)
            sim = jnp.where(mask, -jnp.finfo(sim.dtype).max, sim)
            attn = jax.nn.softmax(sim, axis=-1)
            out = jnp.einsum('bhwij,bhwjd->bhwid', attn, bv)
            return out.reshape(b, h, n, d)

        def _layer(x, wqkv, qs, ksc, wo, lg, lb, w1, b1, w2, b2):
            b, n, _ = x.shape
            h = shift_token(x)
            qkv = h @ wqkv
            q, k, v = jnp.split(qkv, 3, axis=-1)
            to_heads = lambda t: t.reshape(b, n, HEADS, DIM_HEAD).transpose(0, 2, 1, 3)
            q, k, v = (to_heads(q), to_heads(k), to_heads(v))
            q = l2norm(q) * qs
            k = l2norm(k) * ksc
            q, k = rotary_xpos(q, k)
            o = local_attention(q, k, v)
            o = o.transpose(0, 2, 1, 3).reshape(b, n, INNER)
            x = x + o @ wo
            h = shift_token(x)
            mu = h.mean(-1, keepdims=True)
            var = h.var(-1, keepdims=True)
            h = (h - mu) / jnp.sqrt(var + 1e-05) * lg + lb
            h = h @ w1 + b1
            a, g = jnp.split(h, 2, axis=-1)
            h = a * jax.nn.gelu(g, approximate=False)
            x = x + h @ w2 + b2
            return x
        for l in range(DEPTH):
            x = _layer(x, wqkv[l], q_scale[l], k_scale[l], wo[l], ln_g[l], ln_b[l], w1[l], b1[l], w2[l], b2[l])
        return x

    def _L1_attn_ref(embedded, Wq, bq, Wk, bk, Wv, bv, gamma, beta):
        import jax, jax.numpy as jnp
        import numpy as np
        B, S, D, H = (2, 256, 128, 16)
        HD = D // H
        LN_EPS = 1e-05
        b, s, d = embedded.shape
        q = embedded @ Wq.T + bq
        k = embedded @ Wk.T + bk
        v = embedded @ Wv.T + bv
        q = q.reshape(b, s, H, HD).transpose(0, 2, 1, 3)
        k = k.reshape(b, s, H, HD).transpose(0, 2, 1, 3)
        v = v.reshape(b, s, H, HD).transpose(0, 2, 1, 3)
        qk = jnp.einsum('bhqd,bhkd->bhqk', q, k)
        qk = jnp.where(jnp.isnan(qk), -jnp.inf, qk)
        qk = qk / jnp.float32(np.sqrt(s))
        p = jax.nn.softmax(qk, axis=-1)
        p = jnp.where(jnp.isnan(p), 0.0, p)
        v = jnp.where(jnp.isnan(v), 0.0, v)
        mask = jnp.triu(jnp.ones((s, s), dtype=p.dtype), k=0)
        p = p * mask
        z = jnp.einsum('bhqk,bhkd->bhqd', p, v)
        z = z.reshape(b, s, d)
        x = embedded + z
        mu = jnp.mean(x, axis=-1, keepdims=True)
        var = jnp.mean(jnp.square(x - mu), axis=-1, keepdims=True)
        out = (x - mu) * jax.lax.rsqrt(var + LN_EPS) * gamma + beta
        return out

    def _L1_ffn_ref(x, Wg, bg, W1, b1, W2, b2):
        import jax, jax.numpy as jnp
        import numpy as np
        B, S, H, F, E, R, TOPK = (4, 256, 128, 512, 4, 4, 2)

        def _more_forward(x, Wg, bg, W1, b1, W2, b2):
            b, s, h = x.shape
            cur = x
            for r in range(R):
                flat = cur.reshape(-1, h)
                logits = flat @ Wg[r] + bg[r]
                vals, idx = jax.lax.top_k(logits, TOPK)
                w = jax.nn.softmax(vals, axis=-1)
                cw = jnp.sum(jax.nn.one_hot(idx, E, dtype=flat.dtype) * w[..., None], axis=1)
                hmid = jax.nn.gelu(jnp.einsum('nh,ehf->enf', flat, W1) + b1[:, None, :])
                y = jnp.einsum('enf,efh->enh', hmid, W2) + b2[:, None, :]
                out = jnp.einsum('ne,enh->nh', cw, y)
                cur = cur + out.reshape(b, s, h)
            return cur
        return _more_forward(x, Wg, bg, W1, b1, W2, b2)
    x = L0_attn_x
    mod = (_silu(L0_c) @ L0_wmod).reshape(L0_c.shape[0], 6, 1, -1)
    sa, ca, ga, sb, cb, gb = (mod[:, 0], mod[:, 1], mod[:, 2], mod[:, 3], mod[:, 4], mod[:, 5])
    ga = (2 * (ga >= 0) - 1) * jnp.maximum(jnp.abs(ga), 0.25)
    gb = (2 * (gb >= 0) - 1) * jnp.maximum(jnp.abs(gb), 0.25)
    h = _layernorm(x, axis=-1) * (1 + ca) + sa
    x = x + ga * _L0_attn_ref(h, L0_attn_w_qkv, L0_attn_b_qkv, L0_attn_w_lepe, L0_attn_b_lepe)
    h = _layernorm(x, axis=-1) * (1 + cb) + sb
    x = x + gb * _L0_ffn_ref(h, L0_ffn_wqkv, L0_ffn_q_scale, L0_ffn_k_scale, L0_ffn_wo, L0_ffn_ln_g, L0_ffn_ln_b, L0_ffn_w1, L0_ffn_b1, L0_ffn_w2, L0_ffn_b2)
    mod = (_silu(L1_c) @ L1_wmod).reshape(L1_c.shape[0], 6, 1, -1)
    sa, ca, ga, sb, cb, gb = (mod[:, 0], mod[:, 1], mod[:, 2], mod[:, 3], mod[:, 4], mod[:, 5])
    ga = (2 * (ga >= 0) - 1) * jnp.maximum(jnp.abs(ga), 0.25)
    gb = (2 * (gb >= 0) - 1) * jnp.maximum(jnp.abs(gb), 0.25)
    h = _layernorm(x, axis=-1) * (1 + ca) + sa
    x = x + ga * _L1_attn_ref(h, L1_attn_Wq, L1_attn_bq, L1_attn_Wk, L1_attn_bk, L1_attn_Wv, L1_attn_bv, L1_attn_gamma, L1_attn_beta)
    h = _layernorm(x, axis=-1) * (1 + cb) + sb
    x = x + gb * _L1_ffn_ref(h, L1_ffn_Wg, L1_ffn_bg, L1_ffn_W1, L1_ffn_b1, L1_ffn_W2, L1_ffn_b2)
    return x

_drawn_inputs = setup_inputs


def setup_inputs(seed=0):
    import zlib

    import numpy as np

    out = dict(_drawn_inputs(seed))
    spreads = {'L0_ffn_q_scale': (1.0, 0.6),
     'L0_ffn_k_scale': (1.0, 0.6),
     'L0_ffn_ln_g': (1.0, 0.6),
     'L0_ffn_ln_b': (0.0, 0.8),
     'L0_ffn_b1': (0.0, 0.8),
     'L0_ffn_b2': (0.0, 0.762),
     'L1_attn_gamma': (1.0, 0.6),
     'L1_attn_beta': (0.0, 2.0),
     'L1_ffn_bg': (0.0, 2.0),
     'L1_ffn_b1': (0.0, 2.0),
     'L1_ffn_b2': (0.0, 0.8)}
    factors = {'L0_attn_w_qkv': 8.0,
     'L0_attn_b_qkv': 8.0,
     'L0_attn_w_lepe': 8.0,
     'L0_attn_b_lepe': 8.0,
     'L0_ffn_wqkv': 7.696,
     'L0_ffn_wo': 7.754,
     'L0_ffn_w1': 8.0,
     'L0_ffn_w2': 8.0,
     'L1_attn_Wq': 45.05,
     'L1_attn_bq': 64.0,
     'L1_attn_Wk': 46.13,
     'L1_attn_bk': 64.0,
     'L1_attn_Wv': 30.281,
     'L1_attn_bv': 64.0,
     'L1_ffn_Wg': 8.0,
     'L1_ffn_W1': 8.0,
     'L1_ffn_W2': 8.0}
    for name, (base, spread) in spreads.items():
        noise = np.random.default_rng([zlib.crc32(name.encode()), seed]).standard_normal(out[name].shape)
        drawn = base * np.exp(spread * noise) if base else spread * noise
        out[name] = jnp.asarray(drawn.astype(out[name].dtype))
    for name, factor in factors.items():
        out[name] = (out[name] * factor).astype(out[name].dtype)
    return out
```

```python
from contextlib import ExitStack, contextmanager

import numpy as np

import concourse.bass as bass
import concourse.mybir as mybir

F32 = mybir.dt.float32
BF16 = mybir.dt.bfloat16
ALU = mybir.AluOpType
ACT = mybir.ActivationFunctionType
AX = mybir.AxisListType

P = 128
BATCH, SEQ, DIM = 2, 1024, 128
TOK = BATCH * SEQ
CHUNK = 512
CHUNKS = TOK // CHUNK
TILES = TOK // P
SEQ_TILES = SEQ // P
EPS = 1e-5

HEADS, HEAD_DIM = 16, 8
GROUP = 4
GROUPS = HEADS // GROUP
UNITS = GROUPS * BATCH
SPLIT_ROWS = 9 * HEAD_DIM
ROWS = SPLIT_ROWS + 2
RING = 3

DEPTH, W_HEADS, W_DIM, WINDOW, HID = 2, 8, 64, 64, 341
INNER = W_HEADS * W_DIM
PAIRS = W_HEADS // 2
QK_SCALE = 8.0
KEYS = P + WINDOW
MASKED = -1e37
HID_TILES = (128, 128, 85)

ROUNDS, EXPERTS, FF = 4, 4, 512
FF_TILES = FF // P


def shape_constants():
    f = np.float32
    c = {}
    c["identity"] = np.eye(P, dtype=f)
    c["ones_mean"] = np.full((P, P), 1.0 / P, f)
    swap = np.zeros((P, P), f)
    swap[np.arange(P), np.arange(P) ^ GROUP] = 1
    c["pair_swap"] = swap
    pair = np.zeros((P, P), f)
    pair[:W_DIM, :W_DIM] = 1
    pair[W_DIM:, W_DIM:] = 1
    c["head_ones"] = pair
    half = np.arange(0, HEAD_DIM, 2, dtype=f)
    div = np.exp(half * f(-np.log(10000.0) / HEAD_DIM)).astype(f)
    ang = np.arange(SEQ, dtype=f)[:, None] * div
    cos, sin = np.cos(ang).astype(f), np.sin(ang).astype(f)
    d = np.arange(P) // GROUP % HEAD_DIM
    c["rope_cos"] = np.ascontiguousarray(cos[:, d // 2].T)
    c["rope_sin"] = np.ascontiguousarray((sin[:, d // 2] * np.where(d % 2, 1, -1).astype(f)).T)
    half = np.arange(0, W_DIM, 2, dtype=f)
    inv = (f(1.0) / f(10000.0) ** (half / f(W_DIM))).astype(f)
    t = np.arange(SEQ, dtype=f)
    freqs = t[:, None] * inv[None, :]
    base = ((half + f(0.4 * W_DIM)) / f(1.4 * W_DIM)).astype(f)
    power = (t - SEQ // 2) / f(WINDOW // 2)
    scale = (base[None, :] ** power[:, None]).astype(f)
    cos, sin = np.cos(freqs).astype(f), np.sin(freqs).astype(f)
    d = np.arange(P) % W_DIM
    sign = np.where(d < W_DIM // 2, -1, 1).astype(f)[:, None]
    i = d % (W_DIM // 2)
    c["xpos"] = np.stack([(cos * scale).T[i], (sin * scale).T[i] * sign,
                          (cos / scale).T[i], (sin / scale).T[i] * sign], 1).astype(f)
    q, j = np.arange(P)[:, None], np.arange(KEYS)[None, :]
    band = np.where((j >= q) & (j <= q + WINDOW), 0.0, MASKED).astype(f)
    first = np.where(j < WINDOW, f(MASKED), band).astype(f)
    c["band"] = np.stack([band, first], 1)
    c["triangle"] = np.tril(np.ones((P, P), f))
    return c


class Core:
    pass


def sems(nc, *names):
    return [nc.alloc_semaphore(n) for n in names]


@contextmanager
def scope(nc):
    before = nc.snapshot_sems()
    yield
    nc.clear_and_free_semaphores(nc.allocated_since(before))
    nc.all_engine_barrier()


@contextmanager
def rearmed(nc, *names):
    with scope(nc):
        yield sems(nc, *names)


def load_residents(nc, k, A):
    loads = [(k.x[:, :], A["x"]), (k.ident[:, :], A["identity"]), (k.ones_mean[:, :], A["ones_mean"]),
             (k.c[:, :], A["c"])]
    (loaded,) = sems(nc, "residents_loaded")
    with nc.Block() as block:
        @block.sync
        def _(sp):
            for dst, src in loads:
                sp.dma_start(dst, src).then_inc(loaded, 16)
            sp.wait_ge(loaded, 16 * len(loads))

        @block.vector
        def _(dve):
            dve.memset(k.eps[:, :], EPS)
            dve.wait_ge(loaded, 16 * len(loads))
            dve.tensor_copy(k.ident_bf[:, :], k.ident[:, :])


def modulation(nc, k, A):
    PARTS = 6
    w_in, silu, mods, exps, chain = sems(nc, "wmod_loaded", "silu_ready", "mod_ready", "exp_ready", "mod_chain")
    ctx = ExitStack()
    with ctx:
        w = ctx.enter_context(nc.sbuf_tensor("wmod", [P, 2, PARTS * DIM], F32))
        e = ctx.enter_context(nc.sbuf_tensor("silu_tmp", [P, 4], F32))
        s = ctx.enter_context(nc.sbuf_tensor("silu_c", [P, 4], F32))
        t = ctx.enter_context(nc.sbuf_tensor("gate_tmp", [P, 2, 2, BATCH], F32))
        ps = k.psum[:, 0, 0:2 * PARTS * BATCH].rearrange("p (l m b) -> p l m b", l=2, b=BATCH)
        block = ctx.enter_context(nc.Block())

        @block.sync
        def _(sp):
            for l in range(2):
                sp.dma_start(w[:, l, :], A[f"wmod{l}"]).then_inc(w_in, 16)

        @block.scalar
        def _(act):
            act.activation(e[:, :], k.c[:, :], ACT.Exp, scale=-1.0).then_inc(exps, 1)

        @block.tensor
        def _(pe):
            pe.wait_ge(w_in, 32)
            pe.wait_ge(silu, 1)
            for l in range(2):
                for m in range(PARTS):
                    last = pe.matmul(ps[:, l, m, :], w[:, l, m * DIM:(m + 1) * DIM],
                                     s[:, l * BATCH:(l + 1) * BATCH], start=True, stop=True)
            last.then_inc(mods, 1)

        @block.vector
        def _(dve):
            n = [0]

            def link(ins):
                n[0] += 1
                ins.then_inc(chain, 1)
                dve.wait_ge(chain, n[0])

            dve.wait_ge(exps, 1)
            link(dve.tensor_scalar(e[:, :], e[:, :], 1.0, None, ALU.add))
            link(dve.reciprocal(e[:, :], e[:, :]))
            dve.tensor_tensor(s[:, :], k.c[:, :], e[:, :], ALU.mult).then_inc(silu, 1)
            dve.wait_ge(mods, 1)
            link(dve.tensor_copy(k.mod[:, :, :, :], ps))
            link(dve.tensor_scalar(k.mod[:, :, 1::3, :], k.mod[:, :, 1::3, :], 1.0, None, ALU.add))
            link(dve.tensor_scalar(t[:, :, :, :], k.mod[:, :, 2::3, :], 0.0, 2.0, ALU.is_ge, ALU.mult))
            link(dve.tensor_scalar(t[:, :, :, :], t[:, :, :, :], -1.0, None, ALU.add))
            link(dve.tensor_tensor(k.mod[:, :, 2::3, :], k.mod[:, :, 2::3, :], t[:, :, :, :], ALU.mult))
            link(dve.tensor_scalar(k.mod[:, :, 2::3, :], k.mod[:, :, 2::3, :], 0.25, None, ALU.max))
            link(dve.tensor_tensor(k.mod[:, :, 2::3, :], k.mod[:, :, 2::3, :], t[:, :, :, :], ALU.mult))


def layer_norm(nc, k, tag, src, dst, scale, shift, residual=None, names=sems):
    mean, centred, squared, var, rooted, chain = names(
        nc, *(f"{tag}_{n}" for n in ("mean", "centred", "squared", "var", "rooted", "chain")))
    ctx = ExitStack()
    with ctx:
        d = ctx.enter_context(nc.sbuf_tensor(f"{tag}_centred_x", [P, TOK], F32))
        sq = ctx.enter_context(nc.sbuf_tensor(f"{tag}_square", [P, TOK], F32))
        at = [slice(c * CHUNK, (c + 1) * CHUNK) for c in range(CHUNKS)]
        block = ctx.enter_context(nc.Block())

        @block.tensor
        def _(pe):
            for c in range(CHUNKS):
                pe.matmul(k.psum[:, c, :], k.ones_mean[:, :], src[:, at[c]], start=True, stop=True).then_inc(mean, 1)
            for c in range(CHUNKS):
                pe.wait_ge(squared, c + 1)
                pe.matmul(k.psum[:, 4 + c, :], k.ones_mean[:, :], sq[:, at[c]], start=True, stop=True).then_inc(var, 1)

        @block.scalar
        def _(act):
            for c in range(CHUNKS):
                act.wait_ge(centred, c + 1)
                act.activation(sq[:, at[c]], d[:, at[c]], ACT.Square).then_inc(squared, 1)
            for c in range(CHUNKS):
                act.wait_ge(var, c + 1)
                act.activation(sq[:, at[c]], k.psum[:, 4 + c, :], ACT.Sqrt, bias=k.eps[:, 0:1]).then_inc(rooted, 1)

        @block.vector
        def _(dve):
            for c in range(CHUNKS):
                dve.wait_ge(mean, c + 1)
                dve.tensor_tensor(d[:, at[c]], src[:, at[c]], k.psum[:, c, :], ALU.subtract).then_inc(centred, 1)
            for c in range(CHUNKS):
                dve.wait_ge(rooted, c + 1)
                dve.reciprocal(sq[:, at[c]], sq[:, at[c]]).then_inc(chain, 1)
            for c in range(CHUNKS):
                dve.wait_ge(chain, c + 1)
                dve.tensor_tensor(d[:, at[c]], d[:, at[c]], sq[:, at[c]], ALU.mult).then_inc(chain, 1)
            for c in range(CHUNKS):
                b = c * CHUNK // SEQ
                dve.wait_ge(chain, CHUNKS + c + 1)
                dve.tensor_scalar(dst[:, at[c]], d[:, at[c]], scale(b), shift(b), ALU.mult, ALU.add).then_inc(chain, 1)
            if residual:
                x, gate = residual
                for c in range(CHUNKS):
                    dve.wait_ge(chain, 2 * CHUNKS + c + 1)
                    dve.scalar_tensor_tensor(x[:, at[c]], dst[:, at[c]], gate(c * CHUNK // SEQ), x[:, at[c]],
                                             ALU.mult, ALU.add)


def project_heads(nc, k, tag, h, A, rotary):
    (w_in, projected, drained, floored, exped, feature, swapped, swap_drained, cosined, sined, operand, hi_done,
     rest1, mid_done, lo_done, stored, v_ps, v_done, v_turned, v_tok_done, v_clean) = sems(nc, *(f"{tag}_{n}" for n in (
        "weights_loaded", "projected", "projection_drained", "floored", "exp_done", "feature_ready", "pair_swapped",
        "swap_drained", "cos_done", "sin_done", "operand_ready", "hi_done", "rest1_done", "mid_done", "lo_done",
        "parts_stored", "v_projected", "v_ready", "v_turned", "v_tok_ready", "v_clean")))
    NU = 2 * CHUNKS
    ctx = ExitStack()
    with ctx:
        def sb(name, shape, dt=F32):
            return ctx.enter_context(nc.sbuf_tensor(f"{tag}_{name}", shape, dt))

        w = sb("w", [P, 3 * DIM])
        bias = sb("b", [P, 3])
        val = sb("val", [P, NU, CHUNK])
        part = [sb(n, [P, 2, TOK], BF16) for n in ("hi", "mid", "lo")]
        if rotary:
            tmp = sb("tmp", [P, NU, CHUNK])
            swap = sb("swap", [P, P])
            cos, sin = sb("cos", [P, SEQ]), sb("sin", [P, SEQ])
        else:
            same = sb("same", [P, TOK])
            vraw = sb("vraw", [P, TOK])
        loads = [(w[:, :], A[f"{tag}_w"]), (bias[:, :], A[f"{tag}_b"])]
        if rotary:
            loads += [(swap[:, :], A["pair_swap"]), (cos[:, :], A["rope_cos"]), (sin[:, :], A["rope_sin"])]
        bank = [k.psum[:, i, :] for i in range(8)]
        cols = [slice(c * CHUNK, (c + 1) * CHUNK) for c in range(CHUNKS)]

        def pos(s):
            return slice((s // 2) * CHUNK % SEQ, (s // 2) * CHUNK % SEQ + CHUNK)

        def of(t, s):
            return t[:, s % 2, cols[s // 2]]

        block = ctx.enter_context(nc.Block())

        @block.sync
        def _(sp):
            for dst, src in loads:
                sp.dma_start(dst, src).then_inc(w_in, 16)
            n = 0
            for b in range(BATCH):
                done = NU // BATCH * (b + 1)
                sp.wait_ge(lo_done, done)
                for which in range(2):
                    for i in range(3):
                        sp.dma_start(k.parts[which, i, b].rearrange("g d h t -> (g d h) t"), part[i][:, which, b * SEQ:(b + 1) * SEQ]).then_inc(stored, 16)
                        n += 1
            sp.wait_ge(stored, 16 * n)

        @block.tensor
        def _(pe):
            pe.wait_ge(w_in, 16 * len(loads))

            def project(s):
                if s >= 2:
                    pe.wait_ge(drained if rotary else operand, s - 1)
                pe.matmul(bank[s % 2], w[:, (s % 2) * DIM:(s % 2 + 1) * DIM], h[:, cols[s // 2]],
                          start=True, stop=True).then_inc(projected, 1)

            def swap_pairs(s):
                pe.wait_ge(feature, s + 1)
                if s >= 2:
                    pe.wait_ge(swap_drained, s - 1)
                pe.matmul(bank[2 + s % 2], swap[:, :], val[:, s, :], start=True, stop=True).then_inc(swapped, 1)

            def project_v(c):
                if c >= 2:
                    pe.wait_ge(v_done, c - 1)
                pe.matmul(bank[4 + c % 2], w[:, 2 * DIM:3 * DIM], h[:, cols[c]], start=True, stop=True)\
                    .then_inc(v_ps, 1)

            def turn_v(c):
                pe.wait_ge(v_done if rotary else v_clean, c + 1)
                if c >= 2:
                    pe.wait_ge(v_tok_done, c - 1)
                for t in range(4):
                    last = pe.transpose(bank[6 + c % 2][:, t * P:(t + 1) * P],
                                        k.v_ch[:, c * CHUNK + t * P:c * CHUNK + (t + 1) * P], k.ident[:, :])
                last.then_inc(v_turned, 1)

            for s in range(NU + 2):
                if s < NU:
                    project(s)
                if rotary and s >= 2:
                    swap_pairs(s - 2)
                if s % 2 == 0 and s < NU:
                    project_v(s // 2)
                if s % 2 == 1 and 3 <= s < NU + 2:
                    turn_v((s - 3) // 2)

        @block.scalar
        def _(act):
            act.wait_ge(w_in, 16 * len(loads))

            def exp_low(s):
                act.wait_ge(floored, s + 1)
                act.activation(tmp[:, s, :], tmp[:, s, :], ACT.Exp).then_inc(exped, 1)

            def biased(s):
                act.wait_ge(projected, s + 1)
                act.activation(val[:, s, :], bank[s % 2], ACT.Identity, bias=bias[:, s % 2:s % 2 + 1])\
                   .then_inc(operand, 1)

            def hi(s):
                act.wait_ge(operand, s + 1)
                act.activation(of(part[0], s), val[:, s, :], ACT.Copy).then_inc(hi_done, 1)

            def mid(s):
                act.wait_ge(rest1, s + 1)
                act.activation(of(part[1], s), val[:, s, :], ACT.Copy).then_inc(mid_done, 1)

            def v_bias(c):
                act.wait_ge(v_ps, c + 1)
                act.activation((k.v_ch if rotary else vraw)[:, cols[c]], bank[4 + c % 2], ACT.Identity,
                               bias=bias[:, 2:3]).then_inc(v_done, 1)

            def v_tok(c):
                act.wait_ge(v_turned, c + 1)
                b, t0 = c // 2, c % 2 * 4
                act.activation(k.v_tok[:, t0:t0 + 4, b * GROUPS:(b + 1) * GROUPS, :],
                               bank[6 + c % 2].rearrange("p (t g c) -> p t g c", t=4, c=32), ACT.Copy)\
                   .then_inc(v_tok_done, 1)

            for s in range(NU + 4):
                if s < NU:
                    (exp_low if rotary else biased)(s)
                if s % 2 == 0 and s < NU:
                    v_bias(s // 2)
                if 3 <= s < NU + 3:
                    hi(s - 3)
                if s >= 4:
                    mid(s - 4)
                if s % 2 == 1 and 3 <= s < NU + 2:
                    v_tok((s - 3) // 2)

        @block.vector
        def _(dve):
            dve.wait_ge(w_in, 16 * len(loads))

            def ramps(s):
                dve.wait_ge(projected, s + 1)
                b = bias[:, s % 2:s % 2 + 1]
                dve.tensor_scalar(tmp[:, s, :], bank[s % 2], b, 0.0, ALU.add, ALU.min).then_inc(floored, 1)
                dve.tensor_scalar(val[:, s, :], bank[s % 2], b, 0.0, ALU.add, ALU.max).then_inc(drained, 1)

            def times_cos(s):
                dve.wait_ge(feature, s + 1)
                dve.tensor_tensor(tmp[:, s, :], val[:, s, :], cos[:, pos(s)], ALU.mult).then_inc(cosined, 1)

            def times_sin(s):
                dve.wait_ge(swapped, s + 1)
                dve.wait_ge(cosined, s + 1)
                dve.tensor_tensor(val[:, s, :], bank[2 + s % 2], sin[:, pos(s)], ALU.mult).then_inc(swap_drained, 1)

            def less_hi(s):
                dve.wait_ge(hi_done, s + 1)
                dve.tensor_tensor(val[:, s, :], val[:, s, :], of(part[0], s), ALU.subtract).then_inc(rest1, 1)

            for s in range(NU + 4):
                if rotary and s < NU:
                    ramps(s)
                if rotary and 1 <= s < NU + 1:
                    times_cos(s - 1)
                if rotary and 2 <= s < NU + 2:
                    times_sin(s - 2)
                if s >= 4:
                    less_hi(s - 4)
                if not rotary and s % 2 == 1 and s < NU:
                    c = s // 2
                    dve.wait_ge(v_done, c + 1)
                    dve.tensor_tensor(same[:, cols[c]], vraw[:, cols[c]], vraw[:, cols[c]], ALU.is_equal)\
                       .then_inc(sined, 1)
                    dve.memset(k.v_ch[:, cols[c]], 0.0).then_inc(sined, 1)
                    dve.wait_ge(sined, 2 * c + 2)
                    dve.copy_predicated(k.v_ch[:, cols[c]], same[:, cols[c]].bitcast(mybir.dt.uint32),
                                        vraw[:, cols[c]]).then_inc(v_clean, 1)

        @block.gpsimd
        def _(pool):
            def feature_sum(s):
                pool.wait_ge(exped, s + 1)
                pool.wait_ge(drained, s + 1)
                pool.tensor_tensor(val[:, s, :], val[:, s, :], tmp[:, s, :], ALU.add).then_inc(feature, 1)

            def rotary_sum(s):
                pool.wait_ge(swap_drained, s + 1)
                pool.tensor_tensor(val[:, s, :], val[:, s, :], tmp[:, s, :], ALU.add).then_inc(operand, 1)

            def lo(s):
                pool.wait_ge(mid_done, s + 1)
                pool.tensor_tensor(of(part[2], s), val[:, s, :], of(part[1], s), ALU.subtract).then_inc(lo_done, 1)

            for s in range(NU + 4):
                if rotary and s < NU:
                    feature_sum(s)
                if rotary and 2 <= s < NU + 2:
                    rotary_sum(s - 2)
                if s >= 4:
                    lo(s - 4)


def attention(nc, k, tag, scale, causal):
    (ones_set, hm_ready, ring_ready, ring_free, st_ready, exp_done, pv_done,
     v_staged, v_ready0, masked, evacuated, hi_done, rec_done, tri_loaded) = sems(
        nc, *(f"{tag}_{n}" for n in (
            "ones_set", "max_parts_ready", "ring_filled",
            "ring_drained", "scores_ready", "exp_done", "values_added", "v_staged", "v_cleared",
            "diagonal_masked", "sums_evacuated", "max_hi_done", "reciprocal_ready",
            "triangle_loaded")))
    z_stored, ones_made = sems(nc, f"{tag}_z_stored", f"{tag}_ones_made")
    m_rows = sems(nc, *(f"{tag}_max_rows_loaded{half}" for half in range(2)))
    loaded = sems(nc, *(f"{tag}_operands_loaded{r}" for r in range(RING)))
    STEPS = 2 * SEQ_TILES
    MAXES = GROUP * SEQ_TILES
    ENTRIES = MAXES + 2 + 2
    FIRST = MAXES + 2
    PB = 4
    ctx = ExitStack()
    with ctx:
        def sb(name, shape, dt=F32):
            return ctx.enter_context(nc.sbuf_tensor(f"{tag}_{name}", shape, dt))

        q_op = [sb(f"q_op{r}", [ROWS, GROUP, SEQ], BF16) for r in range(RING)]
        k_op = [sb(f"k_op{r}", [ROWS, GROUP, SEQ], BF16) for r in range(RING)]
        probs = sb("probs", [P, PB, GROUP, CHUNK])
        stage_v = [sb(f"v1_{r}", [P, SEQ_TILES, GROUP, 32]) for r in range(RING)]
        neg = sb("neg_max", [P, SEQ_TILES, GROUP])
        neg_parts = sb("neg_parts", [P, SEQ_TILES, 2, GROUP], BF16)
        one_rows = sb("one_rows", [2, GROUP, SEQ], BF16)
        neg_rows = sb("neg_rows", [2 * GROUP, SEQ], BF16)
        sums = sb("sums", [P, 2, CHUNK])
        rec = sb("rec", [P, 4, GROUP])
        if causal:
            stage_vo = [sb(f"v0_{r}", [P, SEQ_TILES, GROUP, 32]) for r in range(RING)]
            only_ones = sb("only_ones", [P, 32])
            diag = sb("diag", [P, 2, GROUP, P])
            triangle = sb("triangle", [P, P])
        st_bank = [k.psum[:, i, :] for i in range(3)]
        ring = [k.psum[:, 3 + 2 * i:5 + 2 * i, :].rearrange("p a n -> p (a n)") for i in range(2)]
        out_bank = k.psum[:, 7, :]

        def loop(engine, body):
            body(0, None, 0, 0)
            with engine.Fori(0, (UNITS - 2) // RING) as i:
                for u in range(RING):
                    body(i * RING + (u + 1), i * RING + u, i + (u + 1) // RING, (u + 1) % RING)
            body(UNITS - 1, UNITS - 2, (UNITS - 1) // RING, (UNITS - 1) % RING)

        def is_last(it):
            return isinstance(it, int) and it == UNITS - 1

        def entries(it):
            first, last = isinstance(it, int) and it == 0, is_last(it)
            out = []
            for s in range(STEPS):
                if not last:
                    out += [(s, "max", 2 * s), (s, "max", 2 * s + 1)]
                if s == 1 and not first:
                    out.append((s, "turn", 1))
                if s == 2 and not first:
                    out.append((s, "rows", 1))
                if s == SEQ_TILES + 1:
                    out.append((s, "turn", 0))
                if s == SEQ_TILES + 2 and not last:
                    out.append((s, "rows", 0))
            return out

        def base_of(it):
            return FIRST if isinstance(it, int) and it == 0 else it * ENTRIES + (FIRST - 2)

        def max_at(arg):
            half, rest = arg // (MAXES // 2), arg % (MAXES // 2)
            return rest // 4, 4 * half + rest % 4

        def done(it, kind, arg):
            return base_of(it) + [e[1:] for e in entries(it)].index((kind, arg)) + 1

        block = ctx.enter_context(nc.Block())

        @block.sync
        def _(sp):
            def load(it):
                r = it % RING
                for a in range(3):
                    rows9 = slice(3 * HEAD_DIM * a, 3 * HEAD_DIM * (a + 1))
                    part_q = k.parts[0, a, it // GROUPS, it % GROUPS].rearrange("d h t -> d (h t)")
                    sp.dma_start(q_op[r][rows9].rearrange("p h t -> p (h t)"),
                                 part_q.unsqueeze(0).broadcast_to([3, HEAD_DIM, GROUP * SEQ])).then_inc(loaded[r], 16)
                    parts_k = k.parts[1, :, it // GROUPS, it % GROUPS].rearrange("c d h t -> c d (h t)")
                    sp.dma_start(k_op[r][rows9].rearrange("p h t -> p (h t)"), parts_k).then_inc(loaded[r], 16)

            def rows(it, half):
                sp.wait_ge(ring_free, FIRST if it == 0 else done(it, "rows", 1) if half else done(it - 1, "rows", 0))
                sp.dma_start(q_op[it % RING][SPLIT_ROWS:ROWS, :, half * CHUNK:(half + 1) * CHUNK],
                             neg_rows[:, half * CHUNK:(half + 1) * CHUNK]).then_inc(m_rows[half], 16)

            def store_z(it):
                b, g = it // GROUPS, it % GROUPS
                sp.wait_ge(ring_free, done(it, "turn", 0) + 1 if is_last(it) else done(it + 1, "turn", 1))
                for j in range(GROUP):
                    sp.dma_start(k.z[b, g * GROUP + j].rearrange("(t p) d -> p t d", p=P),
                                 k.att[:, :, it, j * HEAD_DIM:(j + 1) * HEAD_DIM]).then_inc(z_stored, 16)

            for r in range(RING):
                load(r)
            sp.wait_ge(ones_made, 1)
            for r in range(RING):
                sp.dma_start(k_op[r][SPLIT_ROWS:ROWS], one_rows[:, :, :]).then_inc(ones_set, 16)
            rows(0, 0)
            rows(0, 1)
            for it in range(UNITS):
                if it + 1 < UNITS:
                    rows(it + 1, 0)
                if it + RING < UNITS:
                    sp.wait_ge(exp_done, GROUP * STEPS * (it + 1))
                    load(it + RING)
                if it + 1 < UNITS:
                    rows(it + 1, 1)
                if causal:
                    store_z(it)
            if causal:
                sp.wait_ge(z_stored, 16 * GROUP * UNITS)

        @block.tensor
        def _(pe):
            def entry(n, base, kind, arg, it, r=None):
                buf = ring[n % 2]
                if not (isinstance(base, int) and base + n < 2):
                    pe.wait_ge(ring_free, base + n - 1)
                if kind == "max":
                    j, t = max_at(arg)
                    for half in range(2):
                        last = pe.matmul(buf[:, half * CHUNK:(half + 1) * CHUNK],
                                         q_op[r][0:SPLIT_ROWS, j, t * P:(t + 1) * P],
                                         k_op[r][0:SPLIT_ROWS, j, half * CHUNK:(half + 1) * CHUNK],
                                         start=True, stop=True)
                elif kind == "rows":
                    pe.wait_ge(hm_ready, 2 * it + arg + 1)
                    for t in range(4):
                        last = pe.matmul(buf[0:2 * GROUP, t * P:(t + 1) * P],
                                         neg_parts[:, arg * 4 + t, :, :].rearrange("p c h -> p (c h)"),
                                         k.ident_bf[:, :], start=True, stop=True)
                else:
                    pe.wait_ge(evacuated, 2 * it + arg + 1)
                    for t in range(4):
                        last = pe.transpose(buf[:, t * P:(t + 1) * P], sums[:, arg, t * P:(t + 1) * P], k.ident[:, :])
                last.then_inc(ring_ready, 1)

            def score(it, r, s, j):
                half, t = s // SEQ_TILES, s % SEQ_TILES
                e = GROUP * s + j
                if not (isinstance(it, int) and GROUP * STEPS * it + e < 3):
                    pe.wait_ge(exp_done, it * (GROUP * STEPS) + e - 2)
                mm = pe.matmul(st_bank[(r + e) % 3], k_op[r][:, j, t * P:(t + 1) * P],
                               q_op[r][:, j, half * CHUNK:(half + 1) * CHUNK], start=True, stop=True)
                mm.then_inc(st_ready, 1)

            def values(it, r, s):
                half, t = s // SEQ_TILES, s % SEQ_TILES
                pe.wait_ge(exp_done, it * (GROUP * STEPS) + GROUP * (s + 1))
                if s == 0:
                    pe.wait_ge(v_staged, it + 1)
                if t == 0 and not (isinstance(it, int) and 2 * it + half == 0):
                    pe.wait_ge(evacuated, 2 * it + half)
                first, final = t == 0, t == SEQ_TILES - 1
                full = CHUNK if not causal else min(max(t - 4 * half, 0) * P, CHUNK)
                for j in range(GROUP):
                    out = out_bank[32 * j:32 * j + 32, :]
                    pr = probs[:, s % PB, j, :]
                    if full:
                        last = pe.matmul(out[:, 0:full], stage_v[r][:, t, j, :], pr[:, 0:full],
                                         start=first, stop=final and full == CHUNK, skip_group_check=causal)
                    if full < CHUNK:
                        last = pe.matmul(out[:, full:CHUNK], only_ones[:, :], pr[:, full:CHUNK],
                                         start=first, stop=final, skip_group_check=causal)
                if causal and 0 <= t - 4 * half < 4:
                    pe.wait_ge(masked, it * SEQ_TILES + t + 1)
                    at = (t - 4 * half) * P
                    for j in range(GROUP):
                        last = pe.matmul(out_bank[32 * j:32 * j + 32, at:at + P], stage_vo[r][:, t, j, :],
                                         diag[:, t % 2, j, :], start=False, stop=final, skip_group_check=True)
                last.then_inc(pv_done, 1)

            def body(it, before, uses, r):
                base = base_of(it)
                todo = list(enumerate(entries(it)))
                if isinstance(it, int) and it == 0:
                    pe.wait_ge(ones_set, 16 * RING)
                for s in range(STEPS):
                    if s % SEQ_TILES == 0:
                        pe.wait_ge(m_rows[s // SEQ_TILES], 16 * (it + 1))
                    for j in range(GROUP):
                        score(it, r, s, j)
                        if j % 2 == 1 and not is_last(it):
                            n, (_, kind, arg) = todo.pop(0)
                            if n == 0:
                                pe.wait_ge(loaded[(r + 1) % RING], 96 * (uses + (r + 1) // RING + 1))
                            entry(n, base, kind, arg, None, (r + 1) % RING)
                    if s >= 1:
                        values(it, r, s - 1)
                    elif before is not None:
                        values(before, (r - 1) % RING, STEPS - 1)
                    while todo and todo[0][1][0] == s:
                        n, (_, kind, arg) = todo.pop(0)
                        late = (kind, arg) == ("turn", 1)
                        ahead = (kind, arg) == ("rows", 0)
                        entry(n, base, kind, arg, before if late else it + 1 if ahead else it)
                if is_last(it):
                    values(it, r, STEPS - 1)
                    entry(3, base, "turn", 1, it)

            def first():
                pe.wait_ge(loaded[0], 96)
                for n in range(MAXES):
                    entry(n, 0, "max", n, 0, 0)
                entry(MAXES, 0, "rows", 0, 0)
                entry(MAXES + 1, 0, "rows", 1, 0)

            first()
            loop(pe, body)

        @block.scalar
        def _(act):
            def take_sums(it, half):
                act.wait_ge(pv_done, it * STEPS + (half + 1) * SEQ_TILES)
                act.activation(sums[:, half, :], out_bank, ACT.Copy).then_inc(evacuated, 1)

            def body(it, before, uses, r):
                for s in range(STEPS):
                    for j in range(GROUP):
                        e = GROUP * s + j
                        act.wait_ge(st_ready, it * (GROUP * STEPS) + e + 1)
                        if j == 0 and not (isinstance(it, int) and it * STEPS + s < PB):
                            act.wait_ge(pv_done, it * STEPS + s - PB + 1)
                        ins = act.activation(probs[:, s % PB, j, :], st_bank[(r + e) % 3], ACT.Exp, scale=scale)
                        ins.then_inc(exp_done, 1)
                        if j == 0 and s == 1 and before is not None:
                            take_sums(before, 1)
                        if j == 0 and s == SEQ_TILES + 1:
                            take_sums(it, 0)
                if is_last(it):
                    take_sums(it, 1)

            loop(act, body)

        @block.vector
        def _(dve):
            def entry(n, base, kind, arg, it):
                buf = ring[n % 2]
                dve.wait_ge(ring_ready, base + n + 1)
                if kind == "max":
                    j, t = max_at(arg)
                    ins = dve.tensor_reduce(neg[:, t, j:j + 1], buf, AX.X, ALU.max, negate=True)
                    ins.then_inc(ring_free, 1)
                    if (arg + 1) % (MAXES // 2) == 0:
                        half = arg // (MAXES // 2)
                        at = slice(4 * half, 4 * half + 4)
                        dve.wait_ge(ring_free, base + n + 1)
                        dve.tensor_copy(neg_parts[:, at, 0, :], neg[:, at, :]).then_inc(hi_done, 1)
                        dve.wait_ge(hi_done, 2 * it + half + 1)
                        dve.tensor_tensor(neg_parts[:, at, 1, :], neg[:, at, :], neg_parts[:, at, 0, :], ALU.subtract)\
                           .then_inc(hm_ready, 1)
                elif kind == "rows":
                    if not (isinstance(it, int) and it == 0):
                        dve.wait_ge(m_rows[arg], 16 * it)
                    dve.wait_ge(hm_ready, 2 * it + arg + 1)
                    dve.tensor_copy(neg_rows[:, arg * CHUNK:(arg + 1) * CHUNK], buf[0:2 * GROUP, 0:CHUNK])\
                       .then_inc(ring_free, 1)
                else:
                    tile = buf[:, 0:CHUNK].rearrange("p (t h c) -> p t h c", t=4, c=32)
                    if is_last(it):
                        dve.wait_ge(ring_free, base + n)
                    dve.reciprocal(rec[:, :, :], tile[:, :, :, HEAD_DIM]).then_inc(rec_done, 1)
                    dve.wait_ge(rec_done, 2 * it + arg + 1)
                    out = k.att[:, 4 * arg:4 * arg + 4, it, :].rearrange("p t (h c) -> p t h c", c=HEAD_DIM)
                    num = tile[:, :, :, 0:HEAD_DIM]
                    by = rec[:, :, :].unsqueeze(3).broadcast_to([P, 4, GROUP, HEAD_DIM])
                    dve.tensor_tensor(out, num, by, ALU.mult).then_inc(ring_free, 1)

            def body(it, before, uses, r):
                for n, (s, kind, arg) in enumerate(entries(it)):
                    of_unit = it + 1 if kind == "max" or (kind, arg) == ("rows", 0) else \
                        before if (kind, arg) == ("turn", 1) else it
                    entry(n, base_of(it), kind, arg, of_unit)
                if is_last(it):
                    entry(3, base_of(it), "turn", 1, it)

            def first():
                for n in range(MAXES):
                    entry(n, 0, "max", n, 0)
                entry(MAXES, 0, "rows", 0, 0)
                entry(MAXES + 1, 0, "rows", 1, 0)

            first()
            loop(dve, body)

        @block.gpsimd
        def _(pool):
            if causal:
                pool.dma_start(triangle[:, :], k.A["triangle"]).then_inc(tri_loaded, 16)
                pool.wait_ge(tri_loaded, 16)
            pool.memset(one_rows[:, :, :], 1.0).then_inc(ones_made, 1)
            stages = stage_v + (stage_vo if causal else [])
            for t in stages:
                pool.memset(t[:, :, :, :], 0.0).then_inc(v_ready0, 1)
            n = len(stages)
            if causal:
                pool.memset(only_ones[:, :], 0.0).then_inc(v_ready0, 1)
                n += 1
            pool.wait_ge(v_ready0, n)
            for t in stage_v:
                pool.memset(t[:, :, :, HEAD_DIM:HEAD_DIM + 1], 1.0).then_inc(v_ready0, 1)
            n += RING
            if causal:
                pool.memset(only_ones[:, HEAD_DIM:HEAD_DIM + 1], 1.0).then_inc(v_ready0, 1)
                n += 1
            pool.wait_ge(v_ready0, n)

            def stage(it, r):
                src = k.v_tok[:, :, it, :].rearrange("p t (h c) -> p t h c", c=HEAD_DIM)
                if causal:
                    pool.tensor_copy(stage_vo[r][:, :, :, 0:HEAD_DIM], src)
                pool.tensor_copy(stage_v[r][:, :, :, 0:HEAD_DIM], src).then_inc(v_staged, 1)

            def body(it, before, uses, r):
                if not is_last(it):
                    if not (isinstance(it, int) and it == 0):
                        pool.wait_ge(pv_done, it * STEPS)
                    stage(it + 1, (r + 1) % RING)
                if causal:
                    for t in range(SEQ_TILES):
                        s = t if t < 4 else SEQ_TILES + t
                        pool.wait_ge(exp_done, it * (GROUP * STEPS) + GROUP * (s + 1))
                        if not (isinstance(it, int) and it * SEQ_TILES + t < 2):
                            back = t - 2 if t >= 2 else t + 6
                            sb_ = back if back < 4 else SEQ_TILES + back
                            pool.wait_ge(pv_done, (it if t >= 2 else it - 1) * STEPS + sb_ + 1)
                        at = (t % 4) * P
                        pool.tensor_tensor(diag[:, t % 2, :, :], probs[:, s % PB, :, at:at + P],
                                           triangle[:, :].unsqueeze(1).broadcast_to([P, GROUP, P]), ALU.mult)\
                            .then_inc(masked, 1)

            stage(0, 0)
            loop(pool, body)


def residual_attention(nc, k, tag, A):
    w_in, turned, drained, taps = sems(nc, *(f"{tag}_{n}" for n in ("taps_loaded", "att_turned", "turned_drained", "taps_done")))
    gate = lambda b: k.mod[:, 0, 2, b:b + 1]
    ctx = ExitStack()
    with ctx:
        tap = ctx.enter_context(nc.sbuf_tensor("lepe_taps", [P, 4], F32))
        acc = ctx.enter_context(nc.sbuf_tensor("lepe", [P, BATCH, SEQ], F32))
        v = k.v_ch[:, :].rearrange("p (b n) -> p b n", b=BATCH)
        x = k.x[:, :].rearrange("p (b n) -> p b n", b=BATCH)
        block = ctx.enter_context(nc.Block())

        @block.sync
        def _(sp):
            sp.dma_start(tap[:, :], A["lepe"]).then_inc(w_in, 16)

        @block.tensor
        def _(pe):
            for c in range(CHUNKS):
                b, t0 = c // 2, c % 2 * 4
                for t in range(4):
                    last = pe.transpose(k.psum[:, c, t * P:(t + 1) * P], k.att[:, t0 + t, b * GROUPS:(b + 1) * GROUPS, :].rearrange("p g c -> p (g c)"), k.ident[:, :])
                last.then_inc(turned, 1)

        @block.vector
        def _(dve):
            dve.wait_ge(w_in, 16)
            dve.tensor_scalar(acc[:, :, :], v, tap[:, 1:2], tap[:, 3:4], ALU.mult, ALU.add).then_inc(taps, 1)
            dve.wait_ge(taps, 1)
            dve.scalar_tensor_tensor(acc[:, :, 1:SEQ], v[:, :, 0:SEQ - 1], tap[:, 0:1], acc[:, :, 1:SEQ],
                                     ALU.mult, ALU.add).then_inc(taps, 1)
            dve.wait_ge(taps, 2)
            dve.scalar_tensor_tensor(acc[:, :, 0:SEQ - 1], v[:, :, 1:SEQ], tap[:, 2:3], acc[:, :, 0:SEQ - 1],
                                     ALU.mult, ALU.add).then_inc(taps, 1)
            dve.wait_ge(taps, 3)
            for c in range(CHUNKS):
                b, at = c // 2, slice(c % 2 * CHUNK, (c % 2 + 1) * CHUNK)
                dve.wait_ge(turned, c + 1)
                dve.tensor_tensor(acc[:, b, at], acc[:, b, at], k.psum[:, c, :], ALU.add).then_inc(drained, 1)
                dve.wait_ge(drained, c + 1)
                dve.scalar_tensor_tensor(x[:, b, at], acc[:, b, at], gate(b), x[:, b, at], ALU.mult, ALU.add)


def windowed_layers(nc, k, A, part):
    with ExitStack() as ctx:
        def sb(name, shape, dt=F32):
            return ctx.enter_context(nc.sbuf_tensor(f"win_{name}", shape, dt))

        s = Core()
        s.y = sb("y", [P, TOK])
        layer_norm(nc, k, "ln1", k.x, s.y, part(0, 4), part(0, 3))
        s.h = sb("h", [P, TOK])
        s.wj = sb("w_pair", [P, 5, DIM])
        s.wo = sb("wo", [P, PAIRS, DIM])
        s.w1 = sb("w1", [P, 2 * HID])
        s.w2 = sb("w2", [P, 3, DIM])
        s.cols = sb("cols", [P, COLS])
        s.table = sb("table", [P, 4, SEQ])
        s.head_ones = sb("head_ones", [P, P])
        s.band = sb("band", [P, 2, KEYS])
        s.q = sb("q", [P, TOK])
        s.k_half = [sb(f"k_half{e}", [P, WINDOW + TOK]) for e in range(2)]
        s.v = sb("v", [P, TILES, DIM])
        s.q_norm = sb("q_norm", [P, TILES, 2])
        s.q_scale = sb("q_scale", [P, 2, TILES, 2])
        s.o = sb("o", [P, PAIRS, TOK])
        s.loaded_w = sems(nc, "pair_weights_loaded")[0]
        once = [(s.head_ones[:, :], A["head_ones"]), (s.band[:, :, :], A["band"]), (s.wj[:, :, :], A["win_wj"][0])]
        (loaded,) = sems(nc, "win_constants_loaded")
        with nc.Block() as block:
            @block.sync
            def _(sp):
                for dst, src in once:
                    sp.dma_start(dst, src).then_inc(loaded, 16)
                sp.wait_ge(loaded, 16 * len(once))

            @block.gpsimd
            def _(pool):
                for e in range(2):
                    pool.memset(s.k_half[e][:, :], 0.0)

        with nc.Fori(0, DEPTH) as l:
            layer_start(nc, s, A, l)
            with nc.Fori(0, PAIRS) as j:
                project_pair(nc, k, s)
                attend_pair(nc, k, s, A, l, j)
            output_projection(nc, k, s)
            with rearmed(nc, *(f"ln5_{n}" for n in ("mean", "centred", "squared", "var", "rooted", "chain"))) as own:
                layer_norm(nc, k, "ln5", s.h, s.h, lambda b: s.cols[:, LN_G:LN_G + 1],
                           lambda b: s.cols[:, LN_B:LN_B + 1], names=lambda nc, *names: own)
            geglu(nc, k, s)

        with nc.Block() as block:
            @block.vector
            def _(dve):
                for b in range(BATCH):
                    at = slice(b * SEQ, (b + 1) * SEQ)
                    dve.scalar_tensor_tensor(k.x[:, at], s.y[:, at], part(0, 5)(b), k.x[:, at], ALU.mult, ALU.add)


SCALES, LN_G, LN_B, B2, B1_A, B1_G, COLS = 0, 4, 5, 6, 7, 10, 13


def shift_tokens(dve, s):
    half = DIM // 2
    y = s.y[:, :].rearrange("p (b n) -> p b n", b=BATCH)
    h = s.h[:, :].rearrange("p (b n) -> p b n", b=BATCH)
    dve.tensor_copy(h[0:half], y[0:half])
    dve.tensor_copy(h[half:P, :, 1:SEQ], y[half:P, :, 0:SEQ - 1])
    dve.memset(h[half:P, :, 0:1], 0.0)


def layer_start(nc, s, A, l):
    with rearmed(nc, "layer_loaded") as (loaded,), nc.Block() as block:
        loads = [(s.cols[:, :], A["win_cols"][l]), (s.table[:, :, :], A["xpos"]), (s.wo[:, :, :], A["win_wo"][l]),
                 (s.w1[:, :], A["win_w1"][l]), (s.w2[:, :, :], A["win_w2"][l])]

        @block.sync
        def _(sp):
            for dst, src in loads:
                sp.dma_start(dst, src).then_inc(loaded, 16)
            sp.wait_ge(loaded, 16 * len(loads))

        @block.vector
        def _(dve):
            shift_tokens(dve, s)
            dve.wait_ge(loaded, 16 * len(loads))
            for i in range(4):
                dve.tensor_scalar(s.table[:, i, :], s.table[:, i, :], s.cols[:, SCALES + i:SCALES + i + 1], None,
                                  ALU.mult)


def project_pair(nc, k, s):
    with (rearmed(nc, "pair_projected", "pair_squared", "pair_sums_k", "pair_sums_q", "pair_rooted", "pair_q_parts",
                  "pair_k_parts", "pair_k_inverse", "pair_floored", "pair_k_sum", "pair_q_done", "pair_k_done",
                  "pair_v", "pair_v_done", "pair_q_rooted", "pair_q_chain") as
          (projected, squared, sums_k, sums_q, rooted, q_parts, k_parts, k_inverse, floored, k_sum, q_done, k_done,
           v_ready, v_done, q_rooted, q_chain),
          nc.sbuf_tensor("pair_sq", [P, 2, 2, CHUNK], F32) as sq,
          nc.sbuf_tensor("pair_tmp", [P, 2, 4, CHUNK], F32) as tmp,
          nc.sbuf_tensor("pair_rk", [P, 2, CHUNK], F32) as rk,
          nc.Block() as block):
        cols = [slice(c * CHUNK, (c + 1) * CHUNK) for c in range(CHUNKS)]
        ORDER = (1, 0, 3, 2)

        @block.tensor
        def _(pe):
            def project(c):
                for n, i in enumerate(ORDER):
                    if c:
                        pe.wait_ge(q_parts if i < 2 else k_parts, 2 * (c - 1) + n % 2 + 1)
                    pe.matmul(k.psum[:, i, :], s.wj[:, i, :], s.h[:, cols[c]], start=True, stop=True)\
                      .then_inc(projected, 1)

            def norms(c):
                pe.wait_ge(squared, 2 * c + 2)
                if c:
                    pe.wait_ge(rooted, c)
                pe.matmul(k.psum[:, 4, :], s.head_ones[:, :], sq[:, c % 2, 1, :], start=True, stop=True)\
                  .then_inc(sums_k, 1)
                for t in range(4):
                    i = 4 * c + t
                    last = pe.matmul(k.psum[:, 5, 2 * i:2 * i + 2], sq[:, c % 2, 0, t * P:(t + 1) * P],
                                     s.head_ones[:, 0:P:W_DIM], start=True, stop=True)
                last.then_inc(sums_q, 1)

            def values(c):
                if c >= 2:
                    pe.wait_ge(v_done, c - 1)
                for t in range(4):
                    i = 4 * c + t
                    last = pe.matmul(k.psum[:, 6 + c % 2, t * P:(t + 1) * P], s.h[:, i * P:(i + 1) * P],
                                     s.wj[:, 4, :], start=True, stop=True)
                last.then_inc(v_ready, 1)

            project(0)
            for c in range(CHUNKS):
                values(c)
                if c + 1 < CHUNKS:
                    project(c + 1)
                norms(c)

        @block.scalar
        def _(act):
            def squares(c):
                if c >= 2:
                    act.wait_ge(sums_q, c - 1)
                for i in range(2):
                    act.wait_ge(projected, 4 * c + 2 * i + 2)
                    act.activation(sq[:, c % 2, i, :], k.psum[:, 2 * i, :], ACT.Square).then_inc(squared, 1)

            def root(c):
                act.wait_ge(sums_k, c + 1)
                if c >= 2:
                    act.wait_ge(k_done, 2 * (c - 1))
                act.activation(rk[:, c % 2, :], k.psum[:, 4, :], ACT.Sqrt).then_inc(rooted, 1)

            for c in range(CHUNKS + 1):
                if c < CHUNKS:
                    squares(c)
                if c:
                    root(c - 1)
                    act.wait_ge(v_ready, c)
                    act.activation(s.v[:, 4 * (c - 1):4 * c, :],
                                   k.psum[:, 6 + (c - 1) % 2, :].rearrange("p (t n) -> p t n", t=4), ACT.Copy)\
                       .then_inc(v_done, 1)
            act.wait_ge(sums_q, CHUNKS)
            act.activation(s.q_norm[:, :, :], k.psum[:, 5, 0:2 * TILES].rearrange("p (t e) -> p t e", e=2), ACT.Sqrt)\
               .then_inc(q_rooted, 1)

        @block.vector
        def _(dve):
            def parts(c):
                at = slice(c * CHUNK % SEQ, c * CHUNK % SEQ + CHUNK)
                for n, i in enumerate(ORDER):
                    dve.wait_ge(projected, 4 * c + n + 1)
                    if i % 2 == 0:
                        dve.wait_ge(squared, 2 * c + i // 2 + 1)
                    if c >= 2 and n == 0:
                        dve.wait_ge(q_done, c - 1)
                    if c >= 2 and n == 2:
                        dve.wait_ge(k_sum, c - 1)
                        dve.wait_ge(k_done, 2 * (c - 1))
                    dve.tensor_tensor(tmp[:, c % 2, i, :], k.psum[:, i, :], s.table[:, i, at], ALU.mult)\
                       .then_inc(q_parts if i < 2 else k_parts, 1)

            def finish(c):
                dve.wait_ge(q_parts, 2 * c + 2)
                dve.tensor_tensor(s.q[:, cols[c]], tmp[:, c % 2, 0, :], tmp[:, c % 2, 1, :], ALU.add)\
                   .then_inc(q_done, 1)
                dve.wait_ge(rooted, c + 1)
                dve.tensor_scalar(rk[:, c % 2, :], rk[:, c % 2, :], 1e-12, None, ALU.max).then_inc(floored, 1)
                dve.wait_ge(floored, c + 1)
                dve.reciprocal(rk[:, c % 2, :], rk[:, c % 2, :]).then_inc(k_inverse, 1)

            for c in range(CHUNKS + 1):
                if c < CHUNKS:
                    parts(c)
                if c:
                    finish(c - 1)
            dve.wait_ge(q_rooted, 1)
            dve.tensor_scalar(s.q_norm[:, :, :], s.q_norm[:, :, :], 1e-12, None, ALU.max).then_inc(q_chain, 1)
            dve.wait_ge(q_chain, 1)
            dve.reciprocal(s.q_norm[:, :, :], s.q_norm[:, :, :]).then_inc(q_chain, 1)
            dve.wait_ge(q_chain, 2)
            for i, v in enumerate((QK_SCALE, -QK_SCALE)):
                dve.tensor_scalar(s.q_scale[:, i, :, :], s.q_norm[:, :, :], v, None, ALU.mult)

        @block.gpsimd
        def _(pool):
            for c in range(CHUNKS):
                if c:
                    pool.wait_ge(k_done, 2 * c)
                pool.wait_ge(k_parts, 2 * c + 2)
                pool.tensor_tensor(tmp[:, c % 2, 2, :], tmp[:, c % 2, 2, :], tmp[:, c % 2, 3, :], ALU.add)\
                    .then_inc(k_sum, 1)
                pool.wait_ge(k_sum, c + 1)
                pool.wait_ge(k_inverse, c + 1)
                for e in range(2):
                    rows = slice(e * W_DIM, (e + 1) * W_DIM)
                    pool.tensor_tensor(s.k_half[e][rows, WINDOW + c * CHUNK:WINDOW + (c + 1) * CHUNK],
                                       tmp[rows, c % 2, 2, :], rk[rows, c % 2, :], ALU.mult).then_inc(k_done, 1)


def attend_pair(nc, k, s, A, l, j):
    with (rearmed(nc, "win_weights", "win_scores", "win_masked", "win_bias", "win_exp", "win_inverse", "win_scaled",
                  "win_turned", "win_turned_copied", "win_values", "win_out", "win_cleared") as
          (w_next, scores, masked, bias_done, exp_done, inverse, scaled, turned, copied, values_done, out_done, cleared),
          nc.sbuf_tensor("win_sm", [P, 2, 2, KEYS], F32) as sm,
          nc.sbuf_tensor("win_p", [P, 2, 2, 2 * P], F32) as pr,
          nc.sbuf_tensor("win_pt", [P, 2, 2, 2, P], F32) as pt,
          nc.sbuf_tensor("win_max", [P, TILES, 2], F32) as mx,
          nc.sbuf_tensor("win_nb", [P, TILES, 2], F32) as nb,
          nc.sbuf_tensor("win_rs", [P, TILES, 2], F32) as rs,
          nc.sbuf_tensor("win_ri", [P, TILES, 2], F32) as ri,
          nc.Block() as block):

        def s_bank(i):
            return k.psum[:, i % 2, 0:2 * KEYS].rearrange("p (e n) -> p e n", e=2)

        def t_bank(i):
            return k.psum[:, 2 + i % 2, :].rearrange("p (e a n) -> p e a n", e=2, a=2)

        def o_bank(i):
            return k.psum[:, 4 + i // 4 % 2, i % 4 * P:(i % 4 + 1) * P]

        def near(i):
            return (1,) if i % SEQ_TILES == 0 else (0, 1)

        @block.sync
        def _(sp):
            sp.dma_start(s.wj[:, :, :], A["win_wj"][l * PAIRS + (j + 1)]).then_inc(w_next, 16)
            sp.wait_ge(w_next, 16)

        @block.tensor
        def _(pe):
            def score(i):
                if i >= 2:
                    pe.wait_ge(masked, 2 * (i - 1))
                for e in range(2):
                    last = pe.matmul(s_bank(i)[:, e, :], s.q[:, i * P:(i + 1) * P],
                                     s.k_half[e][:, i * P:i * P + KEYS], start=True, stop=True)
                last.then_inc(scores, 1)

            def turn(i):
                pe.wait_ge(scaled, i + 1)
                if i >= 2:
                    pe.wait_ge(copied, i - 1)
                for e in range(2):
                    for a in near(i):
                        last = pe.transpose(t_bank(i)[:, e, a, :], pr[:, i % 2, e, a * P:(a + 1) * P], k_ident)
                last.then_inc(turned, 1)

            def values(i):
                pe.wait_ge(copied, i + 1)
                if i % 4 == 0 and i >= 8:
                    pe.wait_ge(out_done, i // 4 - 1)
                for e in range(2):
                    for a in near(i):
                        last = pe.matmul(o_bank(i)[e * W_DIM:(e + 1) * W_DIM, :],
                                         s.v[:, i - 1 + a, e * W_DIM:(e + 1) * W_DIM], pt[:, i % 2, e, a, :],
                                         start=a == near(i)[0], stop=a == 1)
                last.then_inc(values_done, 1)

            k_ident = k.ident[:, :]
            for i in range(TILES + 3):
                if i < TILES:
                    score(i)
                if 2 <= i < TILES + 2:
                    turn(i - 2)
                if i >= 3:
                    values(i - 3)

        @block.scalar
        def _(act):
            def copy_turned(i):
                act.wait_ge(turned, i + 1)
                if i >= 2:
                    act.wait_ge(values_done, i - 1)
                a = near(i)[0]
                act.activation(pt[:, i % 2, :, a:2, :], t_bank(i)[:, :, a:2, :], ACT.Copy).then_inc(copied, 1)

            for i in range(TILES + 2):
                if i < TILES:
                    act.wait_ge(bias_done, i + 1)
                    if i == 0:
                        act.wait_ge(cleared, 1)
                    if i >= 2:
                        act.wait_ge(turned, i - 1)
                    for e in range(2):
                        act.activation(pr[:, i % 2, e, WINDOW:2 * P], sm[:, i % 2, e, :], ACT.Exp,
                                       bias=nb[:, i, e:e + 1], scale=s.q_scale[:, 0, i, e:e + 1],
                                       accum_out=rs[:, i, e:e + 1]).then_inc(exp_done, 1)
                if i >= 2:
                    copy_turned(i - 2)

        @block.vector
        def _(dve):
            def mask(i):
                dve.wait_ge(scores, i + 1)
                if i >= 2:
                    dve.wait_ge(exp_done, 2 * (i - 1))
                for e in range(2):
                    dve.tensor_tensor_reduce(sm[:, i % 2, e, :], s_bank(i)[:, e, :],
                                             s.band[:, int(i % SEQ_TILES == 0), :], 1.0, MASKED * 10,
                                             ALU.add, ALU.max, mx[:, i, e:e + 1]).then_inc(masked, 1)
                dve.wait_ge(masked, 2 * i + 2)
                dve.tensor_tensor(nb[:, i, :], mx[:, i, :], s.q_scale[:, 1, i, :], ALU.mult).then_inc(bias_done, 1)

            def invert(i):
                dve.wait_ge(exp_done, 2 * i + 2)
                dve.reciprocal(ri[:, i, :], rs[:, i, :]).then_inc(inverse, 1)

            def take_out(n):
                dve.wait_ge(values_done, 4 * n + 4)
                dve.tensor_copy(s.o[:, j, n * CHUNK:(n + 1) * CHUNK], k.psum[:, 4 + n % 2, :]).then_inc(out_done, 1)

            for i in range(TILES + 1):
                if i < TILES:
                    mask(i)
                if i:
                    invert(i - 1)
                if i >= 4 + 4 and i % 4 == 0:
                    take_out(i // 4 - 2)
            take_out(3)

        @block.gpsimd
        def _(pool):
            pool.memset(pr[:, :, :, 0:WINDOW], 0.0).then_inc(cleared, 1)
            for i in range(TILES):
                pool.wait_ge(inverse, i + 1)
                if i == 0:
                    pool.wait_ge(cleared, 1)
                pool.tensor_tensor(pr[:, i % 2, :, WINDOW:2 * P], pr[:, i % 2, :, WINDOW:2 * P],
                                   ri[:, i, :].unsqueeze(2).broadcast_to([P, 2, KEYS]), ALU.mult).then_inc(scaled, 1)


def output_projection(nc, k, s):
    with rearmed(nc, "wo_ready", "wo_added") as (ready, added), nc.Block() as block:
        @block.tensor
        def _(pe):
            for c in range(CHUNKS):
                for j in range(PAIRS):
                    last = pe.matmul(k.psum[:, c, :], s.wo[:, j, :], s.o[:, j, c * CHUNK:(c + 1) * CHUNK],
                                     start=j == 0, stop=j == PAIRS - 1)
                last.then_inc(ready, 1)

        @block.vector
        def _(dve):
            for c in range(CHUNKS):
                at = slice(c * CHUNK, (c + 1) * CHUNK)
                dve.wait_ge(ready, c + 1)
                dve.tensor_tensor(s.y[:, at], s.y[:, at], k.psum[:, c, :], ALU.add).then_inc(added, 1)
            dve.wait_ge(added, CHUNKS)
            shift_tokens(dve, s)


def geglu(nc, k, s):
    NT = len(HID_TILES)
    with (rearmed(nc, "ffn_a", "ffn_g", "ffn_gelu", "ffn_gated", "ffn_out", "ffn_added") as
          (a_ready, g_ready, gelu_done, gated, out_ready, added),
          nc.sbuf_tensor("ffn_gelu_x", [P, 2, NT, CHUNK], F32) as gelu,
          nc.sbuf_tensor("ffn_hidden", [P, 2, NT, CHUNK], F32) as hid,
          nc.Block() as block):
        @block.tensor
        def _(pe):
            def up(c):
                for i, m in enumerate(HID_TILES):
                    if c:
                        pe.wait_ge(gelu_done, NT * (c - 1) + i + 1)
                    pe.matmul(k.psum[0:m, 3 + i, :], s.w1[:, HID + i * P:HID + i * P + m],
                              s.h[:, c * CHUNK:(c + 1) * CHUNK], start=True, stop=True).then_inc(g_ready, 1)
                for i, m in enumerate(HID_TILES):
                    if c:
                        pe.wait_ge(gated, NT * (c - 1) + i + 1)
                    pe.matmul(k.psum[0:m, i, :], s.w1[:, i * P:i * P + m],
                              s.h[:, c * CHUNK:(c + 1) * CHUNK], start=True, stop=True).then_inc(a_ready, 1)

            def down(c):
                pe.wait_ge(gated, NT * (c + 1))
                if c >= 2:
                    pe.wait_ge(added, c - 1)
                for i, m in enumerate(HID_TILES):
                    last = pe.matmul(k.psum[:, 6 + c % 2, :], s.w2[0:m, i, :], hid[0:m, c % 2, i, :],
                                     start=i == 0, stop=i == NT - 1)
                last.then_inc(out_ready, 1)

            up(0)
            for c in range(CHUNKS):
                if c + 1 < CHUNKS:
                    up(c + 1)
                down(c)

        @block.scalar
        def _(act):
            for c in range(CHUNKS):
                for i, m in enumerate(HID_TILES):
                    act.wait_ge(g_ready, NT * c + i + 1)
                    if c >= 2:
                        act.wait_ge(gated, NT * (c - 2) + i + 1)
                    act.activation(gelu[0:m, c % 2, i, :], k.psum[0:m, 3 + i, :], ACT.Gelu,
                                   bias=s.cols[0:m, B1_G + i:B1_G + i + 1]).then_inc(gelu_done, 1)

        @block.vector
        def _(dve):
            for c in range(CHUNKS + 1):
                if c < CHUNKS:
                    for i, m in enumerate(HID_TILES):
                        dve.wait_ge(a_ready, NT * c + i + 1)
                        dve.wait_ge(gelu_done, NT * c + i + 1)
                        if c >= 2:
                            dve.wait_ge(out_ready, c - 1)
                        dve.scalar_tensor_tensor(hid[0:m, c % 2, i, :], k.psum[0:m, i, :],
                                                 s.cols[0:m, B1_A + i:B1_A + i + 1], gelu[0:m, c % 2, i, :],
                                                 ALU.add, ALU.mult).then_inc(gated, 1)
                if c:
                    at = slice((c - 1) * CHUNK, c * CHUNK)
                    dve.wait_ge(out_ready, c)
                    dve.scalar_tensor_tensor(s.y[:, at], k.psum[:, 6 + (c - 1) % 2, :], s.cols[:, B2:B2 + 1],
                                             s.y[:, at], ALU.add, ALU.add).then_inc(added, 1)


def add_heads(nc, k, tag, h):
    loaded, turned, same_done, z_done = sems(nc, *(f"{tag}_{n}" for n in (
        "z_loaded", "z_turned", "z_compared", "z_guarded")))
    with (nc.sbuf_tensor(f"{tag}_z_raw", [P, TILES, DIM], F32) as raw,
          nc.sbuf_tensor(f"{tag}_z_same", [P, TILES, DIM], F32) as same,
          nc.sbuf_tensor(f"{tag}_z_tok", [P, TILES, DIM], F32) as z, nc.Block() as block):
        @block.sync
        def _(sp):
            rows = k.z.rearrange("b h (n q) d -> (b h n) (q d)", q=DIM // HEAD_DIM)
            sp.dma_start(raw[:, :, :], rows.rearrange("(t p) c -> p t c", p=P)).then_inc(loaded, 16)

        @block.tensor
        def _(pe):
            pe.wait_ge(z_done, 1)
            for c in range(CHUNKS):
                for t in range(4):
                    last = pe.transpose(k.psum[:, c, t * P:(t + 1) * P], z[:, 4 * c + t, :], k.ident[:, :])
                last.then_inc(turned, 1)

        @block.vector
        def _(dve):
            dve.memset(z[:, :, :], 0.0).then_inc(same_done, 1)
            dve.wait_ge(loaded, 16)
            dve.tensor_tensor(same[:, :, :], raw[:, :, :], raw[:, :, :], ALU.is_equal).then_inc(same_done, 1)
            dve.wait_ge(same_done, 2)
            dve.copy_predicated(z[:, :, :], same[:, :, :].bitcast(mybir.dt.uint32), raw[:, :, :]).then_inc(z_done, 1)
            for c in range(CHUNKS):
                at = slice(c * CHUNK, (c + 1) * CHUNK)
                dve.wait_ge(turned, c + 1)
                dve.tensor_tensor(h[:, at], h[:, at], k.psum[:, c, :], ALU.add)


def causal_block(nc, k, A, part):
    with ExitStack() as a:
        k.v_ch = a.enter_context(nc.sbuf_tensor("v_ch1", [P, TOK], F32))
        k.v_tok = a.enter_context(nc.sbuf_tensor("v_tok1", [P, SEQ_TILES, UNITS, 32], F32))
        k.att = a.enter_context(nc.sbuf_tensor("att1", [P, SEQ_TILES, UNITS, 32], F32))
        h = a.enter_context(nc.sbuf_tensor("h1", [P, TOK], F32))
        norm = a.enter_context(nc.sbuf_tensor("norm_cols", [P, 2], F32))
        (loaded,) = sems(nc, "norm_cols_loaded")
        with nc.Block() as block:
            @block.sync
            def _(sp):
                sp.dma_start(norm[:, :], A["norm_cols"]).then_inc(loaded, 16)
                sp.wait_ge(loaded, 16)
        layer_norm(nc, k, "ln2", k.x, h, part(1, 1), part(1, 0))
        project_heads(nc, k, "plain", h, A, False)
        attention(nc, k, "att1", 1.0 / float(np.sqrt(SEQ)), True)
        add_heads(nc, k, "z", h)
        layer_norm(nc, k, "ln3", h, h, lambda b: norm[:, 0:1], lambda b: norm[:, 1:2], residual=(k.x, part(1, 2)))


def experts(nc, k, A, part):
    with ExitStack() as ctx:
        def sb(name, shape, dt=F32):
            return ctx.enter_context(nc.sbuf_tensor(f"moe_{name}", shape, dt))

        cur = sb("cur", [P, TOK])
        layer_norm(nc, k, "ln4", k.x, cur, part(1, 4), part(1, 3))
        acc = sb("acc", [P, TILES, DIM])
        w1 = sb("w1", [P, EXPERTS, FF])
        w2 = sb("w2", [P, EXPERTS, FF_TILES, DIM])
        b1 = sb("b1", [P, EXPERTS, FF_TILES])
        b2 = sb("b2", [P, EXPERTS, DIM])
        wg = sb("wg", [P, ROUNDS, EXPERTS])
        bg = sb("bg", [P, ROUNDS, EXPERTS])
        hidden = sb("hidden", [P, 2, FF_TILES, CHUNK])
        bias = sb("bias_sum", [P, TILES, DIM])
        bias_e = sb("bias_term", [P, TILES, DIM])
        wg_r = sb("wg_round", [P, EXPERTS])
        bg_r = sb("bg_round", [P, EXPERTS])
        logit = sb("logit", [P, TILES, EXPERTS])
        top = sb("top", [P, TILES])
        ex = sb("exp", [P, TILES, EXPERTS])
        rank = sb("rank", [P, TILES, EXPERTS])
        wins = sb("wins", [P, TILES, EXPERTS])
        weight = sb("weight", [P, TILES, EXPERTS])
        total = sb("total", [P, TILES])
        cols = [slice(c * CHUNK, (c + 1) * CHUNK) for c in range(CHUNKS)]

        def wide(ap):
            return ap.broadcast_to([P, TILES, EXPERTS])

        loads = [(w1[:, :, :], A["moe_w1"]), (w2[:, :, :, :], A["moe_w2"]), (b1[:, :, :], A["moe_b1"]),
                 (b2[:, :, :], A["moe_b2"]), (wg[:, :, :], A["moe_wg"]), (bg[:, :, :], A["moe_bg"])]
        loaded, turned = sems(nc, "moe_loaded", "moe_turned")
        with nc.Block() as block:
            @block.sync
            def _(sp):
                for dst, src in loads:
                    sp.dma_start(dst, src).then_inc(loaded, 16)
                sp.wait_ge(loaded, 16 * len(loads))

            @block.tensor
            def _(pe):
                for c in range(CHUNKS):
                    for t in range(4):
                        last = pe.transpose(k.psum[:, c, t * P:(t + 1) * P],
                                            cur[:, c * CHUNK + t * P:c * CHUNK + (t + 1) * P], k.ident[:, :])
                    last.then_inc(turned, 1)

            @block.vector
            def _(dve):
                for c in range(CHUNKS):
                    dve.wait_ge(turned, c + 1)
                    dve.tensor_copy(acc[:, 4 * c:4 * c + 4, :], k.psum[:, c, :].rearrange("p (t n) -> p t n", t=4))

        NSTEP = CHUNKS * EXPERTS
        with (nc.Fori(0, ROUNDS) as r,
              rearmed(nc, "moe_gate_weights", "moe_logits", "moe_shifted", "moe_exp", "moe_gate_chain", "moe_weights",
                      "moe_bias_chain", "moe_bias", "moe_up", "moe_gelu", "moe_down", "moe_combined", "moe_acc_chain",
                      "moe_acc_turned", "moe_cur") as
              (gate_w, logits, shifted, exped, chain, weights, bias_chain, biased, up_done, gelu_done, down_done,
               combined, acc_chain, acc_turned, cur_done),
              nc.Block() as block):
            @block.tensor
            def _(pe):
                def up(n):
                    c, e = n // EXPERTS, n % EXPERTS
                    for f in range(FF_TILES):
                        if n:
                            pe.wait_ge(gelu_done, FF_TILES * (n - 1) + f + 1)
                        pe.matmul(k.psum[:, f, :], w1[:, e, f * P:(f + 1) * P], cur[:, cols[c]],
                                  start=True, stop=True).then_inc(up_done, 1)

                def down(n):
                    e = n % EXPERTS
                    pe.wait_ge(gelu_done, FF_TILES * (n + 1))
                    if n >= 2:
                        pe.wait_ge(combined, n - 1)
                    for t in range(4):
                        for f in range(FF_TILES):
                            last = pe.matmul(k.psum[:, 4 + n % 2, t * P:(t + 1) * P],
                                             hidden[:, n % 2, f, t * P:(t + 1) * P], w2[:, e, f, :],
                                             start=f == 0, stop=f == FF_TILES - 1)
                    last.then_inc(down_done, 1)

                def turn(c):
                    pe.wait_ge(combined, EXPERTS * (c + 1))
                    if c >= 2:
                        pe.wait_ge(cur_done, c - 1)
                    for t in range(4):
                        last = pe.transpose(k.psum[:, 6 + c % 2, t * P:(t + 1) * P], acc[:, 4 * c + t, :],
                                            k.ident[:, :])
                    last.then_inc(acc_turned, 1)

                pe.wait_ge(gate_w, 2)
                for t in range(TILES):
                    last = pe.matmul(k.psum[:, 6, t * EXPERTS:(t + 1) * EXPERTS], cur[:, t * P:(t + 1) * P],
                                     wg_r[:, :], start=True, stop=True)
                last.then_inc(logits, 1)
                up(0)
                for n in range(NSTEP):
                    if n + 1 < NSTEP:
                        up(n + 1)
                    down(n)
                    if n % EXPERTS == 0 and n:
                        turn(n // EXPERTS - 1)
                turn(CHUNKS - 1)

            @block.scalar
            def _(act):
                act.wait_ge(shifted, 1)
                act.activation(ex[:, :, :], ex[:, :, :], ACT.Exp).then_inc(exped, 1)
                for n in range(NSTEP):
                    e = n % EXPERTS
                    if n >= 2:
                        act.wait_ge(down_done, n - 1)
                    for f in range(FF_TILES):
                        act.wait_ge(up_done, FF_TILES * n + f + 1)
                        act.activation(hidden[:, n % 2, f, :], k.psum[:, f, :], ACT.Gelu_apprx_tanh,
                                       bias=b1[:, e, f:f + 1]).then_inc(gelu_done, 1)

            @block.gpsimd
            def _(pool):
                pool.tensor_copy(wg_r[:, :], wg[:, r, :]).then_inc(gate_w, 1)
                pool.tensor_copy(bg_r[:, :], bg[:, r, :]).then_inc(gate_w, 1)
                pool.wait_ge(weights, 1)
                m = 0
                for e in range(EXPERTS):
                    dst = bias if e == 0 else bias_e
                    pool.tensor_tensor(dst[:, :, :], b2[:, e, :].unsqueeze(1).broadcast_to([P, TILES, DIM]),
                                       weight[:, :, e:e + 1].broadcast_to([P, TILES, DIM]), ALU.mult)\
                        .then_inc(bias_chain, 1)
                    m += 1
                    if e:
                        pool.wait_ge(bias_chain, m)
                        pool.tensor_tensor(bias[:, :, :], bias[:, :, :], bias_e[:, :, :], ALU.add)\
                            .then_inc(bias_chain if e + 1 < EXPERTS else biased, 1)
                        m += 1
                        if e + 1 < EXPERTS:
                            pool.wait_ge(bias_chain, m)

            @block.vector
            def _(dve):
                n = [0]

                def link(ins):
                    n[0] += 1
                    ins.then_inc(chain, 1)
                    dve.wait_ge(chain, n[0])

                dve.wait_ge(logits, 1)
                dve.wait_ge(gate_w, 2)
                link(dve.tensor_tensor(logit[:, :, :],
                                       k.psum[:, 6, 0:TILES * EXPERTS].rearrange("p (t e) -> p t e", e=EXPERTS),
                                       bg_r[:, :].unsqueeze(1).broadcast_to([P, TILES, EXPERTS]), ALU.add))
                link(dve.tensor_reduce(top[:, :], logit[:, :, :], AX.X, ALU.max))
                dve.tensor_tensor(ex[:, :, :], logit[:, :, :], wide(top[:, :].unsqueeze(2)), ALU.subtract)\
                   .then_inc(shifted, 1)
                for e in range(EXPERTS):
                    dve.memset(rank[:, :, e:e + 1], float(EXPERTS - 1 - e)).then_inc(chain, 1)
                    n[0] += 1
                for d in range(1, EXPERTS):
                    m = EXPERTS - d
                    link(dve.tensor_tensor(wins[:, :, 0:m], logit[:, :, 0:m], logit[:, :, d:EXPERTS], ALU.is_ge))
                    link(dve.tensor_tensor(rank[:, :, d:EXPERTS], rank[:, :, d:EXPERTS], wins[:, :, 0:m], ALU.add))
                    link(dve.tensor_tensor(rank[:, :, 0:m], rank[:, :, 0:m], wins[:, :, 0:m], ALU.subtract))
                link(dve.tensor_scalar(rank[:, :, :], rank[:, :, :], 2.0, None, ALU.is_lt))
                dve.wait_ge(exped, 1)
                link(dve.tensor_tensor(ex[:, :, :], ex[:, :, :], rank[:, :, :], ALU.mult))
                link(dve.tensor_reduce(total[:, :], ex[:, :, :], AX.X, ALU.add))
                link(dve.reciprocal(total[:, :], total[:, :]))
                dve.tensor_tensor(weight[:, :, :], ex[:, :, :], wide(total[:, :].unsqueeze(2)), ALU.mult)\
                   .then_inc(weights, 1)
                dve.wait_ge(weights, 1)
                for i in range(NSTEP):
                    c, e = i // EXPERTS, i % EXPERTS
                    dve.wait_ge(down_done, i + 1)
                    if i:
                        dve.wait_ge(combined, i)
                    for t in range(4):
                        tile = 4 * c + t
                        last = dve.scalar_tensor_tensor(acc[:, tile, :], k.psum[:, 4 + i % 2, t * P:(t + 1) * P],
                                                        weight[:, tile, e:e + 1], acc[:, tile, :], ALU.mult, ALU.add)
                        if t < 3 or e == EXPERTS - 1:
                            last.then_inc(acc_chain, 1)
                    if e == EXPERTS - 1:
                        dve.wait_ge(biased, 1)
                        dve.wait_ge(acc_chain, 3 * i + 3 + (c + 1))
                        last = dve.tensor_tensor(acc[:, 4 * c:4 * c + 4, :], acc[:, 4 * c:4 * c + 4, :],
                                                 bias[:, 4 * c:4 * c + 4, :], ALU.add)
                    last.then_inc(combined, 1)
                    if e == 1 and c:
                        dve.wait_ge(acc_turned, c)
                        dve.tensor_copy(cur[:, cols[c - 1]], k.psum[:, 6 + (c - 1) % 2, :]).then_inc(cur_done, 1)
                dve.wait_ge(acc_turned, CHUNKS)
                dve.tensor_copy(cur[:, cols[CHUNKS - 1]], k.psum[:, 6 + (CHUNKS - 1) % 2, :]).then_inc(cur_done, 1)

        with nc.Block() as block:
            @block.vector
            def _(dve):
                for c in range(CHUNKS):
                    dve.scalar_tensor_tensor(k.x[:, cols[c]], cur[:, cols[c]], part(1, 5)(c * CHUNK // SEQ),
                                             k.x[:, cols[c]], ALU.mult, ALU.add)


def build(nc, A, out, stages="ABCD"):
    k = Core()
    k.A = A
    with ExitStack() as ctx:
        def sb(name, shape, dt=F32):
            return ctx.enter_context(nc.sbuf_tensor(name, shape, dt))

        k.x = sb("x_ch", [P, TOK])
        k.ident = sb("ident", [P, P])
        k.ident_bf = sb("ident_bf", [P, P], BF16)
        k.ones_mean = sb("ones_mean_sb", [P, P])
        k.c = sb("c_cols", [P, 2 * BATCH])
        k.eps = sb("eps", [P, 1])
        k.mod = sb("mod", [P, 2, 6, BATCH])
        k.psum = ctx.enter_context(nc.psum_tensor("psum", [P, 8, 512], F32))
        k.parts = nc.dram_tensor("qk_parts", (2, 3, BATCH, GROUPS, HEAD_DIM, GROUP, SEQ), BF16).ap()
        k.z = nc.dram_tensor("z_heads", (BATCH, HEADS, SEQ, HEAD_DIM), F32).ap()
        load_residents(nc, k, A)
        modulation(nc, k, A)
        m = k.mod

        def part(l, i):
            return lambda b: m[:, l, i, b:b + 1]

        if "A" in stages:
            with scope(nc), ExitStack() as a:
                k.v_ch = a.enter_context(nc.sbuf_tensor("v_ch0", [P, TOK], F32))
                k.v_tok = a.enter_context(nc.sbuf_tensor("v_tok0", [P, SEQ_TILES, UNITS, 32], F32))
                k.att = a.enter_context(nc.sbuf_tensor("att0", [P, SEQ_TILES, UNITS, 32], F32))
                with nc.sbuf_tensor("h0", [P, TOK], F32) as h:
                    layer_norm(nc, k, "ln0", k.x, h, part(0, 1), part(0, 0))
                    project_heads(nc, k, "rot", h, A, True)
                attention(nc, k, "att0", 1.0 / float(np.sqrt(HEAD_DIM)), False)
                residual_attention(nc, k, "res0", A)
        if "B" in stages:
            with scope(nc):
                windowed_layers(nc, k, A, part)
        if "C" in stages:
            with scope(nc):
                causal_block(nc, k, A, part)
        if "D" in stages:
            with scope(nc):
                experts(nc, k, A, part)
        (stored,) = sems(nc, "x_stored")
        with nc.Block() as block:
            @block.sync
            def _(sp):
                sp.dma_start(out, k.x[:, :]).then_inc(stored, 16)
                sp.wait_ge(stored, 16)


def lay_out(inputs):
    i = {n: np.asarray(a) for n, a in inputs.items()}
    f = np.ascontiguousarray
    A = dict(shape_constants())
    A["x"] = f(i["L0_attn_x"].reshape(TOK, DIM).T)
    A["c"] = f(np.concatenate([i["L0_c"], i["L1_c"]]).T)
    A["wmod0"], A["wmod1"] = i["L0_wmod"], i["L1_wmod"]
    def by_channel(t):
        qk = t[..., :2 * DIM].reshape(t.shape[:-1] + (2, GROUPS, GROUP, HEAD_DIM)).swapaxes(-1, -2)
        return np.concatenate([qk.reshape(t.shape[:-1] + (2 * DIM,)), t[..., 2 * DIM:]], -1)

    A["rot_w"] = f(by_channel(i["L0_attn_w_qkv"].T))
    A["rot_b"] = f(by_channel(i["L0_attn_b_qkv"]).reshape(3, DIM).T)
    A["lepe"] = f(np.concatenate([i["L0_attn_w_lepe"][:, 0, :], i["L0_attn_b_lepe"][:, None]], 1))
    A["plain_w"] = f(by_channel(np.concatenate([i[f"L1_attn_W{n}"].T for n in "qkv"], 1)))
    A["plain_b"] = f(by_channel(np.concatenate([i[f"L1_attn_b{n}"] for n in "qkv"])).reshape(3, DIM).T)
    A["norm_cols"] = f(np.stack([i["L1_attn_gamma"], i["L1_attn_beta"]], 1))
    A["moe_w1"] = f(i["L1_ffn_W1"].transpose(1, 0, 2))
    A["moe_w2"] = f(i["L1_ffn_W2"].reshape(EXPERTS, FF_TILES, P, DIM).transpose(2, 0, 1, 3))
    A["moe_b1"] = f(i["L1_ffn_b1"].reshape(EXPERTS, FF_TILES, P).transpose(2, 0, 1))
    A["moe_b2"] = f(np.broadcast_to(i["L1_ffn_b2"][None], (P, EXPERTS, DIM)))
    A["moe_wg"] = f(i["L1_ffn_Wg"].transpose(1, 0, 2))
    A["moe_bg"] = f(np.broadcast_to(i["L1_ffn_bg"][None], (P, ROUNDS, EXPERTS)))
    rot = (np.arange(W_DIM) + W_DIM // 2) % W_DIM
    wqkv = i["L0_ffn_wqkv"].reshape(DEPTH, DIM, 3, PAIRS, 2, W_DIM)
    turned = wqkv[..., rot]
    five = np.stack([wqkv[:, :, 0], turned[:, :, 0], wqkv[:, :, 1], turned[:, :, 1], wqkv[:, :, 2]], 2)
    five = five.reshape(DEPTH, DIM, 5, PAIRS, P).transpose(0, 3, 1, 2, 4).reshape(DEPTH * PAIRS, DIM, 5, P)
    A["win_wj"] = f(np.concatenate([five, five[-1:]]))
    A["win_wo"] = f(i["L0_ffn_wo"].reshape(DEPTH, PAIRS, P, DIM).transpose(0, 2, 1, 3))
    A["win_w1"] = f(i["L0_ffn_w1"])
    w2 = np.pad(i["L0_ffn_w2"], ((0, 0), (0, 3 * P - HID), (0, 0)))
    A["win_w2"] = f(w2.reshape(DEPTH, 3, P, DIM).transpose(0, 2, 1, 3))
    cols = np.zeros((DEPTH, P, COLS), np.float32)
    for n, name in enumerate(("L0_ffn_q_scale", "L0_ffn_k_scale")):
        cols[:, :, SCALES + 2 * n] = np.tile(i[name], (1, 2))
        cols[:, :, SCALES + 2 * n + 1] = np.tile(i[name][:, rot], (1, 2))
    cols[:, :, LN_G], cols[:, :, LN_B], cols[:, :, B2] = i["L0_ffn_ln_g"], i["L0_ffn_ln_b"], i["L0_ffn_b2"]
    for n, m in enumerate(HID_TILES):
        cols[:, :m, B1_A + n] = i["L0_ffn_b1"][:, n * P:n * P + m]
        cols[:, :m, B1_G + n] = i["L0_ffn_b1"][:, HID + n * P:HID + n * P + m]
    A["win_cols"] = cols
    return A


def kernel(**inputs):
    import concourse.bacc as bacc
    from concourse.bass_utils import run_bass_kernel_spmd

    nc = bacc.Bacc("TRN2", target_bir_lowering=False, num_devices=1)
    arrays = {f"in_{n}": a for n, a in lay_out(inputs).items()}
    A = {n[3:]: nc.dram_tensor(n, a.shape, mybir.dt.from_np(a.dtype), kind="ExternalInput").ap()
         for n, a in arrays.items()}
    out = nc.dram_tensor("out_x", (DIM, TOK), F32, kind="ExternalOutput").ap()
    build(nc, A, out)
    run = run_bass_kernel_spmd(nc, [arrays], core_ids=[0])
    return np.ascontiguousarray(run.results[0]["out_x"].T).reshape(BATCH, SEQ, DIM)
```

```python
from contextlib import ExitStack, contextmanager

import numpy as np

import concourse.bass as bass
import concourse.mybir as mybir

F32 = mybir.dt.float32
BF16 = mybir.dt.bfloat16
F32R = mybir.dt.float32r
ALU = mybir.AluOpType
ACT = mybir.ActivationFunctionType
AX = mybir.AxisListType

P = 128
BATCH, SEQ, DIM = 2, 1024, 128
TOK = BATCH * SEQ
CHUNK = 512
CHUNKS = TOK // CHUNK
TILES = TOK // P
SEQ_TILES = SEQ // P
EPS = 1e-5

HEADS, HEAD_DIM = 16, 8
GROUP = 4
GROUPS = HEADS // GROUP
UNITS = GROUPS * BATCH
SPLIT_ROWS = 9 * HEAD_DIM
ROWS = SPLIT_ROWS + 2
RING = 3

DEPTH, W_HEADS, W_DIM, WINDOW, HID = 2, 8, 64, 64, 341
INNER = W_HEADS * W_DIM
PAIRS = W_HEADS // 2
QK_SCALE = 8.0
KEYS = P + WINDOW
MASKED = -1e37
HID_TILES = (128, 128, 85)

ROUNDS, EXPERTS, FF = 4, 4, 512
FF_TILES = FF // P


def high_part(dve, dst, src):
    return dve.tensor_copy(dst, src)


def low_part(dve, dst, src, high):
    return dve.tensor_tensor(dst, src, high.bitcast(F32), ALU.subtract)


def matmul_split(pe, out, w_high, w_low, x_high, x_low, start=True, stop=True):
    pe.matmul(out, w_high, x_high, start=start, stop=False)
    pe.matmul(out, w_high, x_low, start=False, stop=False)
    return pe.matmul(out, w_low, x_high, start=False, stop=stop)


def shape_constants():
    f = np.float32
    c = {}
    c["identity"] = np.eye(P, dtype=f)
    c["ones_mean"] = np.full((P, P), 1.0 / P, f)
    swap = np.zeros((P, P), f)
    swap[np.arange(P), np.arange(P) ^ GROUP] = 1
    c["pair_swap"] = swap
    pair = np.zeros((P, P), f)
    pair[:W_DIM, :W_DIM] = 1
    pair[W_DIM:, W_DIM:] = 1
    c["head_ones"] = pair
    half = np.arange(0, HEAD_DIM, 2, dtype=f)
    div = np.exp(half * f(-np.log(10000.0) / HEAD_DIM)).astype(f)
    ang = np.arange(SEQ, dtype=f)[:, None] * div
    cos, sin = np.cos(ang).astype(f), np.sin(ang).astype(f)
    d = np.arange(P) // GROUP % HEAD_DIM
    c["rope_cos"] = np.ascontiguousarray(cos[:, d // 2].T)
    c["rope_sin"] = np.ascontiguousarray((sin[:, d // 2] * np.where(d % 2, 1, -1).astype(f)).T)
    half = np.arange(0, W_DIM, 2, dtype=f)
    inv = (f(1.0) / f(10000.0) ** (half / f(W_DIM))).astype(f)
    t = np.arange(SEQ, dtype=f)
    freqs = t[:, None] * inv[None, :]
    base = ((half + f(0.4 * W_DIM)) / f(1.4 * W_DIM)).astype(f)
    power = (t - SEQ // 2) / f(WINDOW // 2)
    scale = (base[None, :] ** power[:, None]).astype(f)
    cos, sin = np.cos(freqs).astype(f), np.sin(freqs).astype(f)
    d = np.arange(P) % W_DIM
    sign = np.where(d < W_DIM // 2, -1, 1).astype(f)[:, None]
    i = d % (W_DIM // 2)
    c["xpos"] = np.stack([(cos * scale).T[i], (sin * scale).T[i] * sign,
                          (cos / scale).T[i], (sin / scale).T[i] * sign], 1).astype(f)
    q, j = np.arange(P)[:, None], np.arange(KEYS)[None, :]
    band = np.where((j >= q) & (j <= q + WINDOW), 0.0, MASKED).astype(f)
    first = np.where(j < WINDOW, f(MASKED), band).astype(f)
    c["band"] = np.stack([band, first], 1)
    c["triangle"] = np.tril(np.ones((P, P), f))
    return c


class Core:
    pass


def sems(nc, *names):
    return [nc.alloc_semaphore(n) for n in names]


@contextmanager
def scope(nc):
    before = nc.snapshot_sems()
    yield
    nc.clear_and_free_semaphores(nc.allocated_since(before))
    nc.all_engine_barrier()


@contextmanager
def rearmed(nc, *names):
    with scope(nc):
        yield sems(nc, *names)


def load_residents(nc, k, A):
    loads = [(k.x[:, :], A["x"]), (k.ident[:, :], A["identity"]), (k.ones_mean[:, :], A["ones_mean"]),
             (k.c[:, :], A["c"])]
    (loaded,) = sems(nc, "residents_loaded")
    with nc.Block() as block:
        @block.sync
        def _(sp):
            for dst, src in loads:
                sp.dma_start(dst, src).then_inc(loaded, 16)
            sp.wait_ge(loaded, 16 * len(loads))

        @block.vector
        def _(dve):
            dve.memset(k.eps[:, :], EPS)
            dve.wait_ge(loaded, 16 * len(loads))
            dve.tensor_copy(k.ident_bf[:, :], k.ident[:, :])


def modulation(nc, k, A):
    PARTS = 6
    w_in, silu, mods, exps, chain = sems(nc, "wmod_loaded", "silu_ready", "mod_ready", "exp_ready", "mod_chain")
    ctx = ExitStack()
    with ctx:
        w = ctx.enter_context(nc.sbuf_tensor("wmod", [P, 2, PARTS * DIM], F32))
        e = ctx.enter_context(nc.sbuf_tensor("silu_tmp", [P, 4], F32))
        s = ctx.enter_context(nc.sbuf_tensor("silu_c", [P, 4], F32))
        t = ctx.enter_context(nc.sbuf_tensor("gate_tmp", [P, 2, 2, BATCH], F32))
        ps = k.psum[:, 0, 0:2 * PARTS * BATCH].rearrange("p (l m b) -> p l m b", l=2, b=BATCH)
        block = ctx.enter_context(nc.Block())

        @block.sync
        def _(sp):
            for l in range(2):
                sp.dma_start(w[:, l, :], A[f"wmod{l}"]).then_inc(w_in, 16)

        @block.scalar
        def _(act):
            act.activation(e[:, :], k.c[:, :], ACT.Exp, scale=-1.0).then_inc(exps, 1)

        @block.tensor
        def _(pe):
            pe.wait_ge(w_in, 32)
            pe.wait_ge(silu, 1)
            for l in range(2):
                for m in range(PARTS):
                    last = pe.matmul(ps[:, l, m, :], w[:, l, m * DIM:(m + 1) * DIM],
                                     s[:, l * BATCH:(l + 1) * BATCH], start=True, stop=True)
            last.then_inc(mods, 1)

        @block.vector
        def _(dve):
            n = [0]

            def link(ins):
                n[0] += 1
                ins.then_inc(chain, 1)
                dve.wait_ge(chain, n[0])

            dve.wait_ge(exps, 1)
            link(dve.tensor_scalar(e[:, :], e[:, :], 1.0, None, ALU.add))
            link(dve.reciprocal(e[:, :], e[:, :]))
            dve.tensor_tensor(s[:, :], k.c[:, :], e[:, :], ALU.mult).then_inc(silu, 1)
            dve.wait_ge(mods, 1)
            link(dve.tensor_copy(k.mod[:, :, :, :], ps))
            link(dve.tensor_scalar(k.mod[:, :, 1::3, :], k.mod[:, :, 1::3, :], 1.0, None, ALU.add))
            link(dve.tensor_scalar(t[:, :, :, :], k.mod[:, :, 2::3, :], 0.0, 2.0, ALU.is_ge, ALU.mult))
            link(dve.tensor_scalar(t[:, :, :, :], t[:, :, :, :], -1.0, None, ALU.add))
            link(dve.tensor_tensor(k.mod[:, :, 2::3, :], k.mod[:, :, 2::3, :], t[:, :, :, :], ALU.mult))
            link(dve.tensor_scalar(k.mod[:, :, 2::3, :], k.mod[:, :, 2::3, :], 0.25, None, ALU.max))
            link(dve.tensor_tensor(k.mod[:, :, 2::3, :], k.mod[:, :, 2::3, :], t[:, :, :, :], ALU.mult))


LN_SEMS = ("mean", "centred", "squared", "var", "rooted", "inverse", "spread", "scaled", "shifted")


def layer_norm(nc, k, tag, src, dst, scale, shift, residual=None, names=sems):
    mean, centred, squared, var, rooted, inverse, spread, scaled, shifted = names(nc, *(f"{tag}_{n}" for n in LN_SEMS))
    ctx = ExitStack()
    with ctx:
        d = ctx.enter_context(nc.sbuf_tensor(f"{tag}_centred_x", [P, TOK], F32))
        sq = ctx.enter_context(nc.sbuf_tensor(f"{tag}_square", [P, TOK], F32))
        dev = ctx.enter_context(nc.sbuf_tensor(f"{tag}_deviation", [P, TILES], F32))
        inv = ctx.enter_context(nc.sbuf_tensor(f"{tag}_inverse", [P, TILES], F32))
        at = [slice(c * CHUNK, (c + 1) * CHUNK) for c in range(CHUNKS)]
        tiles = [slice(4 * c, 4 * c + 4) for c in range(CHUNKS)]
        var_bank = [k.psum[:, 4 + c % 2, 4 * c:4 * c + 4] for c in range(CHUNKS)]
        spread_bank = [k.psum[:, i, :] for i in (6, 7, 0, 1)]
        block = ctx.enter_context(nc.Block())

        @block.tensor
        def _(pe):
            for c in range(CHUNKS):
                pe.matmul(k.psum[:, c, :], k.ones_mean[:, :], src[:, at[c]], start=True, stop=True).then_inc(mean, 1)

            def variance(c):
                pe.wait_ge(squared, c + 1)
                if c >= 2:
                    pe.wait_ge(rooted, c - 1)
                for t in range(4):
                    i = 4 * c + t
                    last = pe.matmul(var_bank[c][:, t:t + 1], sq[:, i * P:(i + 1) * P], k.ones_mean[:, 0:1],
                                     start=True, stop=True)
                last.then_inc(var, 1)

            def spread_inverse(c):
                pe.wait_ge(inverse, c + 1)
                for t in range(4):
                    i = 4 * c + t
                    last = pe.matmul(spread_bank[c][:, t * P:(t + 1) * P], inv[:, i:i + 1].broadcast_to([P, P]),
                                     k.ident[:, :], start=True, stop=True)
                last.then_inc(spread, 1)

            for c in range(CHUNKS + 1):
                if c < CHUNKS:
                    variance(c)
                if c:
                    spread_inverse(c - 1)

        @block.scalar
        def _(act):
            def square(c):
                act.wait_ge(centred, c + 1)
                act.activation(sq[:, at[c]], d[:, at[c]], ACT.Square).then_inc(squared, 1)

            def root(c):
                act.wait_ge(var, c + 1)
                act.activation(dev[:, tiles[c]], var_bank[c], ACT.Sqrt, bias=k.eps[:, 0:1]).then_inc(rooted, 1)

            def add_shift(c):
                act.wait_ge(scaled, c + 1)
                act.activation(dst[:, at[c]], d[:, at[c]], ACT.Identity, bias=shift(c * CHUNK // SEQ))\
                   .then_inc(shifted, 1)

            square(0)
            for c in range(CHUNKS):
                if c + 1 < CHUNKS:
                    square(c + 1)
                root(c)
                if c:
                    add_shift(c - 1)
            add_shift(CHUNKS - 1)

        @block.vector
        def _(dve):
            def centre(c):
                dve.wait_ge(mean, c + 1)
                dve.tensor_tensor(d[:, at[c]], src[:, at[c]], k.psum[:, c, :], ALU.subtract).then_inc(centred, 1)

            def invert(c):
                dve.wait_ge(rooted, c + 1)
                dve.reciprocal(inv[:, tiles[c]], dev[:, tiles[c]]).then_inc(inverse, 1)

            def rescale(c):
                dve.wait_ge(spread, c + 1)
                dve.scalar_tensor_tensor(d[:, at[c]], d[:, at[c]], scale(c * CHUNK // SEQ), spread_bank[c],
                                         ALU.mult, ALU.mult).then_inc(scaled, 1)

            centre(0)
            centre(1)
            for c in range(CHUNKS + 1):
                if c < CHUNKS:
                    invert(c)
                if c + 2 < CHUNKS:
                    centre(c + 2)
                if c:
                    rescale(c - 1)
            if residual:
                x, gate = residual
                for c in range(CHUNKS):
                    dve.wait_ge(shifted, c + 1)
                    dve.scalar_tensor_tensor(x[:, at[c]], dst[:, at[c]], gate(c * CHUNK // SEQ), x[:, at[c]],
                                             ALU.mult, ALU.add)


def project_heads(nc, k, tag, h, A, rotary):
    (w_in, projected, drained, floored, exped, feature, swapped, swap_drained, cosined, sined, operand, hi_done,
     rest1, mid_done, lo_done, stored, v_ps, v_done, v_turned, v_tok_done, v_clean) = sems(nc, *(f"{tag}_{n}" for n in (
        "weights_loaded", "projected", "projection_drained", "floored", "exp_done", "feature_ready", "pair_swapped",
        "swap_drained", "cos_done", "sin_done", "operand_ready", "hi_done", "rest1_done", "mid_done", "lo_done",
        "parts_stored", "v_projected", "v_ready", "v_turned", "v_tok_ready", "v_clean")))
    NU = 2 * CHUNKS
    ctx = ExitStack()
    with ctx:
        def sb(name, shape, dt=F32):
            return ctx.enter_context(nc.sbuf_tensor(f"{tag}_{name}", shape, dt))

        w = sb("w", [P, 3 * DIM])
        bias = sb("b", [P, 3])
        val = sb("val", [P, NU, CHUNK])
        part = [sb(n, [P, 2, TOK], BF16) for n in ("hi", "mid", "lo")]
        if rotary:
            tmp = sb("tmp", [P, NU, CHUNK])
            swap = sb("swap", [P, P])
            cos, sin = sb("cos", [P, SEQ]), sb("sin", [P, SEQ])
        else:
            same = sb("same", [P, TOK])
            vraw = sb("vraw", [P, TOK])
        loads = [(w[:, :], A[f"{tag}_w"]), (bias[:, :], A[f"{tag}_b"])]
        if rotary:
            loads += [(swap[:, :], A["pair_swap"]), (cos[:, :], A["rope_cos"]), (sin[:, :], A["rope_sin"])]
        bank = [k.psum[:, i, :] for i in range(8)]
        cols = [slice(c * CHUNK, (c + 1) * CHUNK) for c in range(CHUNKS)]

        def pos(s):
            return slice((s // 2) * CHUNK % SEQ, (s // 2) * CHUNK % SEQ + CHUNK)

        def of(t, s):
            return t[:, s % 2, cols[s // 2]]

        block = ctx.enter_context(nc.Block())

        @block.sync
        def _(sp):
            for dst, src in loads:
                sp.dma_start(dst, src).then_inc(w_in, 16)
            n = 0
            for b in range(BATCH):
                done = NU // BATCH * (b + 1)
                sp.wait_ge(lo_done, done)
                for which in range(2):
                    for i in range(3):
                        sp.dma_start(k.parts[which, i, b].rearrange("g d h t -> (g d h) t"), part[i][:, which, b * SEQ:(b + 1) * SEQ]).then_inc(stored, 16)
                        n += 1
            sp.wait_ge(stored, 16 * n)

        @block.tensor
        def _(pe):
            pe.wait_ge(w_in, 16 * len(loads))

            def project(s):
                if s >= 2:
                    pe.wait_ge(drained if rotary else operand, s - 1)
                pe.matmul(bank[s % 2], w[:, (s % 2) * DIM:(s % 2 + 1) * DIM], h[:, cols[s // 2]],
                          start=True, stop=True).then_inc(projected, 1)

            def swap_pairs(s):
                pe.wait_ge(feature, s + 1)
                if s >= 2:
                    pe.wait_ge(swap_drained, s - 1)
                pe.matmul(bank[2 + s % 2], swap[:, :], val[:, s, :], start=True, stop=True).then_inc(swapped, 1)

            def project_v(c):
                if c >= 2:
                    pe.wait_ge(v_done, c - 1)
                pe.matmul(bank[4 + c % 2], w[:, 2 * DIM:3 * DIM], h[:, cols[c]], start=True, stop=True)\
                    .then_inc(v_ps, 1)

            def turn_v(c):
                pe.wait_ge(v_done if rotary else v_clean, c + 1)
                if c >= 2:
                    pe.wait_ge(v_tok_done, c - 1)
                for t in range(4):
                    last = pe.transpose(bank[6 + c % 2][:, t * P:(t + 1) * P],
                                        k.v_ch[:, c * CHUNK + t * P:c * CHUNK + (t + 1) * P], k.ident[:, :])
                last.then_inc(v_turned, 1)

            for s in range(NU + 2):
                if s < NU:
                    project(s)
                if rotary and s >= 2:
                    swap_pairs(s - 2)
                if s % 2 == 0 and s < NU:
                    project_v(s // 2)
                if s % 2 == 1 and 3 <= s < NU + 2:
                    turn_v((s - 3) // 2)

        @block.scalar
        def _(act):
            act.wait_ge(w_in, 16 * len(loads))

            def exp_low(s):
                act.wait_ge(floored, s + 1)
                act.activation(tmp[:, s, :], tmp[:, s, :], ACT.Exp).then_inc(exped, 1)

            def biased(s):
                act.wait_ge(projected, s + 1)
                act.activation(val[:, s, :], bank[s % 2], ACT.Identity, bias=bias[:, s % 2:s % 2 + 1])\
                   .then_inc(operand, 1)

            def hi(s):
                act.wait_ge(operand, s + 1)
                act.activation(of(part[0], s), val[:, s, :], ACT.Copy).then_inc(hi_done, 1)

            def mid(s):
                act.wait_ge(rest1, s + 1)
                act.activation(of(part[1], s), val[:, s, :], ACT.Copy).then_inc(mid_done, 1)

            def v_bias(c):
                act.wait_ge(v_ps, c + 1)
                act.activation((k.v_ch if rotary else vraw)[:, cols[c]], bank[4 + c % 2], ACT.Identity,
                               bias=bias[:, 2:3]).then_inc(v_done, 1)

            def v_tok(c):
                act.wait_ge(v_turned, c + 1)
                b, t0 = c // 2, c % 2 * 4
                act.activation(k.v_tok[:, t0:t0 + 4, b * GROUPS:(b + 1) * GROUPS, :],
                               bank[6 + c % 2].rearrange("p (t g c) -> p t g c", t=4, c=32), ACT.Copy)\
                   .then_inc(v_tok_done, 1)

            for s in range(NU + 4):
                if s < NU:
                    (exp_low if rotary else biased)(s)
                if s % 2 == 0 and s < NU:
                    v_bias(s // 2)
                if 3 <= s < NU + 3:
                    hi(s - 3)
                if s >= 4:
                    mid(s - 4)
                if s % 2 == 1 and 3 <= s < NU + 2:
                    v_tok((s - 3) // 2)

        @block.vector
        def _(dve):
            dve.wait_ge(w_in, 16 * len(loads))

            def ramps(s):
                dve.wait_ge(projected, s + 1)
                b = bias[:, s % 2:s % 2 + 1]
                dve.tensor_scalar(tmp[:, s, :], bank[s % 2], b, 0.0, ALU.add, ALU.min).then_inc(floored, 1)
                dve.tensor_scalar(val[:, s, :], bank[s % 2], b, 0.0, ALU.add, ALU.max).then_inc(drained, 1)

            def times_cos(s):
                dve.wait_ge(feature, s + 1)
                dve.tensor_tensor(tmp[:, s, :], val[:, s, :], cos[:, pos(s)], ALU.mult).then_inc(cosined, 1)

            def times_sin(s):
                dve.wait_ge(swapped, s + 1)
                dve.wait_ge(cosined, s + 1)
                dve.tensor_tensor(val[:, s, :], bank[2 + s % 2], sin[:, pos(s)], ALU.mult).then_inc(swap_drained, 1)

            def less_hi(s):
                dve.wait_ge(hi_done, s + 1)
                dve.tensor_tensor(val[:, s, :], val[:, s, :], of(part[0], s), ALU.subtract).then_inc(rest1, 1)

            for s in range(NU + 4):
                if rotary and s < NU:
                    ramps(s)
                if rotary and 1 <= s < NU + 1:
                    times_cos(s - 1)
                if rotary and 2 <= s < NU + 2:
                    times_sin(s - 2)
                if s >= 4:
                    less_hi(s - 4)
                if not rotary and s % 2 == 1 and s < NU:
                    c = s // 2
                    dve.wait_ge(v_done, c + 1)
                    dve.tensor_tensor(same[:, cols[c]], vraw[:, cols[c]], vraw[:, cols[c]], ALU.is_equal)\
                       .then_inc(sined, 1)
                    dve.memset(k.v_ch[:, cols[c]], 0.0).then_inc(sined, 1)
                    dve.wait_ge(sined, 2 * c + 2)
                    dve.copy_predicated(k.v_ch[:, cols[c]], same[:, cols[c]].bitcast(mybir.dt.uint32),
                                        vraw[:, cols[c]]).then_inc(v_clean, 1)

        @block.gpsimd
        def _(pool):
            def feature_sum(s):
                pool.wait_ge(exped, s + 1)
                pool.wait_ge(drained, s + 1)
                pool.tensor_tensor(val[:, s, :], val[:, s, :], tmp[:, s, :], ALU.add).then_inc(feature, 1)

            def rotary_sum(s):
                pool.wait_ge(swap_drained, s + 1)
                pool.tensor_tensor(val[:, s, :], val[:, s, :], tmp[:, s, :], ALU.add).then_inc(operand, 1)

            def lo(s):
                pool.wait_ge(mid_done, s + 1)
                pool.tensor_tensor(of(part[2], s), val[:, s, :], of(part[1], s), ALU.subtract).then_inc(lo_done, 1)

            for s in range(NU + 4):
                if rotary and s < NU:
                    feature_sum(s)
                if rotary and 2 <= s < NU + 2:
                    rotary_sum(s - 2)
                if s >= 4:
                    lo(s - 4)


def attention(nc, k, tag, scale, causal):
    (ones_set, hm_ready, ring_ready, ring_free, st_ready, exp_done, pv_done,
     v_staged, v_ready0, masked, evacuated, hi_done, rec_done, tri_loaded) = sems(
        nc, *(f"{tag}_{n}" for n in (
            "ones_set", "max_parts_ready", "ring_filled",
            "ring_drained", "scores_ready", "exp_done", "values_added", "v_staged", "v_cleared",
            "diagonal_masked", "sums_evacuated", "max_hi_done", "reciprocal_ready",
            "triangle_loaded")))
    z_stored, ones_made = sems(nc, f"{tag}_z_stored", f"{tag}_ones_made")
    m_rows = sems(nc, *(f"{tag}_max_rows_loaded{half}" for half in range(2)))
    loaded = sems(nc, *(f"{tag}_operands_loaded{r}" for r in range(RING)))
    STEPS = 2 * SEQ_TILES
    MAXES = GROUP * SEQ_TILES
    ENTRIES = MAXES + 2 + 2
    FIRST = MAXES + 2
    PB = 4
    ctx = ExitStack()
    with ctx:
        def sb(name, shape, dt=F32):
            return ctx.enter_context(nc.sbuf_tensor(f"{tag}_{name}", shape, dt))

        q_op = [sb(f"q_op{r}", [ROWS, GROUP, SEQ], BF16) for r in range(RING)]
        k_op = [sb(f"k_op{r}", [ROWS, GROUP, SEQ], BF16) for r in range(RING)]
        probs = sb("probs", [P, PB, GROUP, CHUNK])
        stage_v = [sb(f"v1_{r}", [P, SEQ_TILES, GROUP, 32]) for r in range(RING)]
        neg = sb("neg_max", [P, SEQ_TILES, GROUP])
        neg_parts = sb("neg_parts", [P, SEQ_TILES, 2, GROUP], BF16)
        one_rows = sb("one_rows", [2, GROUP, SEQ], BF16)
        neg_rows = sb("neg_rows", [2 * GROUP, SEQ], BF16)
        sums = sb("sums", [P, 2, CHUNK])
        rec = sb("rec", [P, 4, GROUP])
        if causal:
            stage_vo = [sb(f"v0_{r}", [P, SEQ_TILES, GROUP, 32]) for r in range(RING)]
            only_ones = sb("only_ones", [P, 32])
            diag = sb("diag", [P, 2, GROUP, P])
            triangle = sb("triangle", [P, P])
        st_bank = [k.psum[:, i, :] for i in range(3)]
        ring = [k.psum[:, 3 + 2 * i:5 + 2 * i, :].rearrange("p a n -> p (a n)") for i in range(2)]
        out_bank = k.psum[:, 7, :]

        def loop(engine, body):
            body(0, None, 0, 0)
            with engine.Fori(0, (UNITS - 2) // RING) as i:
                for u in range(RING):
                    body(i * RING + (u + 1), i * RING + u, i + (u + 1) // RING, (u + 1) % RING)
            body(UNITS - 1, UNITS - 2, (UNITS - 1) // RING, (UNITS - 1) % RING)

        def is_last(it):
            return isinstance(it, int) and it == UNITS - 1

        def entries(it):
            first, last = isinstance(it, int) and it == 0, is_last(it)
            out = []
            for s in range(STEPS):
                if not last:
                    out += [(s, "max", 2 * s), (s, "max", 2 * s + 1)]
                if s == 1 and not first:
                    out.append((s, "turn", 1))
                if s == 2 and not first:
                    out.append((s, "rows", 1))
                if s == SEQ_TILES + 1:
                    out.append((s, "turn", 0))
                if s == SEQ_TILES + 2 and not last:
                    out.append((s, "rows", 0))
            return out

        def base_of(it):
            return FIRST if isinstance(it, int) and it == 0 else it * ENTRIES + (FIRST - 2)

        def max_at(arg):
            half, rest = arg // (MAXES // 2), arg % (MAXES // 2)
            return rest // 4, 4 * half + rest % 4

        def done(it, kind, arg):
            return base_of(it) + [e[1:] for e in entries(it)].index((kind, arg)) + 1

        block = ctx.enter_context(nc.Block())

        @block.sync
        def _(sp):
            def load(it):
                r = it % RING
                for a in range(3):
                    rows9 = slice(3 * HEAD_DIM * a, 3 * HEAD_DIM * (a + 1))
                    part_q = k.parts[0, a, it // GROUPS, it % GROUPS].rearrange("d h t -> d (h t)")
                    sp.dma_start(q_op[r][rows9].rearrange("p h t -> p (h t)"),
                                 part_q.unsqueeze(0).broadcast_to([3, HEAD_DIM, GROUP * SEQ])).then_inc(loaded[r], 16)
                    parts_k = k.parts[1, :, it // GROUPS, it % GROUPS].rearrange("c d h t -> c d (h t)")
                    sp.dma_start(k_op[r][rows9].rearrange("p h t -> p (h t)"), parts_k).then_inc(loaded[r], 16)

            def rows(it, half):
                sp.wait_ge(ring_free, FIRST if it == 0 else done(it, "rows", 1) if half else done(it - 1, "rows", 0))
                sp.dma_start(q_op[it % RING][SPLIT_ROWS:ROWS, :, half * CHUNK:(half + 1) * CHUNK],
                             neg_rows[:, half * CHUNK:(half + 1) * CHUNK]).then_inc(m_rows[half], 16)

            def store_z(it):
                b, g = it // GROUPS, it % GROUPS
                sp.wait_ge(ring_free, done(it, "turn", 0) + 1 if is_last(it) else done(it + 1, "turn", 1))
                for j in range(GROUP):
                    sp.dma_start(k.z[b, g * GROUP + j].rearrange("(t p) d -> p t d", p=P),
                                 k.att[:, :, it, j * HEAD_DIM:(j + 1) * HEAD_DIM]).then_inc(z_stored, 16)

            for r in range(RING):
                load(r)
            sp.wait_ge(ones_made, 1)
            for r in range(RING):
                sp.dma_start(k_op[r][SPLIT_ROWS:ROWS], one_rows[:, :, :]).then_inc(ones_set, 16)
            rows(0, 0)
            rows(0, 1)
            for it in range(UNITS):
                if it + 1 < UNITS:
                    rows(it + 1, 0)
                if it + RING < UNITS:
                    sp.wait_ge(exp_done, GROUP * STEPS * (it + 1))
                    load(it + RING)
                if it + 1 < UNITS:
                    rows(it + 1, 1)
                if causal:
                    store_z(it)
            if causal:
                sp.wait_ge(z_stored, 16 * GROUP * UNITS)

        @block.tensor
        def _(pe):
            def entry(n, base, kind, arg, it, r=None):
                buf = ring[n % 2]
                if not (isinstance(base, int) and base + n < 2):
                    pe.wait_ge(ring_free, base + n - 1)
                if kind == "max":
                    j, t = max_at(arg)
                    for half in range(2):
                        last = pe.matmul(buf[:, half * CHUNK:(half + 1) * CHUNK],
                                         q_op[r][0:SPLIT_ROWS, j, t * P:(t + 1) * P],
                                         k_op[r][0:SPLIT_ROWS, j, half * CHUNK:(half + 1) * CHUNK],
                                         start=True, stop=True)
                elif kind == "rows":
                    pe.wait_ge(hm_ready, 2 * it + arg + 1)
                    for t in range(4):
                        last = pe.matmul(buf[0:2 * GROUP, t * P:(t + 1) * P],
                                         neg_parts[:, arg * 4 + t, :, :].rearrange("p c h -> p (c h)"),
                                         k.ident_bf[:, :], start=True, stop=True)
                else:
                    pe.wait_ge(evacuated, 2 * it + arg + 1)
                    for t in range(4):
                        last = pe.transpose(buf[:, t * P:(t + 1) * P], sums[:, arg, t * P:(t + 1) * P], k.ident[:, :])
                last.then_inc(ring_ready, 1)

            def score(it, r, s, j):
                half, t = s // SEQ_TILES, s % SEQ_TILES
                e = GROUP * s + j
                if not (isinstance(it, int) and GROUP * STEPS * it + e < 3):
                    pe.wait_ge(exp_done, it * (GROUP * STEPS) + e - 2)
                mm = pe.matmul(st_bank[(r + e) % 3], k_op[r][:, j, t * P:(t + 1) * P],
                               q_op[r][:, j, half * CHUNK:(half + 1) * CHUNK], start=True, stop=True)
                mm.then_inc(st_ready, 1)

            def values(it, r, s):
                half, t = s // SEQ_TILES, s % SEQ_TILES
                pe.wait_ge(exp_done, it * (GROUP * STEPS) + GROUP * (s + 1))
                if s == 0:
                    pe.wait_ge(v_staged, it + 1)
                if t == 0 and not (isinstance(it, int) and 2 * it + half == 0):
                    pe.wait_ge(evacuated, 2 * it + half)
                first, final = t == 0, t == SEQ_TILES - 1
                full = CHUNK if not causal else min(max(t - 4 * half, 0) * P, CHUNK)
                for j in range(GROUP):
                    out = out_bank[32 * j:32 * j + 32, :]
                    pr = probs[:, s % PB, j, :]
                    if full:
                        last = pe.matmul(out[:, 0:full], stage_v[r][:, t, j, :], pr[:, 0:full],
                                         start=first, stop=final and full == CHUNK, skip_group_check=causal)
                    if full < CHUNK:
                        last = pe.matmul(out[:, full:CHUNK], only_ones[:, :], pr[:, full:CHUNK],
                                         start=first, stop=final, skip_group_check=causal)
                if causal and 0 <= t - 4 * half < 4:
                    pe.wait_ge(masked, it * SEQ_TILES + t + 1)
                    at = (t - 4 * half) * P
                    for j in range(GROUP):
                        last = pe.matmul(out_bank[32 * j:32 * j + 32, at:at + P], stage_vo[r][:, t, j, :],
                                         diag[:, t % 2, j, :], start=False, stop=final, skip_group_check=True)
                last.then_inc(pv_done, 1)

            def body(it, before, uses, r):
                base = base_of(it)
                todo = list(enumerate(entries(it)))
                if isinstance(it, int) and it == 0:
                    pe.wait_ge(ones_set, 16 * RING)
                for s in range(STEPS):
                    if s % SEQ_TILES == 0:
                        pe.wait_ge(m_rows[s // SEQ_TILES], 16 * (it + 1))
                    for j in range(GROUP):
                        score(it, r, s, j)
                        if j % 2 == 1 and not is_last(it):
                            n, (_, kind, arg) = todo.pop(0)
                            if n == 0:
                                pe.wait_ge(loaded[(r + 1) % RING], 96 * (uses + (r + 1) // RING + 1))
                            entry(n, base, kind, arg, None, (r + 1) % RING)
                    if s >= 1:
                        values(it, r, s - 1)
                    elif before is not None:
                        values(before, (r - 1) % RING, STEPS - 1)
                    while todo and todo[0][1][0] == s:
                        n, (_, kind, arg) = todo.pop(0)
                        late = (kind, arg) == ("turn", 1)
                        ahead = (kind, arg) == ("rows", 0)
                        entry(n, base, kind, arg, before if late else it + 1 if ahead else it)
                if is_last(it):
                    values(it, r, STEPS - 1)
                    entry(3, base, "turn", 1, it)

            def first():
                pe.wait_ge(loaded[0], 96)
                for n in range(MAXES):
                    entry(n, 0, "max", n, 0, 0)
                entry(MAXES, 0, "rows", 0, 0)
                entry(MAXES + 1, 0, "rows", 1, 0)

            first()
            loop(pe, body)

        @block.scalar
        def _(act):
            def take_sums(it, half):
                act.wait_ge(pv_done, it * STEPS + (half + 1) * SEQ_TILES)
                act.activation(sums[:, half, :], out_bank, ACT.Copy).then_inc(evacuated, 1)

            def body(it, before, uses, r):
                for s in range(STEPS):
                    for j in range(GROUP):
                        e = GROUP * s + j
                        act.wait_ge(st_ready, it * (GROUP * STEPS) + e + 1)
                        if j == 0 and not (isinstance(it, int) and it * STEPS + s < PB):
                            act.wait_ge(pv_done, it * STEPS + s - PB + 1)
                        ins = act.activation(probs[:, s % PB, j, :], st_bank[(r + e) % 3], ACT.Exp, scale=scale)
                        ins.then_inc(exp_done, 1)
                        if j == 0 and s == 1 and before is not None:
                            take_sums(before, 1)
                        if j == 0 and s == SEQ_TILES + 1:
                            take_sums(it, 0)
                if is_last(it):
                    take_sums(it, 1)

            loop(act, body)

        @block.vector
        def _(dve):
            def entry(n, base, kind, arg, it):
                buf = ring[n % 2]
                dve.wait_ge(ring_ready, base + n + 1)
                if kind == "max":
                    j, t = max_at(arg)
                    ins = dve.tensor_reduce(neg[:, t, j:j + 1], buf, AX.X, ALU.max, negate=True)
                    ins.then_inc(ring_free, 1)
                    if (arg + 1) % (MAXES // 2) == 0:
                        half = arg // (MAXES // 2)
                        at = slice(4 * half, 4 * half + 4)
                        dve.wait_ge(ring_free, base + n + 1)
                        dve.tensor_copy(neg_parts[:, at, 0, :], neg[:, at, :]).then_inc(hi_done, 1)
                        dve.wait_ge(hi_done, 2 * it + half + 1)
                        dve.tensor_tensor(neg_parts[:, at, 1, :], neg[:, at, :], neg_parts[:, at, 0, :], ALU.subtract)\
                           .then_inc(hm_ready, 1)
                elif kind == "rows":
                    if not (isinstance(it, int) and it == 0):
                        dve.wait_ge(m_rows[arg], 16 * it)
                    dve.wait_ge(hm_ready, 2 * it + arg + 1)
                    dve.tensor_copy(neg_rows[:, arg * CHUNK:(arg + 1) * CHUNK], buf[0:2 * GROUP, 0:CHUNK])\
                       .then_inc(ring_free, 1)
                else:
                    tile = buf[:, 0:CHUNK].rearrange("p (t h c) -> p t h c", t=4, c=32)
                    if is_last(it):
                        dve.wait_ge(ring_free, base + n)
                    dve.reciprocal(rec[:, :, :], tile[:, :, :, HEAD_DIM]).then_inc(rec_done, 1)
                    dve.wait_ge(rec_done, 2 * it + arg + 1)
                    out = k.att[:, 4 * arg:4 * arg + 4, it, :].rearrange("p t (h c) -> p t h c", c=HEAD_DIM)
                    num = tile[:, :, :, 0:HEAD_DIM]
                    by = rec[:, :, :].unsqueeze(3).broadcast_to([P, 4, GROUP, HEAD_DIM])
                    dve.tensor_tensor(out, num, by, ALU.mult).then_inc(ring_free, 1)

            def body(it, before, uses, r):
                for n, (s, kind, arg) in enumerate(entries(it)):
                    of_unit = it + 1 if kind == "max" or (kind, arg) == ("rows", 0) else \
                        before if (kind, arg) == ("turn", 1) else it
                    entry(n, base_of(it), kind, arg, of_unit)
                if is_last(it):
                    entry(3, base_of(it), "turn", 1, it)

            def first():
                for n in range(MAXES):
                    entry(n, 0, "max", n, 0)
                entry(MAXES, 0, "rows", 0, 0)
                entry(MAXES + 1, 0, "rows", 1, 0)

            first()
            loop(dve, body)

        @block.gpsimd
        def _(pool):
            if causal:
                pool.dma_start(triangle[:, :], k.A["triangle"]).then_inc(tri_loaded, 16)
                pool.wait_ge(tri_loaded, 16)
            pool.memset(one_rows[:, :, :], 1.0).then_inc(ones_made, 1)
            stages = stage_v + (stage_vo if causal else [])
            for t in stages:
                pool.memset(t[:, :, :, :], 0.0).then_inc(v_ready0, 1)
            n = len(stages)
            if causal:
                pool.memset(only_ones[:, :], 0.0).then_inc(v_ready0, 1)
                n += 1
            pool.wait_ge(v_ready0, n)
            for t in stage_v:
                pool.memset(t[:, :, :, HEAD_DIM:HEAD_DIM + 1], 1.0).then_inc(v_ready0, 1)
            n += RING
            if causal:
                pool.memset(only_ones[:, HEAD_DIM:HEAD_DIM + 1], 1.0).then_inc(v_ready0, 1)
                n += 1
            pool.wait_ge(v_ready0, n)

            def stage(it, r):
                src = k.v_tok[:, :, it, :].rearrange("p t (h c) -> p t h c", c=HEAD_DIM)
                if causal:
                    pool.tensor_copy(stage_vo[r][:, :, :, 0:HEAD_DIM], src)
                pool.tensor_copy(stage_v[r][:, :, :, 0:HEAD_DIM], src).then_inc(v_staged, 1)

            def body(it, before, uses, r):
                if not is_last(it):
                    if not (isinstance(it, int) and it == 0):
                        pool.wait_ge(pv_done, it * STEPS)
                    stage(it + 1, (r + 1) % RING)
                if causal:
                    for t in range(SEQ_TILES):
                        s = t if t < 4 else SEQ_TILES + t
                        pool.wait_ge(exp_done, it * (GROUP * STEPS) + GROUP * (s + 1))
                        if not (isinstance(it, int) and it * SEQ_TILES + t < 2):
                            back = t - 2 if t >= 2 else t + 6
                            sb_ = back if back < 4 else SEQ_TILES + back
                            pool.wait_ge(pv_done, (it if t >= 2 else it - 1) * STEPS + sb_ + 1)
                        at = (t % 4) * P
                        pool.tensor_tensor(diag[:, t % 2, :, :], probs[:, s % PB, :, at:at + P],
                                           triangle[:, :].unsqueeze(1).broadcast_to([P, GROUP, P]), ALU.mult)\
                            .then_inc(masked, 1)

            stage(0, 0)
            loop(pool, body)


def residual_attention(nc, k, tag, A):
    w_in, turned, drained, taps = sems(nc, *(f"{tag}_{n}" for n in ("taps_loaded", "att_turned", "turned_drained", "taps_done")))
    gate = lambda b: k.mod[:, 0, 2, b:b + 1]
    ctx = ExitStack()
    with ctx:
        tap = ctx.enter_context(nc.sbuf_tensor("lepe_taps", [P, 4], F32))
        acc = ctx.enter_context(nc.sbuf_tensor("lepe", [P, BATCH, SEQ], F32))
        v = k.v_ch[:, :].rearrange("p (b n) -> p b n", b=BATCH)
        x = k.x[:, :].rearrange("p (b n) -> p b n", b=BATCH)
        block = ctx.enter_context(nc.Block())

        @block.sync
        def _(sp):
            sp.dma_start(tap[:, :], A["lepe"]).then_inc(w_in, 16)

        @block.tensor
        def _(pe):
            for c in range(CHUNKS):
                b, t0 = c // 2, c % 2 * 4
                for t in range(4):
                    last = pe.transpose(k.psum[:, c, t * P:(t + 1) * P], k.att[:, t0 + t, b * GROUPS:(b + 1) * GROUPS, :].rearrange("p g c -> p (g c)"), k.ident[:, :])
                last.then_inc(turned, 1)

        @block.vector
        def _(dve):
            dve.wait_ge(w_in, 16)
            dve.tensor_scalar(acc[:, :, :], v, tap[:, 1:2], tap[:, 3:4], ALU.mult, ALU.add).then_inc(taps, 1)
            dve.wait_ge(taps, 1)
            dve.scalar_tensor_tensor(acc[:, :, 1:SEQ], v[:, :, 0:SEQ - 1], tap[:, 0:1], acc[:, :, 1:SEQ],
                                     ALU.mult, ALU.add).then_inc(taps, 1)
            dve.wait_ge(taps, 2)
            dve.scalar_tensor_tensor(acc[:, :, 0:SEQ - 1], v[:, :, 1:SEQ], tap[:, 2:3], acc[:, :, 0:SEQ - 1],
                                     ALU.mult, ALU.add).then_inc(taps, 1)
            dve.wait_ge(taps, 3)
            for c in range(CHUNKS):
                b, at = c // 2, slice(c % 2 * CHUNK, (c % 2 + 1) * CHUNK)
                dve.wait_ge(turned, c + 1)
                dve.tensor_tensor(acc[:, b, at], acc[:, b, at], k.psum[:, c, :], ALU.add).then_inc(drained, 1)
                dve.wait_ge(drained, c + 1)
                dve.scalar_tensor_tensor(x[:, b, at], acc[:, b, at], gate(b), x[:, b, at], ALU.mult, ALU.add)


def windowed_layers(nc, k, A, part):
    with ExitStack() as ctx:
        def sb(name, shape, dt=F32):
            return ctx.enter_context(nc.sbuf_tensor(f"win_{name}", shape, dt))

        s = Core()
        s.y = sb("y", [P, TOK])
        s.h = sb("h", [P, TOK])
        s.h_high, s.h_low = sb("h_high", [P, TOK], F32R), sb("h_low", [P, TOK], F32R)
        s.wj = sb("w_pair", [P, 5, DIM])
        s.wj_high, s.wj_low = sb("w_pair_high", [P, 4, DIM], F32R), sb("w_pair_low", [P, 4, DIM], F32R)
        s.wo = sb("wo", [P, PAIRS, DIM])
        s.w1 = sb("w1", [P, 2 * HID])
        s.w2 = sb("w2", [P, 3, DIM])
        s.cols = sb("cols", [P, COLS])
        s.table = sb("table", [P, 4, SEQ])
        s.head_ones = sb("head_ones", [P, P])
        s.band = sb("band", [P, 2, KEYS])
        s.q = sb("q", [P, TOK])
        s.k_half = [sb(f"k_half{e}", [P, WINDOW + TOK]) for e in range(2)]
        s.v = sb("v", [P, TILES, DIM])
        s.norm = sb("norm", [P, TILES, 2, 2])
        s.q_scale = sb("q_scale", [P, 2, TILES, 2])
        s.o = sb("o", [P, PAIRS, TOK])
        once = [(s.head_ones[:, :], A["head_ones"]), (s.wj[:, :, :], A["win_wj"][0]), (s.band[:, :, :], A["band"]),
                (s.table[:, :, :], A["xpos"])]
        loaded, w_high, s.weights_loaded = sems(nc, "win_constants_loaded", "first_pair_weights_high",
                                                "layer_weights_loaded")
        with nc.Block() as block:
            @block.sync
            def _(sp):
                for dst, src in once:
                    sp.dma_start(dst, src).then_inc(loaded, 16)

            @block.gpsimd
            def _(pool):
                for e in range(2):
                    pool.memset(s.k_half[e][:, :], 0.0)

        layer_norm(nc, k, "ln1", k.x, s.y, part(0, 4), part(0, 3))
        with nc.Block() as block:
            @block.vector
            def _(dve):
                dve.wait_ge(loaded, 16 * len(once))
                split_pair_weights(dve, s, w_high, 0)

        with nc.Fori(0, DEPTH) as l:
            layer_start(nc, s, A, l)
            with nc.Fori(0, PAIRS) as j:
                project_pair(nc, k, s)
                attend_pair(nc, k, s, A, l, j)
            output_projection(nc, k, s, l)
            with rearmed(nc, *(f"ln5_{n}" for n in LN_SEMS)) as own:
                layer_norm(nc, k, "ln5", s.h, s.h, lambda b: s.cols[:, LN_G:LN_G + 1],
                           lambda b: s.cols[:, LN_B:LN_B + 1], names=lambda nc, *names: own)
            geglu(nc, k, s)

        with nc.Block() as block:
            @block.vector
            def _(dve):
                for b in range(BATCH):
                    at = slice(b * SEQ, (b + 1) * SEQ)
                    dve.scalar_tensor_tensor(k.x[:, at], s.y[:, at], part(0, 5)(b), k.x[:, at], ALU.mult, ALU.add)


SCALES, LN_G, LN_B, B2, B1_A, B1_G, COLS = 0, 4, 5, 6, 7, 10, 13


def shift_tokens(dve, s, done=None):
    half = DIM // 2
    y = s.y[:, :].rearrange("p (b n) -> p b n", b=BATCH)
    h = s.h[:, :].rearrange("p (b n) -> p b n", b=BATCH)
    dve.tensor_copy(h[0:half], y[0:half])
    dve.tensor_copy(h[half:P, :, 1:SEQ], y[half:P, :, 0:SEQ - 1])
    last = dve.memset(h[half:P, :, 0:1], 0.0)
    if done is not None:
        last.then_inc(done, 1)


def split_pair_weights(dve, s, high_done, before):
    high_part(dve, s.wj_high[:, :, :], s.wj[:, 0:4, :]).then_inc(high_done, 1)
    dve.wait_ge(high_done, before + 1)
    low_part(dve, s.wj_low[:, :, :], s.wj[:, 0:4, :], s.wj_high[:, :, :])


LAYER_WEIGHTS = 3


def layer_start(nc, s, A, l):
    with rearmed(nc, "cols_loaded", "shifted", "h_high") as (cols_loaded, shifted, high), nc.Block() as block:
        @block.sync
        def _(sp):
            sp.dma_start(s.cols[:, :], A["win_cols"][l]).then_inc(cols_loaded, 16)
            for dst, src in ((s.wo[:, :, :], A["win_wo"][l]), (s.w1[:, :], A["win_w1"][l]),
                             (s.w2[:, :, :], A["win_w2"][l])):
                sp.dma_start(dst, src).then_inc(s.weights_loaded, 16)
            sp.wait_ge(cols_loaded, 16)

        @block.vector
        def _(dve):
            shift_tokens(dve, s, shifted)
            dve.wait_ge(shifted, 1)
            for c in range(CHUNKS):
                at = slice(c * CHUNK, (c + 1) * CHUNK)
                high_part(dve, s.h_high[:, at], s.h[:, at]).then_inc(high, 1)
            for c in range(CHUNKS):
                at = slice(c * CHUNK, (c + 1) * CHUNK)
                dve.wait_ge(high, c + 1)
                low_part(dve, s.h_low[:, at], s.h[:, at], s.h_high[:, at])


def project_pair(nc, k, s):
    with (rearmed(nc, "pair_projected", "pair_squared", "pair_sums", "pair_rooted", "pair_floored", "pair_inverse",
                  "pair_spread", "pair_q_parts", "pair_k_parts", "pair_q_sum", "pair_k_sum", "pair_k_done",
                  "pair_v", "pair_v_done") as
          (projected, squared, sums, rooted, floored, inverse, spread, q_parts, k_parts, q_sum, k_sum, k_done,
           v_ready, v_done),
          nc.sbuf_tensor("pair_sq", [P, 2, 2, CHUNK], F32) as sq,
          nc.sbuf_tensor("pair_tmp", [P, 2, 4, CHUNK], F32) as tmp,
          nc.sbuf_tensor("pair_first_root", [P, 1], F32) as first_root,
          nc.Block() as block):
        cols = [slice(c * CHUNK, (c + 1) * CHUNK) for c in range(CHUNKS)]
        tiles = [slice(4 * c, 4 * c + 4) for c in range(CHUNKS)]
        ORDER = (1, 0, 3, 2)
        sums_bank = k.psum[:, 5, 0:4 * TILES].rearrange("p (t w e) -> p t w e", w=2, e=2)
        spread_bank = k.psum[:, 4, :]

        @block.tensor
        def _(pe):
            def project(c):
                for n, i in enumerate(ORDER):
                    if c:
                        pe.wait_ge(q_parts if i < 2 else k_parts, 2 * (c - 1) + n % 2 + 1)
                    matmul_split(pe, k.psum[:, i, :], s.wj_high[:, i, :], s.wj_low[:, i, :], s.h_high[:, cols[c]],
                                 s.h_low[:, cols[c]]).then_inc(projected, 1)

            def norms(c):
                pe.wait_ge(squared, 2 * c + 2)
                if c:
                    pe.wait_ge(rooted, c)
                for t in range(4):
                    for w in range(2):
                        last = pe.matmul(sums_bank[:, 4 * c + t, w, :], sq[:, c % 2, w, t * P:(t + 1) * P],
                                         s.head_ones[:, 0:P:W_DIM], start=True, stop=True)
                last.then_inc(sums, 1)

            def values(c):
                if c >= 2:
                    pe.wait_ge(v_done, c - 1)
                for t in range(4):
                    i = 4 * c + t
                    last = pe.matmul(k.psum[:, 6 + c % 2, t * P:(t + 1) * P], s.h[:, i * P:(i + 1) * P],
                                     s.wj[:, 4, :], start=True, stop=True)
                last.then_inc(v_ready, 1)

            def spread_inverse(c):
                pe.wait_ge(inverse, c + 1)
                if c:
                    pe.wait_ge(k_done, 2 * c)
                for t in range(4):
                    for e in range(2):
                        last = pe.matmul(spread_bank[e * W_DIM:(e + 1) * W_DIM, t * P:(t + 1) * P],
                                         s.norm[:, 4 * c + t, 1, e:e + 1].broadcast_to([P, W_DIM]),
                                         k.ident[:, :], start=True, stop=True)
                last.then_inc(spread, 1)

            project(0)
            values(0)
            for c in range(CHUNKS):
                if c + 1 < CHUNKS:
                    project(c + 1)
                norms(c)
                if c + 1 < CHUNKS:
                    values(c + 1)
                spread_inverse(c)

        @block.scalar
        def _(act):
            def squares(c):
                if c >= 2:
                    act.wait_ge(sums, c - 1)
                for i in range(2):
                    act.wait_ge(projected, 4 * c + 2 * i + 2)
                    act.activation(sq[:, c % 2, i, :], k.psum[:, 2 * i, :], ACT.Square).then_inc(squared, 1)

            def root(c):
                act.wait_ge(sums, c + 1)
                act.activation(s.norm[:, tiles[c], :, :], sums_bank[:, tiles[c], :, :], ACT.Sqrt).then_inc(rooted, 1)

            def take_values(c):
                act.wait_ge(v_ready, c + 1)
                act.activation(s.v[:, tiles[c], :],
                               k.psum[:, 6 + c % 2, :].rearrange("p (t n) -> p t n", t=4), ACT.Copy)\
                   .then_inc(v_done, 1)

            act.activation(first_root[:, :], k.eps[:, :], ACT.Sqrt)
            squares(0)
            for c in range(CHUNKS):
                take_values(c)
                if c + 1 < CHUNKS:
                    squares(c + 1)
                root(c)

        @block.vector
        def _(dve):
            def parts(c, which):
                at = slice(c * CHUNK % SEQ, c * CHUNK % SEQ + CHUNK)
                if c >= 2:
                    if which == 0:
                        dve.wait_ge(q_sum, c - 1)
                    else:
                        dve.wait_ge(k_done, 2 * (c - 1))
                for n, i in list(enumerate(ORDER))[2 * which:2 * which + 2]:
                    dve.wait_ge(projected, 4 * c + n + 1)
                    if i % 2 == 0:
                        dve.wait_ge(squared, 2 * c + i // 2 + 1)
                    dve.scalar_tensor_tensor(tmp[:, c % 2, i, :], k.psum[:, i, :], s.cols[:, SCALES + i:SCALES + i + 1],
                                             s.table[:, i, at], ALU.mult, ALU.mult)\
                       .then_inc(q_parts if i < 2 else k_parts, 1)

            def invert(c):
                dve.wait_ge(rooted, c + 1)
                at = s.norm[:, tiles[c], :, :]
                dve.tensor_scalar(at, at, 1e-12, None, ALU.max).then_inc(floored, 1)
                dve.wait_ge(floored, c + 1)
                dve.reciprocal(at, at).then_inc(inverse, 1)

            def divide_k(c):
                dve.wait_ge(spread, c + 1)
                dve.wait_ge(k_sum, c + 1)
                for e in range(2):
                    rows = slice(e * W_DIM, (e + 1) * W_DIM)
                    dve.tensor_tensor(s.k_half[e][rows, WINDOW + c * CHUNK:WINDOW + (c + 1) * CHUNK],
                                      tmp[rows, c % 2, 2, :], spread_bank[rows, :], ALU.mult).then_inc(k_done, 1)

            parts(0, 0)
            parts(0, 1)
            for c in range(CHUNKS):
                if c + 1 < CHUNKS:
                    parts(c + 1, 0)
                invert(c)
                if c + 1 < CHUNKS:
                    parts(c + 1, 1)
                divide_k(c)
            dve.wait_ge(inverse, CHUNKS)
            for i, v in enumerate((QK_SCALE, -QK_SCALE)):
                dve.tensor_scalar(s.q_scale[:, i, :, :], s.norm[:, :, 0, :], v, None, ALU.mult)

        @block.gpsimd
        def _(pool):
            for c in range(CHUNKS):
                pool.wait_ge(q_parts, 2 * c + 2)
                pool.tensor_tensor(s.q[:, cols[c]], tmp[:, c % 2, 0, :], tmp[:, c % 2, 1, :], ALU.add)\
                    .then_inc(q_sum, 1)
                pool.wait_ge(k_parts, 2 * c + 2)
                pool.tensor_tensor(tmp[:, c % 2, 2, :], tmp[:, c % 2, 2, :], tmp[:, c % 2, 3, :], ALU.add)\
                    .then_inc(k_sum, 1)


def attend_pair(nc, k, s, A, l, j):
    NB = 4
    NS = 3
    TURN, VALUES = 3, 5
    with (rearmed(nc, "win_weights", "win_scores", "win_masked", "win_bias", "win_exp", "win_inverse", "win_scaled",
                  "win_turned", "win_turned_copied", "win_values", "win_out", "win_cleared", "win_weights_high") as
          (w_next, scores, masked, bias_done, exp_done, inverse, scaled, turned, copied, values_done, out_done, cleared,
           w_high),
          nc.sbuf_tensor("win_sm", [P, NB, 2, KEYS], F32) as sm,
          nc.sbuf_tensor("win_p", [P, NB, 2, 2 * P], F32) as pr,
          nc.sbuf_tensor("win_pt", [P, NB, 2, 2, P], F32) as pt,
          nc.sbuf_tensor("win_max", [P, TILES, 2], F32) as mx,
          nc.sbuf_tensor("win_nb", [P, TILES, 2], F32) as nb,
          nc.sbuf_tensor("win_rs", [P, TILES, 2], F32) as rs,
          nc.sbuf_tensor("win_ri", [P, TILES, 2], F32) as ri,
          nc.Block() as block):

        def s_bank(i):
            return k.psum[:, i % NS, 0:2 * KEYS].rearrange("p (e n) -> p e n", e=2)

        def t_bank(i):
            return k.psum[:, NS + i % NS, :].rearrange("p (e a n) -> p e a n", e=2, a=2)

        def o_bank(i):
            return k.psum[:, 2 * NS + i // 4 % 2, i % 4 * P:(i % 4 + 1) * P]

        def near(i):
            return (1,) if i % SEQ_TILES == 0 else (0, 1)

        @block.sync
        def _(sp):
            sp.dma_start(s.wj[:, :, :], A["win_wj"][l * PAIRS + (j + 1)]).then_inc(w_next, 16)
            sp.wait_ge(w_next, 16)

        @block.tensor
        def _(pe):
            def score(i):
                if i >= NS:
                    pe.wait_ge(masked, 2 * (i - NS + 1))
                for e in range(2):
                    last = pe.matmul(s_bank(i)[:, e, :], s.q[:, i * P:(i + 1) * P],
                                     s.k_half[e][:, i * P:i * P + KEYS], start=True, stop=True)
                last.then_inc(scores, 1)

            def turn(i):
                pe.wait_ge(scaled, i + 1)
                if i >= NS:
                    pe.wait_ge(copied, i - NS + 1)
                for e in range(2):
                    for a in near(i):
                        last = pe.transpose(t_bank(i)[:, e, a, :], pr[:, i % NB, e, a * P:(a + 1) * P], k_ident)
                last.then_inc(turned, 1)

            def values(i):
                pe.wait_ge(copied, i + 1)
                if i % 4 == 0 and i >= 8:
                    pe.wait_ge(out_done, i // 4 - 1)
                for e in range(2):
                    for a in near(i):
                        last = pe.matmul(o_bank(i)[e * W_DIM:(e + 1) * W_DIM, :],
                                         s.v[:, i - 1 + a, e * W_DIM:(e + 1) * W_DIM], pt[:, i % NB, e, a, :],
                                         start=a == near(i)[0], stop=a == 1)
                last.then_inc(values_done, 1)

            k_ident = k.ident[:, :]
            for i in range(TILES + VALUES):
                if i < TILES:
                    score(i)
                if TURN <= i < TILES + TURN:
                    turn(i - TURN)
                if i >= VALUES:
                    values(i - VALUES)

        @block.scalar
        def _(act):
            def copy_turned(i):
                act.wait_ge(turned, i + 1)
                if i >= NB:
                    act.wait_ge(values_done, i - NB + 1)
                a = near(i)[0]
                act.activation(pt[:, i % NB, :, a:2, :], t_bank(i)[:, :, a:2, :], ACT.Copy).then_inc(copied, 1)

            for i in range(TILES + TURN):
                if i < TILES:
                    act.wait_ge(bias_done, i + 1)
                    if i == 0:
                        act.wait_ge(cleared, 1)
                    if i >= NB:
                        act.wait_ge(turned, i - NB + 1)
                    for e in range(2):
                        act.activation(pr[:, i % NB, e, WINDOW:2 * P], sm[:, i % NB, e, :], ACT.Exp,
                                       bias=nb[:, i, e:e + 1], scale=s.q_scale[:, 0, i, e:e + 1],
                                       accum_out=rs[:, i, e:e + 1]).then_inc(exp_done, 1)
                if i >= TURN:
                    copy_turned(i - TURN)

        @block.vector
        def _(dve):
            def mask(i):
                dve.wait_ge(scores, i + 1)
                if i >= NB:
                    dve.wait_ge(exp_done, 2 * (i - NB + 1))
                for e in range(2):
                    dve.tensor_tensor_reduce(sm[:, i % NB, e, :], s_bank(i)[:, e, :],
                                             s.band[:, int(i % SEQ_TILES == 0), :], 1.0, MASKED * 10,
                                             ALU.add, ALU.max, mx[:, i, e:e + 1]).then_inc(masked, 1)
                dve.wait_ge(masked, 2 * i + 2)
                dve.tensor_tensor(nb[:, i, :], mx[:, i, :], s.q_scale[:, 1, i, :], ALU.mult).then_inc(bias_done, 1)

            def invert(i):
                dve.wait_ge(exp_done, 2 * i + 2)
                dve.reciprocal(ri[:, i, :], rs[:, i, :]).then_inc(inverse, 1)

            def take_out(n):
                dve.wait_ge(values_done, 4 * n + 4)
                dve.tensor_copy(s.o[:, j, n * CHUNK:(n + 1) * CHUNK], k.psum[:, 2 * NS + n % 2, :]).then_inc(out_done, 1)

            for i in range(TILES + 1):
                if i < TILES:
                    mask(i)
                if i:
                    invert(i - 1)
                if i >= 3 + VALUES and (i - 3 - VALUES) % 4 == 0:
                    take_out((i - 3 - VALUES) // 4)
            dve.wait_ge(w_next, 16)
            split_pair_weights(dve, s, w_high, 0)
            take_out(3)

        @block.gpsimd
        def _(pool):
            pool.memset(pr[:, :, :, 0:WINDOW], 0.0).then_inc(cleared, 1)
            for i in range(TILES):
                pool.wait_ge(inverse, i + 1)
                if i == 0:
                    pool.wait_ge(cleared, 1)
                pool.tensor_tensor(pr[:, i % NB, :, WINDOW:2 * P], pr[:, i % NB, :, WINDOW:2 * P],
                                   ri[:, i, :].unsqueeze(2).broadcast_to([P, 2, KEYS]), ALU.mult).then_inc(scaled, 1)


def output_projection(nc, k, s, l):
    with rearmed(nc, "wo_ready", "wo_added") as (ready, added), nc.Block() as block:
        @block.tensor
        def _(pe):
            pe.wait_ge(s.weights_loaded, 16 * LAYER_WEIGHTS * (l + 1))
            for c in range(CHUNKS):
                for j in range(PAIRS):
                    last = pe.matmul(k.psum[:, c, :], s.wo[:, j, :], s.o[:, j, c * CHUNK:(c + 1) * CHUNK],
                                     start=j == 0, stop=j == PAIRS - 1)
                last.then_inc(ready, 1)

        @block.vector
        def _(dve):
            for c in range(CHUNKS):
                at = slice(c * CHUNK, (c + 1) * CHUNK)
                dve.wait_ge(ready, c + 1)
                dve.tensor_tensor(s.y[:, at], s.y[:, at], k.psum[:, c, :], ALU.add).then_inc(added, 1)
            dve.wait_ge(added, CHUNKS)
            shift_tokens(dve, s)


def geglu(nc, k, s):
    NT = len(HID_TILES)
    with (rearmed(nc, "ffn_a", "ffn_g", "ffn_gelu", "ffn_gated", "ffn_out", "ffn_added") as
          (a_ready, g_ready, gelu_done, gated, out_ready, added),
          nc.sbuf_tensor("ffn_gelu_x", [P, 2, NT, CHUNK], F32) as gelu,
          nc.sbuf_tensor("ffn_hidden", [P, 2, NT, CHUNK], F32) as hid,
          nc.Block() as block):
        @block.tensor
        def _(pe):
            def up(c):
                for i, m in enumerate(HID_TILES):
                    if c:
                        pe.wait_ge(gelu_done, NT * (c - 1) + i + 1)
                    pe.matmul(k.psum[0:m, 3 + i, :], s.w1[:, HID + i * P:HID + i * P + m],
                              s.h[:, c * CHUNK:(c + 1) * CHUNK], start=True, stop=True).then_inc(g_ready, 1)
                for i, m in enumerate(HID_TILES):
                    if c:
                        pe.wait_ge(gated, NT * (c - 1) + i + 1)
                    pe.matmul(k.psum[0:m, i, :], s.w1[:, i * P:i * P + m],
                              s.h[:, c * CHUNK:(c + 1) * CHUNK], start=True, stop=True).then_inc(a_ready, 1)

            def down(c):
                pe.wait_ge(gated, NT * (c + 1))
                if c >= 2:
                    pe.wait_ge(added, c - 1)
                for i, m in enumerate(HID_TILES):
                    last = pe.matmul(k.psum[:, 6 + c % 2, :], s.w2[0:m, i, :], hid[0:m, c % 2, i, :],
                                     start=i == 0, stop=i == NT - 1)
                last.then_inc(out_ready, 1)

            up(0)
            for c in range(CHUNKS):
                if c + 1 < CHUNKS:
                    up(c + 1)
                down(c)

        @block.scalar
        def _(act):
            for c in range(CHUNKS):
                for i, m in enumerate(HID_TILES):
                    act.wait_ge(g_ready, NT * c + i + 1)
                    if c >= 2:
                        act.wait_ge(gated, NT * (c - 2) + i + 1)
                    act.activation(gelu[0:m, c % 2, i, :], k.psum[0:m, 3 + i, :], ACT.Gelu,
                                   bias=s.cols[0:m, B1_G + i:B1_G + i + 1]).then_inc(gelu_done, 1)

        @block.vector
        def _(dve):
            for c in range(CHUNKS + 1):
                if c < CHUNKS:
                    for i, m in enumerate(HID_TILES):
                        dve.wait_ge(a_ready, NT * c + i + 1)
                        dve.wait_ge(gelu_done, NT * c + i + 1)
                        if c >= 2:
                            dve.wait_ge(out_ready, c - 1)
                        dve.scalar_tensor_tensor(hid[0:m, c % 2, i, :], k.psum[0:m, i, :],
                                                 s.cols[0:m, B1_A + i:B1_A + i + 1], gelu[0:m, c % 2, i, :],
                                                 ALU.add, ALU.mult).then_inc(gated, 1)
                if c:
                    at = slice((c - 1) * CHUNK, c * CHUNK)
                    dve.wait_ge(out_ready, c)
                    dve.scalar_tensor_tensor(s.y[:, at], k.psum[:, 6 + (c - 1) % 2, :], s.cols[:, B2:B2 + 1],
                                             s.y[:, at], ALU.add, ALU.add).then_inc(added, 1)


def add_heads(nc, k, tag, h):
    loaded, turned, same_done, z_done = sems(nc, *(f"{tag}_{n}" for n in (
        "z_loaded", "z_turned", "z_compared", "z_guarded")))
    with (nc.sbuf_tensor(f"{tag}_z_raw", [P, TILES, DIM], F32) as raw,
          nc.sbuf_tensor(f"{tag}_z_same", [P, TILES, DIM], F32) as same,
          nc.sbuf_tensor(f"{tag}_z_tok", [P, TILES, DIM], F32) as z, nc.Block() as block):
        @block.sync
        def _(sp):
            rows = k.z.rearrange("b h (n q) d -> (b h n) (q d)", q=DIM // HEAD_DIM)
            sp.dma_start(raw[:, :, :], rows.rearrange("(t p) c -> p t c", p=P)).then_inc(loaded, 16)

        @block.tensor
        def _(pe):
            pe.wait_ge(z_done, 1)
            for c in range(CHUNKS):
                for t in range(4):
                    last = pe.transpose(k.psum[:, c, t * P:(t + 1) * P], z[:, 4 * c + t, :], k.ident[:, :])
                last.then_inc(turned, 1)

        @block.vector
        def _(dve):
            dve.memset(z[:, :, :], 0.0).then_inc(same_done, 1)
            dve.wait_ge(loaded, 16)
            dve.tensor_tensor(same[:, :, :], raw[:, :, :], raw[:, :, :], ALU.is_equal).then_inc(same_done, 1)
            dve.wait_ge(same_done, 2)
            dve.copy_predicated(z[:, :, :], same[:, :, :].bitcast(mybir.dt.uint32), raw[:, :, :]).then_inc(z_done, 1)
            for c in range(CHUNKS):
                at = slice(c * CHUNK, (c + 1) * CHUNK)
                dve.wait_ge(turned, c + 1)
                dve.tensor_tensor(h[:, at], h[:, at], k.psum[:, c, :], ALU.add)


def causal_block(nc, k, A, part):
    with ExitStack() as a:
        k.v_ch = a.enter_context(nc.sbuf_tensor("v_ch1", [P, TOK], F32))
        k.v_tok = a.enter_context(nc.sbuf_tensor("v_tok1", [P, SEQ_TILES, UNITS, 32], F32))
        k.att = a.enter_context(nc.sbuf_tensor("att1", [P, SEQ_TILES, UNITS, 32], F32))
        h = a.enter_context(nc.sbuf_tensor("h1", [P, TOK], F32))
        norm = a.enter_context(nc.sbuf_tensor("norm_cols", [P, 2], F32))
        (loaded,) = sems(nc, "norm_cols_loaded")
        with nc.Block() as block:
            @block.sync
            def _(sp):
                sp.dma_start(norm[:, :], A["norm_cols"]).then_inc(loaded, 16)
                sp.wait_ge(loaded, 16)
        layer_norm(nc, k, "ln2", k.x, h, part(1, 1), part(1, 0))
        project_heads(nc, k, "plain", h, A, False)
        attention(nc, k, "att1", 1.0 / float(np.sqrt(SEQ)), True)
        add_heads(nc, k, "z", h)
        layer_norm(nc, k, "ln3", h, h, lambda b: norm[:, 0:1], lambda b: norm[:, 1:2], residual=(k.x, part(1, 2)))


def experts(nc, k, A, part):
    with ExitStack() as ctx:
        def sb(name, shape, dt=F32):
            return ctx.enter_context(nc.sbuf_tensor(f"moe_{name}", shape, dt))

        cur = sb("cur", [P, TOK])
        layer_norm(nc, k, "ln4", k.x, cur, part(1, 4), part(1, 3))
        acc = sb("acc", [P, TILES, DIM])
        w1 = sb("w1", [P, EXPERTS, FF])
        w2 = sb("w2", [P, EXPERTS, FF_TILES, DIM])
        b1 = sb("b1", [P, EXPERTS, FF_TILES])
        b2 = sb("b2", [P, EXPERTS, DIM])
        wg = sb("wg", [P, ROUNDS, EXPERTS])
        bg = sb("bg", [P, ROUNDS, EXPERTS])
        cur_high, cur_low = sb("cur_high", [P, TOK], F32R), sb("cur_low", [P, TOK], F32R)
        w1_high, w1_low = sb("w1_high", [P, EXPERTS, FF], F32R), sb("w1_low", [P, EXPERTS, FF], F32R)
        hidden = sb("hidden", [P, 2, FF_TILES, CHUNK])
        bias = sb("bias_sum", [P, TILES, DIM])
        bias_e = sb("bias_term", [P, 4, DIM])
        wg_r = sb("wg_round", [P, EXPERTS])
        bg_r = sb("bg_round", [P, EXPERTS])
        logit = sb("logit", [P, TILES, EXPERTS])
        top = sb("top", [P, TILES])
        ex = sb("exp", [P, TILES, EXPERTS])
        rank = sb("rank", [P, TILES, EXPERTS])
        wins = sb("wins", [P, TILES, EXPERTS])
        weight = sb("weight", [P, TILES, EXPERTS])
        total = sb("total", [P, TILES])
        cols = [slice(c * CHUNK, (c + 1) * CHUNK) for c in range(CHUNKS)]

        def wide(ap):
            return ap.broadcast_to([P, TILES, EXPERTS])

        loads = [(w1[:, :, :], A["moe_w1"]), (w2[:, :, :, :], A["moe_w2"]), (b1[:, :, :], A["moe_b1"]),
                 (b2[:, :, :], A["moe_b2"]), (wg[:, :, :], A["moe_wg"]), (bg[:, :, :], A["moe_bg"])]
        loaded, turned, first_high = sems(nc, "moe_loaded", "moe_turned", "moe_first_high")
        with nc.Block() as block:
            @block.sync
            def _(sp):
                for dst, src in loads:
                    sp.dma_start(dst, src).then_inc(loaded, 16)
                sp.wait_ge(loaded, 16 * len(loads))

            @block.tensor
            def _(pe):
                for c in range(CHUNKS):
                    for t in range(4):
                        last = pe.transpose(k.psum[:, c, t * P:(t + 1) * P],
                                            cur[:, c * CHUNK + t * P:c * CHUNK + (t + 1) * P], k.ident[:, :])
                    last.then_inc(turned, 1)

            @block.vector
            def _(dve):
                for c in range(CHUNKS):
                    dve.wait_ge(turned, c + 1)
                    dve.tensor_copy(acc[:, 4 * c:4 * c + 4, :], k.psum[:, c, :].rearrange("p (t n) -> p t n", t=4))
                high_part(dve, cur_high[:, :], cur[:, :]).then_inc(first_high, 1)
                dve.wait_ge(loaded, 16 * len(loads))
                high_part(dve, w1_high[:, :, :], w1[:, :, :]).then_inc(first_high, 1)
                dve.wait_ge(first_high, 2)
                low_part(dve, cur_low[:, :], cur[:, :], cur_high[:, :])
                low_part(dve, w1_low[:, :, :], w1[:, :, :], w1_high[:, :, :])

        NSTEP = CHUNKS * EXPERTS
        with (nc.Fori(0, ROUNDS) as r,
              rearmed(nc, "moe_gate_weights", "moe_logits", "moe_shifted", "moe_exp", "moe_gate_chain", "moe_weights",
                      "moe_bias_chain", "moe_up", "moe_gelu", "moe_down", "moe_combined", "moe_acc_chain",
                      "moe_acc_turned", "moe_cur", "moe_cur_high", "moe_cur_split") as
              (gate_w, logits, shifted, exped, chain, weights, bias_chain, up_done, gelu_done, down_done,
               combined, acc_chain, acc_turned, cur_done, cur_high_done, cur_split),
              nc.Block() as block):
            @block.tensor
            def _(pe):
                def up(n):
                    c, e = n // EXPERTS, n % EXPERTS
                    for f in range(FF_TILES):
                        if n:
                            pe.wait_ge(gelu_done, FF_TILES * (n - 1) + f + 1)
                        w = slice(f * P, (f + 1) * P)
                        matmul_split(pe, k.psum[:, f, :], w1_high[:, e, w], w1_low[:, e, w], cur_high[:, cols[c]],
                                     cur_low[:, cols[c]]).then_inc(up_done, 1)

                def down(n):
                    e = n % EXPERTS
                    pe.wait_ge(gelu_done, FF_TILES * (n + 1))
                    if n >= 2:
                        pe.wait_ge(combined, n - 1)
                    for t in range(4):
                        for f in range(FF_TILES):
                            at = slice(t * P, (t + 1) * P)
                            last = pe.matmul(k.psum[:, 4 + n % 2, at], hidden[:, n % 2, f, at], w2[:, e, f, :],
                                             start=f == 0, stop=f == FF_TILES - 1)
                    last.then_inc(down_done, 1)

                def turn(c):
                    pe.wait_ge(combined, EXPERTS * (c + 1))
                    if c >= 2:
                        pe.wait_ge(cur_done, c - 1)
                    for t in range(4):
                        last = pe.transpose(k.psum[:, 6 + c % 2, t * P:(t + 1) * P], acc[:, 4 * c + t, :],
                                            k.ident[:, :])
                    last.then_inc(acc_turned, 1)

                pe.wait_ge(gate_w, 2)
                for t in range(TILES):
                    last = pe.matmul(k.psum[:, 6, t * EXPERTS:(t + 1) * EXPERTS], cur[:, t * P:(t + 1) * P],
                                     wg_r[:, :], start=True, stop=True)
                last.then_inc(logits, 1)
                up(0)
                for n in range(NSTEP):
                    if n + 1 < NSTEP:
                        up(n + 1)
                    down(n)
                    if n % EXPERTS == 0 and n:
                        turn(n // EXPERTS - 1)
                turn(CHUNKS - 1)

            @block.scalar
            def _(act):
                act.wait_ge(shifted, 1)
                act.activation(ex[:, :, :], ex[:, :, :], ACT.Exp).then_inc(exped, 1)
                def take_cur(c):
                    act.wait_ge(acc_turned, c + 1)
                    act.activation(cur[:, cols[c]], k.psum[:, 6 + c % 2, :], ACT.Copy).then_inc(cur_done, 1)

                for n in range(NSTEP):
                    e = n % EXPERTS
                    if n >= 2:
                        act.wait_ge(down_done, n - 1)
                    for f in range(FF_TILES):
                        act.wait_ge(up_done, FF_TILES * n + f + 1)
                        act.activation(hidden[:, n % 2, f, :], k.psum[:, f, :], ACT.Gelu_apprx_tanh,
                                       bias=b1[:, e, f:f + 1]).then_inc(gelu_done, 1)
                    if e == 2 and n > EXPERTS:
                        take_cur(n // EXPERTS - 1)
                take_cur(CHUNKS - 1)

            @block.gpsimd
            def _(pool):
                pool.tensor_copy(wg_r[:, :], wg[:, r, :]).then_inc(gate_w, 1)
                pool.tensor_copy(bg_r[:, :], bg[:, r, :]).then_inc(gate_w, 1)
                def add_bias(c, e, m):
                    tiles = slice(4 * c, 4 * c + 4)
                    dst = bias[:, tiles, :] if e == 0 else bias_e[:, :, :]
                    if m:
                        pool.wait_ge(bias_chain, m)
                    pool.tensor_tensor(dst, b2[:, e, :].unsqueeze(1).broadcast_to([P, 4, DIM]),
                                       weight[:, tiles, e:e + 1].broadcast_to([P, 4, DIM]), ALU.mult)\
                        .then_inc(bias_chain, 1)
                    if e:
                        pool.wait_ge(bias_chain, m + 1)
                        pool.tensor_tensor(bias[:, tiles, :], bias[:, tiles, :], dst, ALU.add).then_inc(bias_chain, 1)

                BIAS_OPS = 2 * EXPERTS - 1
                pool.wait_ge(weights, 1)
                for n in range(NSTEP):
                    c, e = n // EXPERTS, n % EXPERTS
                    add_bias(c, e, BIAS_OPS * c + max(2 * e - 1, 0))

            @block.vector
            def _(dve):
                n = [0]

                def link(ins):
                    n[0] += 1
                    ins.then_inc(chain, 1)
                    dve.wait_ge(chain, n[0])

                dve.wait_ge(logits, 1)
                dve.wait_ge(gate_w, 2)
                link(dve.tensor_tensor(logit[:, :, :],
                                       k.psum[:, 6, 0:TILES * EXPERTS].rearrange("p (t e) -> p t e", e=EXPERTS),
                                       bg_r[:, :].unsqueeze(1).broadcast_to([P, TILES, EXPERTS]), ALU.add))
                link(dve.tensor_reduce(top[:, :], logit[:, :, :], AX.X, ALU.max))
                dve.tensor_tensor(ex[:, :, :], logit[:, :, :], wide(top[:, :].unsqueeze(2)), ALU.subtract)\
                   .then_inc(shifted, 1)
                for e in range(EXPERTS):
                    dve.memset(rank[:, :, e:e + 1], float(EXPERTS - 1 - e)).then_inc(chain, 1)
                    n[0] += 1
                for d in range(1, EXPERTS):
                    m = EXPERTS - d
                    link(dve.tensor_tensor(wins[:, :, 0:m], logit[:, :, 0:m], logit[:, :, d:EXPERTS], ALU.is_ge))
                    link(dve.tensor_tensor(rank[:, :, d:EXPERTS], rank[:, :, d:EXPERTS], wins[:, :, 0:m], ALU.add))
                    link(dve.tensor_tensor(rank[:, :, 0:m], rank[:, :, 0:m], wins[:, :, 0:m], ALU.subtract))
                link(dve.tensor_scalar(rank[:, :, :], rank[:, :, :], 2.0, None, ALU.is_lt))
                dve.wait_ge(exped, 1)
                link(dve.tensor_tensor(ex[:, :, :], ex[:, :, :], rank[:, :, :], ALU.mult))
                link(dve.tensor_reduce(total[:, :], ex[:, :, :], AX.X, ALU.add))
                link(dve.reciprocal(total[:, :], total[:, :]))
                dve.tensor_tensor(weight[:, :, :], ex[:, :, :], wide(total[:, :].unsqueeze(2)), ALU.mult)\
                   .then_inc(weights, 1)
                dve.wait_ge(weights, 1)

                def split_cur(c):
                    dve.wait_ge(cur_done, c + 1)
                    high_part(dve, cur_high[:, cols[c]], cur[:, cols[c]]).then_inc(cur_high_done, 1)
                    dve.wait_ge(cur_high_done, c + 1)
                    low_part(dve, cur_low[:, cols[c]], cur[:, cols[c]], cur_high[:, cols[c]])\
                        .then_inc(cur_split, 1)

                for i in range(NSTEP):
                    c, e = i // EXPERTS, i % EXPERTS
                    dve.wait_ge(down_done, i + 1)
                    if i:
                        dve.wait_ge(combined, i)
                    for t in range(4):
                        tile = 4 * c + t
                        last = dve.scalar_tensor_tensor(acc[:, tile, :], k.psum[:, 4 + i % 2, t * P:(t + 1) * P],
                                                        weight[:, tile, e:e + 1], acc[:, tile, :], ALU.mult, ALU.add)
                        if t < 3 or e == EXPERTS - 1:
                            last.then_inc(acc_chain, 1)
                    if e == EXPERTS - 1:
                        dve.wait_ge(bias_chain, (2 * EXPERTS - 1) * (c + 1))
                        dve.wait_ge(acc_chain, 3 * i + 3 + (c + 1))
                        last = dve.tensor_tensor(acc[:, 4 * c:4 * c + 4, :], acc[:, 4 * c:4 * c + 4, :],
                                                 bias[:, 4 * c:4 * c + 4, :], ALU.add)
                    last.then_inc(combined, 1)
                    if e == 2 and c:
                        split_cur(c - 1)
                split_cur(CHUNKS - 1)

        with nc.Block() as block:
            @block.vector
            def _(dve):
                for c in range(CHUNKS):
                    dve.scalar_tensor_tensor(k.x[:, cols[c]], cur[:, cols[c]], part(1, 5)(c * CHUNK // SEQ),
                                             k.x[:, cols[c]], ALU.mult, ALU.add)


def build(nc, A, out, stages="ABCD"):
    k = Core()
    k.A = A
    with ExitStack() as ctx:
        def sb(name, shape, dt=F32):
            return ctx.enter_context(nc.sbuf_tensor(name, shape, dt))

        k.x = sb("x_ch", [P, TOK])
        k.ident = sb("ident", [P, P])
        k.ident_bf = sb("ident_bf", [P, P], BF16)
        k.ones_mean = sb("ones_mean_sb", [P, P])
        k.c = sb("c_cols", [P, 2 * BATCH])
        k.eps = sb("eps", [P, 1])
        k.mod = sb("mod", [P, 2, 6, BATCH])
        k.psum = ctx.enter_context(nc.psum_tensor("psum", [P, 8, 512], F32))
        k.parts = nc.dram_tensor("qk_parts", (2, 3, BATCH, GROUPS, HEAD_DIM, GROUP, SEQ), BF16).ap()
        k.z = nc.dram_tensor("z_heads", (BATCH, HEADS, SEQ, HEAD_DIM), F32).ap()
        load_residents(nc, k, A)
        modulation(nc, k, A)
        m = k.mod

        def part(l, i):
            return lambda b: m[:, l, i, b:b + 1]

        if "A" in stages:
            with scope(nc), ExitStack() as a:
                k.v_ch = a.enter_context(nc.sbuf_tensor("v_ch0", [P, TOK], F32))
                k.v_tok = a.enter_context(nc.sbuf_tensor("v_tok0", [P, SEQ_TILES, UNITS, 32], F32))
                k.att = a.enter_context(nc.sbuf_tensor("att0", [P, SEQ_TILES, UNITS, 32], F32))
                with nc.sbuf_tensor("h0", [P, TOK], F32) as h:
                    layer_norm(nc, k, "ln0", k.x, h, part(0, 1), part(0, 0))
                    project_heads(nc, k, "rot", h, A, True)
                attention(nc, k, "att0", 1.0 / float(np.sqrt(HEAD_DIM)), False)
                residual_attention(nc, k, "res0", A)
        if "B" in stages:
            with scope(nc):
                windowed_layers(nc, k, A, part)
        if "C" in stages:
            with scope(nc):
                causal_block(nc, k, A, part)
        if "D" in stages:
            with scope(nc):
                experts(nc, k, A, part)
        (stored,) = sems(nc, "x_stored")
        with nc.Block() as block:
            @block.sync
            def _(sp):
                sp.dma_start(out, k.x[:, :]).then_inc(stored, 16)
                sp.wait_ge(stored, 16)


def lay_out(inputs):
    i = {n: np.asarray(a) for n, a in inputs.items()}
    f = np.ascontiguousarray
    A = dict(shape_constants())
    A["x"] = f(i["L0_attn_x"].reshape(TOK, DIM).T)
    A["c"] = f(np.concatenate([i["L0_c"], i["L1_c"]]).T)
    A["wmod0"], A["wmod1"] = i["L0_wmod"], i["L1_wmod"]
    def by_channel(t):
        qk = t[..., :2 * DIM].reshape(t.shape[:-1] + (2, GROUPS, GROUP, HEAD_DIM)).swapaxes(-1, -2)
        return np.concatenate([qk.reshape(t.shape[:-1] + (2 * DIM,)), t[..., 2 * DIM:]], -1)

    A["rot_w"] = f(by_channel(i["L0_attn_w_qkv"].T))
    A["rot_b"] = f(by_channel(i["L0_attn_b_qkv"]).reshape(3, DIM).T)
    A["lepe"] = f(np.concatenate([i["L0_attn_w_lepe"][:, 0, :], i["L0_attn_b_lepe"][:, None]], 1))
    A["plain_w"] = f(by_channel(np.concatenate([i[f"L1_attn_W{n}"].T for n in "qkv"], 1)))
    A["plain_b"] = f(by_channel(np.concatenate([i[f"L1_attn_b{n}"] for n in "qkv"])).reshape(3, DIM).T)
    A["norm_cols"] = f(np.stack([i["L1_attn_gamma"], i["L1_attn_beta"]], 1))
    A["moe_w1"] = f(i["L1_ffn_W1"].transpose(1, 0, 2))
    A["moe_w2"] = f(i["L1_ffn_W2"].reshape(EXPERTS, FF_TILES, P, DIM).transpose(2, 0, 1, 3))
    A["moe_b1"] = f(i["L1_ffn_b1"].reshape(EXPERTS, FF_TILES, P).transpose(2, 0, 1))
    A["moe_b2"] = f(np.broadcast_to(i["L1_ffn_b2"][None], (P, EXPERTS, DIM)))
    A["moe_wg"] = f(i["L1_ffn_Wg"].transpose(1, 0, 2))
    A["moe_bg"] = f(np.broadcast_to(i["L1_ffn_bg"][None], (P, ROUNDS, EXPERTS)))
    rot = (np.arange(W_DIM) + W_DIM // 2) % W_DIM
    wqkv = i["L0_ffn_wqkv"].reshape(DEPTH, DIM, 3, PAIRS, 2, W_DIM)
    turned = wqkv[..., rot]
    five = np.stack([wqkv[:, :, 0], turned[:, :, 0], wqkv[:, :, 1], turned[:, :, 1], wqkv[:, :, 2]], 2)
    five = five.reshape(DEPTH, DIM, 5, PAIRS, P).transpose(0, 3, 1, 2, 4).reshape(DEPTH * PAIRS, DIM, 5, P)
    A["win_wj"] = f(np.concatenate([five, five[-1:]]))
    A["win_wo"] = f(i["L0_ffn_wo"].reshape(DEPTH, PAIRS, P, DIM).transpose(0, 2, 1, 3))
    A["win_w1"] = f(i["L0_ffn_w1"])
    w2 = np.pad(i["L0_ffn_w2"], ((0, 0), (0, 3 * P - HID), (0, 0)))
    A["win_w2"] = f(w2.reshape(DEPTH, 3, P, DIM).transpose(0, 2, 1, 3))
    cols = np.zeros((DEPTH, P, COLS), np.float32)
    for n, name in enumerate(("L0_ffn_q_scale", "L0_ffn_k_scale")):
        cols[:, :, SCALES + 2 * n] = np.tile(i[name], (1, 2))
        cols[:, :, SCALES + 2 * n + 1] = np.tile(i[name][:, rot], (1, 2))
    cols[:, :, LN_G], cols[:, :, LN_B], cols[:, :, B2] = i["L0_ffn_ln_g"], i["L0_ffn_ln_b"], i["L0_ffn_b2"]
    for n, m in enumerate(HID_TILES):
        cols[:, :m, B1_A + n] = i["L0_ffn_b1"][:, n * P:n * P + m]
        cols[:, :m, B1_G + n] = i["L0_ffn_b1"][:, HID + n * P:HID + n * P + m]
    A["win_cols"] = cols
    return A


def kernel(**inputs):
    import concourse.bacc as bacc
    from concourse.bass_utils import run_bass_kernel_spmd

    nc = bacc.Bacc("TRN2", target_bir_lowering=False, num_devices=1)
    arrays = {f"in_{n}": a for n, a in lay_out(inputs).items()}
    A = {n[3:]: nc.dram_tensor(n, a.shape, mybir.dt.from_np(a.dtype), kind="ExternalInput").ap()
         for n, a in arrays.items()}
    out = nc.dram_tensor("out_x", (DIM, TOK), F32, kind="ExternalOutput").ap()
    build(nc, A, out)
    run = run_bass_kernel_spmd(nc, [arrays], core_ids=[0])
    return np.ascontiguousarray(run.results[0]["out_x"].T).reshape(BATCH, SEQ, DIM)
```

```python
from contextlib import ExitStack, contextmanager

import numpy as np

import concourse.bass as bass
import concourse.mybir as mybir

F32 = mybir.dt.float32
BF16 = mybir.dt.bfloat16
F32R = mybir.dt.float32r
ALU = mybir.AluOpType
ACT = mybir.ActivationFunctionType
AX = mybir.AxisListType

P = 128
BATCH, SEQ, DIM = 2, 1024, 128
TOK = BATCH * SEQ
CHUNK = 512
CHUNKS = TOK // CHUNK
TILES = TOK // P
SEQ_TILES = SEQ // P
EPS = 1e-5

HEADS, HEAD_DIM = 16, 8
GROUP = 4
GROUPS = HEADS // GROUP
UNITS = GROUPS * BATCH
SPLIT_ROWS = 9 * HEAD_DIM
ROWS = SPLIT_ROWS + 2
RING = 3

DEPTH, W_HEADS, W_DIM, WINDOW, HID = 2, 8, 64, 64, 341
INNER = W_HEADS * W_DIM
PAIRS = W_HEADS // 2
QK_SCALE = 8.0
KEYS = P + WINDOW
MASKED = -1e37
HID_TILES = (128, 128, 85)

ROUNDS, EXPERTS, FF = 4, 4, 512
FF_TILES = FF // P


def high_part(dve, dst, src):
    return dve.tensor_copy(dst, src)


def low_part(dve, dst, src, high):
    return dve.tensor_tensor(dst, src, high.bitcast(F32), ALU.subtract)


def matmul_split(pe, out, w_high, w_low, x_high, x_low, start=True, stop=True):
    pe.matmul(out, w_high, x_high, start=start, stop=False)
    pe.matmul(out, w_high, x_low, start=False, stop=False)
    return pe.matmul(out, w_low, x_high, start=False, stop=stop)


def shape_constants():
    f = np.float32
    c = {}
    c["identity"] = np.eye(P, dtype=f)
    c["ones_mean"] = np.full((P, P), 1.0 / P, f)
    swap = np.zeros((P, P), f)
    swap[np.arange(P), np.arange(P) ^ GROUP] = 1
    c["pair_swap"] = swap
    pair = np.zeros((P, P), f)
    pair[:W_DIM, :W_DIM] = 1
    pair[W_DIM:, W_DIM:] = 1
    c["head_ones"] = pair
    select = np.zeros((P, EXPERTS, P), f)
    for e in range(EXPERTS):
        select[e:3 * EXPERTS:EXPERTS, e, :] = 1
    c["moe_select"] = select
    half = np.arange(0, HEAD_DIM, 2, dtype=f)
    div = np.exp(half * f(-np.log(10000.0) / HEAD_DIM)).astype(f)
    ang = np.arange(SEQ, dtype=f)[:, None] * div
    cos, sin = np.cos(ang).astype(f), np.sin(ang).astype(f)
    d = np.arange(P) // GROUP % HEAD_DIM
    c["rope_cos"] = np.ascontiguousarray(cos[:, d // 2].T)
    c["rope_sin"] = np.ascontiguousarray((sin[:, d // 2] * np.where(d % 2, 1, -1).astype(f)).T)
    half = np.arange(0, W_DIM, 2, dtype=f)
    inv = (f(1.0) / f(10000.0) ** (half / f(W_DIM))).astype(f)
    t = np.arange(SEQ, dtype=f)
    freqs = t[:, None] * inv[None, :]
    base = ((half + f(0.4 * W_DIM)) / f(1.4 * W_DIM)).astype(f)
    power = (t - SEQ // 2) / f(WINDOW // 2)
    scale = (base[None, :] ** power[:, None]).astype(f)
    cos, sin = np.cos(freqs).astype(f), np.sin(freqs).astype(f)
    d = np.arange(P) % W_DIM
    sign = np.where(d < W_DIM // 2, -1, 1).astype(f)[:, None]
    i = d % (W_DIM // 2)
    c["xpos"] = np.stack([(cos * scale).T[i], (sin * scale).T[i] * sign,
                          (cos / scale).T[i], (sin / scale).T[i] * sign], 1).astype(f)
    q, j = np.arange(P)[:, None], np.arange(KEYS)[None, :]
    band = np.where((j >= q) & (j <= q + WINDOW), 0.0, MASKED).astype(f)
    first = np.where(j < WINDOW, f(MASKED), band).astype(f)
    c["band"] = np.stack([band, first], 1)
    c["triangle"] = np.tril(np.ones((P, P), f))
    return c


class Core:
    pass


def sems(nc, *names):
    return [nc.alloc_semaphore(n) for n in names]


@contextmanager
def scope(nc):
    before = nc.snapshot_sems()
    yield
    nc.clear_and_free_semaphores(nc.allocated_since(before))
    nc.all_engine_barrier()


@contextmanager
def rearmed(nc, *names):
    with scope(nc):
        yield sems(nc, *names)


def prologue(nc, k, A):
    PARTS = 6
    c_in, w_in, ident_in, loaded, silu, mods, exps, chain = sems(
        nc, "c_loaded", "wmod_loaded", "identity_loaded", "residents_loaded", "silu_ready", "mod_ready", "exp_ready",
        "mod_chain")
    ctx = ExitStack()
    with ctx:
        w = ctx.enter_context(nc.sbuf_tensor("wmod", [P, 2, PARTS * DIM], F32))
        e = ctx.enter_context(nc.sbuf_tensor("silu_tmp", [P, 4], F32))
        s = ctx.enter_context(nc.sbuf_tensor("silu_c", [P, 4], F32))
        t = ctx.enter_context(nc.sbuf_tensor("gate_tmp", [P, 2, 2, BATCH], F32))
        ps = k.psum[:, 0, 0:2 * PARTS * BATCH].rearrange("p (l m b) -> p l m b", l=2, b=BATCH)
        block = ctx.enter_context(nc.Block())

        @block.sync
        def _(sp):
            sp.dma_start(k.c[:, :], A["c"]).then_inc(c_in, 16)
            for l in range(2):
                sp.dma_start(w[:, l, :], A[f"wmod{l}"]).then_inc(w_in, 16)
            sp.dma_start(k.ident[:, :], A["identity"]).then_inc(ident_in, 16)
            sp.dma_start(k.ones_mean[:, :], A["ones_mean"]).then_inc(loaded, 16)
            sp.wait_ge(loaded, 32)

        @block.scalar
        def _(act):
            act.dma_start(k.x[:, :], A["x"]).then_inc(loaded, 16)
            act.wait_ge(c_in, 16)
            act.activation(e[:, :], k.c[:, :], ACT.Exp, scale=-1.0).then_inc(exps, 1)

        @block.tensor
        def _(pe):
            pe.wait_ge(w_in, 32)
            pe.wait_ge(silu, 1)
            for l in range(2):
                for m in range(PARTS):
                    last = pe.matmul(ps[:, l, m, :], w[:, l, m * DIM:(m + 1) * DIM],
                                     s[:, l * BATCH:(l + 1) * BATCH], start=True, stop=True)
            last.then_inc(mods, 1)

        @block.vector
        def _(dve):
            n = [0]

            def link(ins):
                n[0] += 1
                ins.then_inc(chain, 1)
                dve.wait_ge(chain, n[0])

            dve.memset(k.eps[:, :], EPS)
            dve.wait_ge(exps, 1)
            link(dve.tensor_scalar(e[:, :], e[:, :], 1.0, None, ALU.add))
            link(dve.reciprocal(e[:, :], e[:, :]))
            dve.tensor_tensor(s[:, :], k.c[:, :], e[:, :], ALU.mult).then_inc(silu, 1)
            dve.wait_ge(mods, 1)
            link(dve.tensor_copy(k.mod[:, :, :, :], ps))
            link(dve.tensor_scalar(k.mod[:, :, 1::3, :], k.mod[:, :, 1::3, :], 1.0, None, ALU.add))
            link(dve.tensor_scalar(t[:, :, :, :], k.mod[:, :, 2::3, :], 0.0, 2.0, ALU.is_ge, ALU.mult))
            link(dve.tensor_scalar(t[:, :, :, :], t[:, :, :, :], -1.0, None, ALU.add))
            link(dve.tensor_tensor(k.mod[:, :, 2::3, :], k.mod[:, :, 2::3, :], t[:, :, :, :], ALU.mult))
            link(dve.tensor_scalar(k.mod[:, :, 2::3, :], k.mod[:, :, 2::3, :], 0.25, None, ALU.max))
            link(dve.tensor_tensor(k.mod[:, :, 2::3, :], k.mod[:, :, 2::3, :], t[:, :, :, :], ALU.mult))
            dve.wait_ge(ident_in, 16)
            dve.tensor_copy(k.ident_bf[:, :], k.ident[:, :])


LN_SEMS = ("mean", "centred", "squared", "var", "rooted", "inverse", "spread", "scaled", "shifted")


def layer_norm(nc, k, tag, src, dst, scale, shift, residual=None, names=sems):
    mean, centred, squared, var, rooted, inverse, spread, scaled, shifted = names(nc, *(f"{tag}_{n}" for n in LN_SEMS))
    ctx = ExitStack()
    with ctx:
        d = ctx.enter_context(nc.sbuf_tensor(f"{tag}_centred_x", [P, TOK], F32))
        sq = ctx.enter_context(nc.sbuf_tensor(f"{tag}_square", [P, TOK], F32))
        dev = ctx.enter_context(nc.sbuf_tensor(f"{tag}_deviation", [P, TILES], F32))
        inv = ctx.enter_context(nc.sbuf_tensor(f"{tag}_inverse", [P, TILES], F32))
        at = [slice(c * CHUNK, (c + 1) * CHUNK) for c in range(CHUNKS)]
        tiles = [slice(4 * c, 4 * c + 4) for c in range(CHUNKS)]
        var_bank = [k.psum[:, 4 + c % 2, 4 * c:4 * c + 4] for c in range(CHUNKS)]
        spread_bank = [k.psum[:, i, :] for i in (6, 7, 0, 1)]
        block = ctx.enter_context(nc.Block())

        @block.tensor
        def _(pe):
            for c in range(CHUNKS):
                pe.matmul(k.psum[:, c, :], k.ones_mean[:, :], src[:, at[c]], start=True, stop=True).then_inc(mean, 1)

            def variance(c):
                pe.wait_ge(squared, c + 1)
                if c >= 2:
                    pe.wait_ge(rooted, c - 1)
                for t in range(4):
                    i = 4 * c + t
                    last = pe.matmul(var_bank[c][:, t:t + 1], sq[:, i * P:(i + 1) * P], k.ones_mean[:, 0:1],
                                     start=True, stop=True)
                last.then_inc(var, 1)

            def spread_inverse(c):
                pe.wait_ge(inverse, c + 1)
                for t in range(4):
                    i = 4 * c + t
                    last = pe.matmul(spread_bank[c][:, t * P:(t + 1) * P], inv[:, i:i + 1].broadcast_to([P, P]),
                                     k.ident[:, :], start=True, stop=True)
                last.then_inc(spread, 1)

            for c in range(CHUNKS + 1):
                if c < CHUNKS:
                    variance(c)
                if c:
                    spread_inverse(c - 1)

        @block.scalar
        def _(act):
            def square(c):
                act.wait_ge(centred, c + 1)
                act.activation(sq[:, at[c]], d[:, at[c]], ACT.Square).then_inc(squared, 1)

            def root(c):
                act.wait_ge(var, c + 1)
                act.activation(dev[:, tiles[c]], var_bank[c], ACT.Sqrt, bias=k.eps[:, 0:1]).then_inc(rooted, 1)

            def add_shift(c):
                act.wait_ge(scaled, c + 1)
                act.activation(dst[:, at[c]], d[:, at[c]], ACT.Identity, bias=shift(c * CHUNK // SEQ))\
                   .then_inc(shifted, 1)

            square(0)
            for c in range(CHUNKS):
                if c + 1 < CHUNKS:
                    square(c + 1)
                root(c)
                if c:
                    add_shift(c - 1)
            add_shift(CHUNKS - 1)

        @block.vector
        def _(dve):
            def centre(c):
                dve.wait_ge(mean, c + 1)
                dve.tensor_tensor(d[:, at[c]], src[:, at[c]], k.psum[:, c, :], ALU.subtract).then_inc(centred, 1)

            def invert(c):
                dve.wait_ge(rooted, c + 1)
                dve.reciprocal(inv[:, tiles[c]], dev[:, tiles[c]]).then_inc(inverse, 1)

            def rescale(c):
                dve.wait_ge(spread, c + 1)
                dve.scalar_tensor_tensor(d[:, at[c]], d[:, at[c]], scale(c * CHUNK // SEQ), spread_bank[c],
                                         ALU.mult, ALU.mult).then_inc(scaled, 1)

            centre(0)
            centre(1)
            for c in range(CHUNKS + 1):
                if c < CHUNKS:
                    invert(c)
                if c + 2 < CHUNKS:
                    centre(c + 2)
                if c:
                    rescale(c - 1)
            if residual:
                x, gate = residual
                for c in range(CHUNKS):
                    dve.wait_ge(shifted, c + 1)
                    dve.scalar_tensor_tensor(x[:, at[c]], dst[:, at[c]], gate(c * CHUNK // SEQ), x[:, at[c]],
                                             ALU.mult, ALU.add)


class OperandRing:

    def __init__(self, nc, k, tag, ctx):
        def tiles(name):
            return [ctx.enter_context(nc.sbuf_tensor(f"{tag}_{name}{r}", [ROWS, GROUP, SEQ], BF16))
                    for r in range(RING)]

        self.parts = k.parts
        self.q, self.k = tiles("q_op"), tiles("k_op")
        self.loaded = sems(nc, *(f"{tag}_operands_loaded{r}" for r in range(RING)))

    def load(self, sp, unit):
        r = unit % RING
        for a in range(3):
            rows = slice(3 * HEAD_DIM * a, 3 * HEAD_DIM * (a + 1))
            part_q = self.parts[0, a, unit // GROUPS, unit % GROUPS].rearrange("d h t -> d (h t)")
            sp.dma_start(self.q[r][rows].rearrange("p h t -> p (h t)"),
                         part_q.unsqueeze(0).broadcast_to([3, HEAD_DIM, GROUP * SEQ])).then_inc(self.loaded[r], 16)
            parts_k = self.parts[1, :, unit // GROUPS, unit % GROUPS].rearrange("c d h t -> c d (h t)")
            sp.dma_start(self.k[r][rows].rearrange("p h t -> p (h t)"), parts_k).then_inc(self.loaded[r], 16)


def project_heads(nc, k, tag, h, A, rotary, operands):
    (w_in, projected, drained, floored, exped, feature, swapped, swap_drained, cosined, sined, operand, hi_done,
     rest1, mid_done, lo_done, stored, v_ps, v_done, v_turned, v_tok_done, v_clean) = sems(nc, *(f"{tag}_{n}" for n in (
        "weights_loaded", "projected", "projection_drained", "floored", "exp_done", "feature_ready", "pair_swapped",
        "swap_drained", "cos_done", "sin_done", "operand_ready", "hi_done", "rest1_done", "mid_done", "lo_done",
        "parts_stored", "v_projected", "v_ready", "v_turned", "v_tok_ready", "v_clean")))
    NU = 2 * CHUNKS
    ctx = ExitStack()
    with ctx:
        def sb(name, shape, dt=F32):
            return ctx.enter_context(nc.sbuf_tensor(f"{tag}_{name}", shape, dt))

        w = sb("w", [P, 3 * DIM])
        bias = sb("b", [P, 3])
        val = sb("val", [P, NU, CHUNK])
        part = [sb(n, [P, 2, TOK], BF16) for n in ("hi", "mid", "lo")]
        if rotary:
            tmp = sb("tmp", [P, NU, CHUNK])
            swap = sb("swap", [P, P])
            cos, sin = sb("cos", [P, SEQ]), sb("sin", [P, SEQ])
        else:
            same = sb("same", [P, TOK])
            vraw = sb("vraw", [P, TOK])
        loads = [(w[:, :], A[f"{tag}_w"]), (bias[:, :], A[f"{tag}_b"])]
        tables = [(swap[:, :], A["pair_swap"]), (cos[:, :], A["rope_cos"]), (sin[:, :], A["rope_sin"])] \
            if rotary else []
        (tables_in,) = sems(nc, f"{tag}_tables_loaded")
        bank = [k.psum[:, i, :] for i in range(8)]
        cols = [slice(c * CHUNK, (c + 1) * CHUNK) for c in range(CHUNKS)]

        def pos(s):
            return slice((s // 2) * CHUNK % SEQ, (s // 2) * CHUNK % SEQ + CHUNK)

        def of(t, s):
            return t[:, s % 2, cols[s // 2]]

        block = ctx.enter_context(nc.Block())

        @block.sync
        def _(sp):
            for dst, src in loads:
                sp.dma_start(dst, src).then_inc(w_in, 16)
            n = 0
            for b in range(BATCH):
                done = NU // BATCH * (b + 1)
                for i, part_done in enumerate((hi_done, mid_done, lo_done)):
                    sp.wait_ge(part_done, done)
                    for which in range(2):
                        sp.dma_start(k.parts[which, i, b].rearrange("g d h t -> (g d h) t"),
                                     part[i][:, which, b * SEQ:(b + 1) * SEQ]).then_inc(stored, 16)
                        n += 1
                if b == 0:
                    sp.wait_ge(stored, 16 * n)
                    operands.load(sp, 0)
            sp.wait_ge(stored, 16 * n)

        @block.tensor
        def _(pe):
            pe.wait_ge(w_in, 16 * len(loads))

            def project(s):
                if s >= 2:
                    pe.wait_ge(drained if rotary else operand, s - 1)
                pe.matmul(bank[s % 2], w[:, (s % 2) * DIM:(s % 2 + 1) * DIM], h[:, cols[s // 2]],
                          start=True, stop=True).then_inc(projected, 1)

            def swap_pairs(s):
                pe.wait_ge(feature, s + 1)
                if s == 0:
                    pe.wait_ge(tables_in, 16 * len(tables))
                if s >= 2:
                    pe.wait_ge(swap_drained, s - 1)
                pe.matmul(bank[2 + s % 2], swap[:, :], val[:, s, :], start=True, stop=True).then_inc(swapped, 1)

            def project_v(c):
                if c >= 2:
                    pe.wait_ge(v_done, c - 1)
                pe.matmul(bank[4 + c % 2], w[:, 2 * DIM:3 * DIM], h[:, cols[c]], start=True, stop=True)\
                    .then_inc(v_ps, 1)

            def turn_v(c):
                pe.wait_ge(v_done if rotary else v_clean, c + 1)
                if c >= 2:
                    pe.wait_ge(v_tok_done, c - 1)
                for t in range(4):
                    last = pe.transpose(bank[6 + c % 2][:, t * P:(t + 1) * P],
                                        k.v_ch[:, c * CHUNK + t * P:c * CHUNK + (t + 1) * P], k.ident[:, :])
                last.then_inc(v_turned, 1)

            for s in range(NU + 2):
                if s < NU:
                    project(s)
                if rotary and s >= 2:
                    swap_pairs(s - 2)
                if s % 2 == 0 and s < NU:
                    project_v(s // 2)
                if s % 2 == 1 and 3 <= s < NU + 2:
                    turn_v((s - 3) // 2)

        @block.scalar
        def _(act):
            for dst, src in tables:
                act.dma_start(dst, src).then_inc(tables_in, 16)
            act.wait_ge(w_in, 16 * len(loads))

            def exp_low(s):
                act.wait_ge(floored, s + 1)
                act.activation(tmp[:, s, :], tmp[:, s, :], ACT.Exp).then_inc(exped, 1)

            def biased(s):
                act.wait_ge(projected, s + 1)
                act.activation(val[:, s, :], bank[s % 2], ACT.Identity, bias=bias[:, s % 2:s % 2 + 1])\
                   .then_inc(operand, 1)

            def hi(s):
                act.wait_ge(operand, s + 1)
                act.activation(of(part[0], s), val[:, s, :], ACT.Copy).then_inc(hi_done, 1)

            def mid(s):
                act.wait_ge(rest1, s + 1)
                act.activation(of(part[1], s), val[:, s, :], ACT.Copy).then_inc(mid_done, 1)

            def v_bias(c):
                act.wait_ge(v_ps, c + 1)
                act.activation((k.v_ch if rotary else vraw)[:, cols[c]], bank[4 + c % 2], ACT.Identity,
                               bias=bias[:, 2:3]).then_inc(v_done, 1)

            def v_tok(c):
                act.wait_ge(v_turned, c + 1)
                b, t0 = c // 2, c % 2 * 4
                act.activation(k.v_tok[:, t0:t0 + 4, b * GROUPS:(b + 1) * GROUPS, :],
                               bank[6 + c % 2].rearrange("p (t g c) -> p t g c", t=4, c=32), ACT.Copy)\
                   .then_inc(v_tok_done, 1)

            for s in range(NU + 4):
                if s < NU:
                    (exp_low if rotary else biased)(s)
                if s % 2 == 0 and s < NU:
                    v_bias(s // 2)
                if 3 <= s < NU + 3:
                    hi(s - 3)
                if s >= 4:
                    mid(s - 4)
                if s % 2 == 1 and 3 <= s < NU + 2:
                    v_tok((s - 3) // 2)

        @block.vector
        def _(dve):
            dve.wait_ge(w_in, 16 * len(loads))

            def ramps(s):
                dve.wait_ge(projected, s + 1)
                b = bias[:, s % 2:s % 2 + 1]
                dve.tensor_scalar(tmp[:, s, :], bank[s % 2], b, 0.0, ALU.add, ALU.min).then_inc(floored, 1)
                dve.tensor_scalar(val[:, s, :], bank[s % 2], b, 0.0, ALU.add, ALU.max).then_inc(drained, 1)

            def times_cos(s):
                dve.wait_ge(feature, s + 1)
                if s == 0:
                    dve.wait_ge(tables_in, 16 * len(tables))
                dve.tensor_tensor(tmp[:, s, :], val[:, s, :], cos[:, pos(s)], ALU.mult).then_inc(cosined, 1)

            def times_sin(s):
                dve.wait_ge(swapped, s + 1)
                dve.wait_ge(cosined, s + 1)
                dve.tensor_tensor(val[:, s, :], bank[2 + s % 2], sin[:, pos(s)], ALU.mult).then_inc(swap_drained, 1)

            def less_hi(s):
                dve.wait_ge(hi_done, s + 1)
                dve.tensor_tensor(val[:, s, :], val[:, s, :], of(part[0], s), ALU.subtract).then_inc(rest1, 1)

            for s in range(NU + 4):
                if rotary and s < NU:
                    ramps(s)
                if rotary and 1 <= s < NU + 1:
                    times_cos(s - 1)
                if rotary and 2 <= s < NU + 2:
                    times_sin(s - 2)
                if s >= 4:
                    less_hi(s - 4)
                if not rotary and s % 2 == 1 and s < NU:
                    c = s // 2
                    dve.wait_ge(v_done, c + 1)
                    dve.tensor_tensor(same[:, cols[c]], vraw[:, cols[c]], vraw[:, cols[c]], ALU.is_equal)\
                       .then_inc(sined, 1)
                    dve.memset(k.v_ch[:, cols[c]], 0.0).then_inc(sined, 1)
                    dve.wait_ge(sined, 2 * c + 2)
                    dve.copy_predicated(k.v_ch[:, cols[c]], same[:, cols[c]].bitcast(mybir.dt.uint32),
                                        vraw[:, cols[c]]).then_inc(v_clean, 1)

        @block.gpsimd
        def _(pool):
            def feature_sum(s):
                pool.wait_ge(exped, s + 1)
                pool.wait_ge(drained, s + 1)
                pool.tensor_tensor(val[:, s, :], val[:, s, :], tmp[:, s, :], ALU.add).then_inc(feature, 1)

            def rotary_sum(s):
                pool.wait_ge(swap_drained, s + 1)
                pool.tensor_tensor(val[:, s, :], val[:, s, :], tmp[:, s, :], ALU.add).then_inc(operand, 1)

            def lo(s):
                pool.wait_ge(mid_done, s + 1)
                pool.tensor_tensor(of(part[2], s), val[:, s, :], of(part[1], s), ALU.subtract).then_inc(lo_done, 1)

            for s in range(NU + 4):
                if rotary and s < NU:
                    feature_sum(s)
                if rotary and 2 <= s < NU + 2:
                    rotary_sum(s - 2)
                if s >= 4:
                    lo(s - 4)


def attention(nc, k, tag, scale, causal, operands, pool_aside=None):
    (ones_set, hm_ready, ring_ready, ring_free, st_ready, exp_done, pv_done,
     v_staged, v_ready0, masked, evacuated, hi_done, rec_done, tri_loaded) = sems(
        nc, *(f"{tag}_{n}" for n in (
            "ones_set", "max_parts_ready", "ring_filled",
            "ring_drained", "scores_ready", "exp_done", "values_added", "v_staged", "v_cleared",
            "diagonal_masked", "sums_evacuated", "max_hi_done", "reciprocal_ready",
            "triangle_loaded")))
    z_stored, ones_made = sems(nc, f"{tag}_z_stored", f"{tag}_ones_made")
    m_rows = sems(nc, *(f"{tag}_max_rows_loaded{half}" for half in range(2)))
    STEPS = 2 * SEQ_TILES
    MAXES = GROUP * SEQ_TILES
    ENTRIES = MAXES + 2 + 2
    FIRST = MAXES + 2
    PB = 4
    ctx = ExitStack()
    with ctx:
        def sb(name, shape, dt=F32):
            return ctx.enter_context(nc.sbuf_tensor(f"{tag}_{name}", shape, dt))

        q_op, k_op, loaded = operands.q, operands.k, operands.loaded
        probs = sb("probs", [P, PB, GROUP, CHUNK])
        stage_v = [sb(f"v1_{r}", [P, SEQ_TILES, GROUP, 32]) for r in range(RING)]
        neg = sb("neg_max", [P, SEQ_TILES, GROUP])
        neg_parts = sb("neg_parts", [P, SEQ_TILES, 2, GROUP], BF16)
        one_rows = sb("one_rows", [2, GROUP, SEQ], BF16)
        neg_rows = sb("neg_rows", [2 * GROUP, SEQ], BF16)
        sums = sb("sums", [P, 2, CHUNK])
        rec = sb("rec", [P, 4, GROUP])
        if causal:
            stage_vo = [sb(f"v0_{r}", [P, SEQ_TILES, GROUP, 32]) for r in range(RING)]
            only_ones = sb("only_ones", [P, 32])
            diag = sb("diag", [P, 2, GROUP, P])
            triangle = sb("triangle", [P, P])
        st_bank = [k.psum[:, i, :] for i in range(3)]
        ring = [k.psum[:, 3 + 2 * i:5 + 2 * i, :].rearrange("p a n -> p (a n)") for i in range(2)]
        out_bank = k.psum[:, 7, :]

        def loop(engine, body):
            body(0, None, 0, 0)
            with engine.Fori(0, (UNITS - 2) // RING) as i:
                for u in range(RING):
                    body(i * RING + (u + 1), i * RING + u, i + (u + 1) // RING, (u + 1) % RING)
            body(UNITS - 1, UNITS - 2, (UNITS - 1) // RING, (UNITS - 1) % RING)

        def is_last(it):
            return isinstance(it, int) and it == UNITS - 1

        def entries(it):
            first, last = isinstance(it, int) and it == 0, is_last(it)
            out = []
            for s in range(STEPS):
                if not last:
                    out += [(s, "max", 2 * s), (s, "max", 2 * s + 1)]
                if s == 1 and not first:
                    out.append((s, "turn", 1))
                if s == 2 and not first:
                    out.append((s, "rows", 1))
                if s == SEQ_TILES + 1:
                    out.append((s, "turn", 0))
                if s == SEQ_TILES + 2 and not last:
                    out.append((s, "rows", 0))
            return out

        def base_of(it):
            return FIRST if isinstance(it, int) and it == 0 else it * ENTRIES + (FIRST - 2)

        def max_at(arg):
            half, rest = arg // (MAXES // 2), arg % (MAXES // 2)
            return rest // 4, 4 * half + rest % 4

        def done(it, kind, arg):
            return base_of(it) + [e[1:] for e in entries(it)].index((kind, arg)) + 1

        block = ctx.enter_context(nc.Block())

        @block.sync
        def _(sp):
            def rows(it, half):
                sp.wait_ge(ring_free, FIRST if it == 0 else done(it, "rows", 1) if half else done(it - 1, "rows", 0))
                sp.dma_start(q_op[it % RING][SPLIT_ROWS:ROWS, :, half * CHUNK:(half + 1) * CHUNK],
                             neg_rows[:, half * CHUNK:(half + 1) * CHUNK]).then_inc(m_rows[half], 16)

            def store_z(it):
                b, g = it // GROUPS, it % GROUPS
                sp.wait_ge(ring_free, done(it, "turn", 0) + 1 if is_last(it) else done(it + 1, "turn", 1))
                for j in range(GROUP):
                    sp.dma_start(k.z[b, g * GROUP + j].rearrange("(t p) d -> p t d", p=P),
                                 k.att[:, :, it, j * HEAD_DIM:(j + 1) * HEAD_DIM]).then_inc(z_stored, 16)

            sp.wait_ge(ones_made, 1)
            for r in range(RING):
                sp.dma_start(k_op[r][SPLIT_ROWS:ROWS], one_rows[:, :, :]).then_inc(ones_set, 16)
            for unit in range(1, RING):
                operands.load(sp, unit)
            rows(0, 0)
            rows(0, 1)
            for it in range(UNITS):
                if it + 1 < UNITS:
                    rows(it + 1, 0)
                if it + RING < UNITS:
                    sp.wait_ge(exp_done, GROUP * STEPS * (it + 1))
                    operands.load(sp, it + RING)
                if it + 1 < UNITS:
                    rows(it + 1, 1)
                if causal:
                    store_z(it)
            if causal:
                sp.wait_ge(z_stored, 16 * GROUP * UNITS)

        @block.tensor
        def _(pe):
            def entry(n, base, kind, arg, it, r=None):
                buf = ring[n % 2]
                if not (isinstance(base, int) and base + n < 2):
                    pe.wait_ge(ring_free, base + n - 1)
                if kind == "max":
                    j, t = max_at(arg)
                    for half in range(2):
                        last = pe.matmul(buf[:, half * CHUNK:(half + 1) * CHUNK],
                                         q_op[r][0:SPLIT_ROWS, j, t * P:(t + 1) * P],
                                         k_op[r][0:SPLIT_ROWS, j, half * CHUNK:(half + 1) * CHUNK],
                                         start=True, stop=True)
                elif kind == "rows":
                    pe.wait_ge(hm_ready, 2 * it + arg + 1)
                    for t in range(4):
                        last = pe.matmul(buf[0:2 * GROUP, t * P:(t + 1) * P],
                                         neg_parts[:, arg * 4 + t, :, :].rearrange("p c h -> p (c h)"),
                                         k.ident_bf[:, :], start=True, stop=True)
                else:
                    pe.wait_ge(evacuated, 2 * it + arg + 1)
                    for t in range(4):
                        last = pe.transpose(buf[:, t * P:(t + 1) * P], sums[:, arg, t * P:(t + 1) * P], k.ident[:, :])
                last.then_inc(ring_ready, 1)

            def score(it, r, s, j):
                half, t = s // SEQ_TILES, s % SEQ_TILES
                e = GROUP * s + j
                if not (isinstance(it, int) and GROUP * STEPS * it + e < 3):
                    pe.wait_ge(exp_done, it * (GROUP * STEPS) + e - 2)
                mm = pe.matmul(st_bank[(r + e) % 3], k_op[r][:, j, t * P:(t + 1) * P],
                               q_op[r][:, j, half * CHUNK:(half + 1) * CHUNK], start=True, stop=True)
                mm.then_inc(st_ready, 1)

            def values(it, r, s):
                half, t = s // SEQ_TILES, s % SEQ_TILES
                pe.wait_ge(exp_done, it * (GROUP * STEPS) + GROUP * (s + 1))
                if s == 0:
                    pe.wait_ge(v_staged, it + 1)
                if t == 0 and not (isinstance(it, int) and 2 * it + half == 0):
                    pe.wait_ge(evacuated, 2 * it + half)
                first, final = t == 0, t == SEQ_TILES - 1
                full = CHUNK if not causal else min(max(t - 4 * half, 0) * P, CHUNK)
                for j in range(GROUP):
                    out = out_bank[32 * j:32 * j + 32, :]
                    pr = probs[:, s % PB, j, :]
                    if full:
                        last = pe.matmul(out[:, 0:full], stage_v[r][:, t, j, :], pr[:, 0:full],
                                         start=first, stop=final and full == CHUNK, skip_group_check=causal)
                    if full < CHUNK:
                        last = pe.matmul(out[:, full:CHUNK], only_ones[:, :], pr[:, full:CHUNK],
                                         start=first, stop=final, skip_group_check=causal)
                if causal and 0 <= t - 4 * half < 4:
                    pe.wait_ge(masked, it * SEQ_TILES + t + 1)
                    at = (t - 4 * half) * P
                    for j in range(GROUP):
                        last = pe.matmul(out_bank[32 * j:32 * j + 32, at:at + P], stage_vo[r][:, t, j, :],
                                         diag[:, t % 2, j, :], start=False, stop=final, skip_group_check=True)
                last.then_inc(pv_done, 1)

            def body(it, before, uses, r):
                base = base_of(it)
                todo = list(enumerate(entries(it)))
                if isinstance(it, int) and it == 0:
                    pe.wait_ge(ones_set, 16 * RING)
                for s in range(STEPS):
                    if s % SEQ_TILES == 0:
                        pe.wait_ge(m_rows[s // SEQ_TILES], 16 * (it + 1))
                    for j in range(GROUP):
                        score(it, r, s, j)
                        if j % 2 == 1 and not is_last(it):
                            n, (_, kind, arg) = todo.pop(0)
                            if n == 0:
                                pe.wait_ge(loaded[(r + 1) % RING], 96 * (uses + (r + 1) // RING + 1))
                            entry(n, base, kind, arg, None, (r + 1) % RING)
                    if s >= 1:
                        values(it, r, s - 1)
                    elif before is not None:
                        values(before, (r - 1) % RING, STEPS - 1)
                    while todo and todo[0][1][0] == s:
                        n, (_, kind, arg) = todo.pop(0)
                        late = (kind, arg) == ("turn", 1)
                        ahead = (kind, arg) == ("rows", 0)
                        entry(n, base, kind, arg, before if late else it + 1 if ahead else it)
                if is_last(it):
                    values(it, r, STEPS - 1)
                    entry(3, base, "turn", 1, it)

            def first():
                pe.wait_ge(loaded[0], 96)
                for n in range(MAXES):
                    entry(n, 0, "max", n, 0, 0)
                entry(MAXES, 0, "rows", 0, 0)
                entry(MAXES + 1, 0, "rows", 1, 0)

            first()
            loop(pe, body)

        @block.scalar
        def _(act):
            def take_sums(it, half):
                act.wait_ge(pv_done, it * STEPS + (half + 1) * SEQ_TILES)
                act.activation(sums[:, half, :], out_bank, ACT.Copy).then_inc(evacuated, 1)

            def body(it, before, uses, r):
                for s in range(STEPS):
                    for j in range(GROUP):
                        e = GROUP * s + j
                        act.wait_ge(st_ready, it * (GROUP * STEPS) + e + 1)
                        if j == 0 and not (isinstance(it, int) and it * STEPS + s < PB):
                            act.wait_ge(pv_done, it * STEPS + s - PB + 1)
                        ins = act.activation(probs[:, s % PB, j, :], st_bank[(r + e) % 3], ACT.Exp, scale=scale)
                        ins.then_inc(exp_done, 1)
                        if j == 0 and s == 1 and before is not None:
                            take_sums(before, 1)
                        if j == 0 and s == SEQ_TILES + 1:
                            take_sums(it, 0)
                if is_last(it):
                    take_sums(it, 1)

            loop(act, body)

        @block.vector
        def _(dve):
            def entry(n, base, kind, arg, it):
                buf = ring[n % 2]
                dve.wait_ge(ring_ready, base + n + 1)
                if kind == "max":
                    j, t = max_at(arg)
                    ins = dve.tensor_reduce(neg[:, t, j:j + 1], buf, AX.X, ALU.max, negate=True)
                    ins.then_inc(ring_free, 1)
                    if (arg + 1) % (MAXES // 2) == 0:
                        half = arg // (MAXES // 2)
                        at = slice(4 * half, 4 * half + 4)
                        dve.wait_ge(ring_free, base + n + 1)
                        dve.tensor_copy(neg_parts[:, at, 0, :], neg[:, at, :]).then_inc(hi_done, 1)
                        dve.wait_ge(hi_done, 2 * it + half + 1)
                        dve.tensor_tensor(neg_parts[:, at, 1, :], neg[:, at, :], neg_parts[:, at, 0, :], ALU.subtract)\
                           .then_inc(hm_ready, 1)
                elif kind == "rows":
                    if not (isinstance(it, int) and it == 0):
                        dve.wait_ge(m_rows[arg], 16 * it)
                    dve.wait_ge(hm_ready, 2 * it + arg + 1)
                    dve.tensor_copy(neg_rows[:, arg * CHUNK:(arg + 1) * CHUNK], buf[0:2 * GROUP, 0:CHUNK])\
                       .then_inc(ring_free, 1)
                else:
                    tile = buf[:, 0:CHUNK].rearrange("p (t h c) -> p t h c", t=4, c=32)
                    if is_last(it):
                        dve.wait_ge(ring_free, base + n)
                    dve.reciprocal(rec[:, :, :], tile[:, :, :, HEAD_DIM]).then_inc(rec_done, 1)
                    dve.wait_ge(rec_done, 2 * it + arg + 1)
                    out = k.att[:, 4 * arg:4 * arg + 4, it, :].rearrange("p t (h c) -> p t h c", c=HEAD_DIM)
                    num = tile[:, :, :, 0:HEAD_DIM]
                    by = rec[:, :, :].unsqueeze(3).broadcast_to([P, 4, GROUP, HEAD_DIM])
                    dve.tensor_tensor(out, num, by, ALU.mult).then_inc(ring_free, 1)

            def body(it, before, uses, r):
                for n, (s, kind, arg) in enumerate(entries(it)):
                    of_unit = it + 1 if kind == "max" or (kind, arg) == ("rows", 0) else \
                        before if (kind, arg) == ("turn", 1) else it
                    entry(n, base_of(it), kind, arg, of_unit)
                if is_last(it):
                    entry(3, base_of(it), "turn", 1, it)

            def first():
                for n in range(MAXES):
                    entry(n, 0, "max", n, 0)
                entry(MAXES, 0, "rows", 0, 0)
                entry(MAXES + 1, 0, "rows", 1, 0)

            first()
            loop(dve, body)

        @block.gpsimd
        def _(pool):
            if causal:
                pool.dma_start(triangle[:, :], k.A["triangle"]).then_inc(tri_loaded, 16)
                pool.wait_ge(tri_loaded, 16)
            pool.memset(one_rows[:, :, :], 1.0).then_inc(ones_made, 1)
            stages = stage_v + (stage_vo if causal else [])
            for t in stages:
                pool.memset(t[:, :, :, :], 0.0).then_inc(v_ready0, 1)
            n = len(stages)
            if causal:
                pool.memset(only_ones[:, :], 0.0).then_inc(v_ready0, 1)
                n += 1
            pool.wait_ge(v_ready0, n)
            for t in stage_v:
                pool.memset(t[:, :, :, HEAD_DIM:HEAD_DIM + 1], 1.0).then_inc(v_ready0, 1)
            n += RING
            if causal:
                pool.memset(only_ones[:, HEAD_DIM:HEAD_DIM + 1], 1.0).then_inc(v_ready0, 1)
                n += 1
            pool.wait_ge(v_ready0, n)

            def stage(it, r):
                src = k.v_tok[:, :, it, :].rearrange("p t (h c) -> p t h c", c=HEAD_DIM)
                if causal:
                    pool.tensor_copy(stage_vo[r][:, :, :, 0:HEAD_DIM], src)
                pool.tensor_copy(stage_v[r][:, :, :, 0:HEAD_DIM], src).then_inc(v_staged, 1)

            def body(it, before, uses, r):
                if not is_last(it):
                    if not (isinstance(it, int) and it == 0):
                        pool.wait_ge(pv_done, it * STEPS)
                    stage(it + 1, (r + 1) % RING)
                if causal:
                    for t in range(SEQ_TILES):
                        s = t if t < 4 else SEQ_TILES + t
                        pool.wait_ge(exp_done, it * (GROUP * STEPS) + GROUP * (s + 1))
                        if not (isinstance(it, int) and it * SEQ_TILES + t < 2):
                            back = t - 2 if t >= 2 else t + 6
                            sb_ = back if back < 4 else SEQ_TILES + back
                            pool.wait_ge(pv_done, (it if t >= 2 else it - 1) * STEPS + sb_ + 1)
                        at = (t % 4) * P
                        pool.tensor_tensor(diag[:, t % 2, :, :], probs[:, s % PB, :, at:at + P],
                                           triangle[:, :].unsqueeze(1).broadcast_to([P, GROUP, P]), ALU.mult)\
                            .then_inc(masked, 1)

            stage(0, 0)
            if pool_aside is not None:
                pool_aside(pool)
            loop(pool, body)


class Lepe:

    def __init__(self, nc, k, A, ctx):
        self.loaded, self.taps_done = sems(nc, "taps_loaded", "taps_done")
        self.tap = ctx.enter_context(nc.sbuf_tensor("lepe_taps", [P, 4], F32))
        self.acc = ctx.enter_context(nc.sbuf_tensor("lepe", [P, BATCH, SEQ], F32))
        self.term = ctx.enter_context(nc.sbuf_tensor("lepe_term", [P, BATCH, SEQ], F32))
        self.v = k.v_ch[:, :].rearrange("p (b n) -> p b n", b=BATCH)
        self.source = A["lepe"]

    def convolve(self, pool):
        tap, acc, term, v = self.tap, self.acc, self.term, self.v
        pool.dma_start(tap[:, :], self.source).then_inc(self.loaded, 16)
        pool.wait_ge(self.loaded, 16)
        pool.tensor_scalar(acc[:, :, :], v, tap[:, 1:2], tap[:, 3:4], ALU.mult, ALU.add).then_inc(self.taps_done, 1)
        n = 1
        for weight, dst, src in ((0, slice(1, SEQ), slice(0, SEQ - 1)), (2, slice(0, SEQ - 1), slice(1, SEQ))):
            pool.wait_ge(self.taps_done, n)
            pool.tensor_scalar(term[:, :, dst], v[:, :, src], tap[:, weight:weight + 1], None, ALU.mult)\
                .then_inc(self.taps_done, 1)
            pool.wait_ge(self.taps_done, n + 1)
            pool.tensor_tensor(acc[:, :, dst], acc[:, :, dst], term[:, :, dst], ALU.add).then_inc(self.taps_done, 1)
            n += 2


def residual_attention(nc, k, tag, lepe):
    turned, drained = sems(nc, f"{tag}_att_turned", f"{tag}_turned_drained")
    gate = lambda b: k.mod[:, 0, 2, b:b + 1]
    acc, x = lepe.acc, k.x[:, :].rearrange("p (b n) -> p b n", b=BATCH)
    with nc.Block() as block:
        @block.tensor
        def _(pe):
            for c in range(CHUNKS):
                b, t0 = c // 2, c % 2 * 4
                for t in range(4):
                    last = pe.transpose(k.psum[:, c, t * P:(t + 1) * P],
                                        k.att[:, t0 + t, b * GROUPS:(b + 1) * GROUPS, :].rearrange("p g c -> p (g c)"),
                                        k.ident[:, :])
                last.then_inc(turned, 1)

        @block.vector
        def _(dve):
            def add_gated(c):
                b, at = c // 2, slice(c % 2 * CHUNK, (c % 2 + 1) * CHUNK)
                dve.wait_ge(drained, c + 1)
                dve.scalar_tensor_tensor(x[:, b, at], acc[:, b, at], gate(b), x[:, b, at], ALU.mult, ALU.add)

            for c in range(CHUNKS):
                b, at = c // 2, slice(c % 2 * CHUNK, (c % 2 + 1) * CHUNK)
                dve.wait_ge(turned, c + 1)
                dve.tensor_tensor(acc[:, b, at], acc[:, b, at], k.psum[:, c, :], ALU.add).then_inc(drained, 1)
                if c:
                    add_gated(c - 1)
            add_gated(CHUNKS - 1)


def windowed_layers(nc, k, A, part):
    with ExitStack() as ctx:
        def sb(name, shape, dt=F32):
            return ctx.enter_context(nc.sbuf_tensor(f"win_{name}", shape, dt))

        s = Core()
        s.y = sb("y", [P, TOK])
        s.h = sb("h", [P, TOK])
        s.h_high, s.h_low = sb("h_high", [P, TOK], F32R), sb("h_low", [P, TOK], F32R)
        s.wj = sb("w_pair", [P, 5, DIM])
        s.wj_high, s.wj_low = sb("w_pair_high", [P, 4, DIM], F32R), sb("w_pair_low", [P, 4, DIM], F32R)
        s.wo = sb("wo", [P, PAIRS, DIM])
        s.w1 = sb("w1", [P, 2 * HID])
        s.w1_high, s.w1_low = sb("w1_high", [P, 2 * HID], F32R), sb("w1_low", [P, 2 * HID], F32R)
        s.w2 = sb("w2", [P, 3, DIM])
        s.cols = sb("cols", [P, COLS])
        s.table = sb("table", [P, 4, SEQ])
        s.head_ones = sb("head_ones", [P, P])
        s.band = sb("band", [P, 2, KEYS])
        s.q = sb("q", [P, TOK])
        s.k_half = [sb(f"k_half{e}", [P, WINDOW + TOK]) for e in range(2)]
        s.v = sb("v", [P, TILES, DIM])
        s.norm = sb("norm", [P, TILES, 2, 2])
        s.q_scale = sb("q_scale", [P, 2, TILES, 2])
        s.o = sb("o", [P, PAIRS, TOK])
        once = [(s.head_ones[:, :], A["head_ones"]), (s.wj[:, :, :], A["win_wj"][0]), (s.band[:, :, :], A["band"]),
                (s.table[:, :, :], A["xpos"])]
        loaded, w_high, s.weights_loaded = sems(nc, "win_constants_loaded", "first_pair_weights_high",
                                                "layer_weights_loaded")
        with nc.Block() as block:
            @block.sync
            def _(sp):
                for dst, src in once:
                    sp.dma_start(dst, src).then_inc(loaded, 16)

            @block.gpsimd
            def _(pool):
                for e in range(2):
                    pool.memset(s.k_half[e][:, :], 0.0)

        layer_norm(nc, k, "ln1", k.x, s.y, part(0, 4), part(0, 3))
        with nc.Block() as block:
            @block.vector
            def _(dve):
                dve.wait_ge(loaded, 16 * len(once))
                split_pair_weights(dve, s, w_high, 0)

        with nc.Fori(0, DEPTH) as l:
            layer_start(nc, s, A, l)
            with nc.Fori(0, PAIRS) as j:
                head_pair(nc, k, s, A, l, j)
            output_projection(nc, k, s, l)
            with rearmed(nc, *(f"ln5_{n}" for n in LN_SEMS)) as own:
                layer_norm(nc, k, "ln5", s.h, s.h, lambda b: s.cols[:, LN_G:LN_G + 1],
                           lambda b: s.cols[:, LN_B:LN_B + 1], names=lambda nc, *names: own)
            geglu(nc, k, s)

        with nc.Block() as block:
            @block.vector
            def _(dve):
                for b in range(BATCH):
                    at = slice(b * SEQ, (b + 1) * SEQ)
                    dve.scalar_tensor_tensor(k.x[:, at], s.y[:, at], part(0, 5)(b), k.x[:, at], ALU.mult, ALU.add)


SCALES, LN_G, LN_B, B2, B1_A, B1_G, COLS = 0, 4, 5, 6, 7, 10, 13


def shift_tokens(dve, s, done=None):
    half = DIM // 2
    y = s.y[:, :].rearrange("p (b n) -> p b n", b=BATCH)
    h = s.h[:, :].rearrange("p (b n) -> p b n", b=BATCH)
    dve.tensor_copy(h[0:half], y[0:half])
    dve.tensor_copy(h[half:P, :, 1:SEQ], y[half:P, :, 0:SEQ - 1])
    last = dve.memset(h[half:P, :, 0:1], 0.0)
    if done is not None:
        last.then_inc(done, 1)


def split_pair_weights(dve, s, high_done, before):
    high_part(dve, s.wj_high[:, :, :], s.wj[:, 0:4, :]).then_inc(high_done, 1)
    dve.wait_ge(high_done, before + 1)
    low_part(dve, s.wj_low[:, :, :], s.wj[:, 0:4, :], s.wj_high[:, :, :])


LAYER_WEIGHTS = 3


def layer_start(nc, s, A, l):
    with rearmed(nc, "cols_loaded", "shifted", "h_high") as (cols_loaded, shifted, high), nc.Block() as block:
        @block.sync
        def _(sp):
            sp.dma_start(s.cols[:, :], A["win_cols"][l]).then_inc(cols_loaded, 16)
            for dst, src in ((s.wo[:, :, :], A["win_wo"][l]), (s.w1[:, :], A["win_w1"][l]),
                             (s.w2[:, :, :], A["win_w2"][l])):
                sp.dma_start(dst, src).then_inc(s.weights_loaded, 16)
            sp.wait_ge(cols_loaded, 16)

        @block.vector
        def _(dve):
            shift_tokens(dve, s, shifted)
            dve.wait_ge(shifted, 1)
            for c in range(CHUNKS):
                at = slice(c * CHUNK, (c + 1) * CHUNK)
                high_part(dve, s.h_high[:, at], s.h[:, at]).then_inc(high, 1)
            for c in range(CHUNKS):
                at = slice(c * CHUNK, (c + 1) * CHUNK)
                dve.wait_ge(high, c + 1)
                low_part(dve, s.h_low[:, at], s.h[:, at], s.h_high[:, at])


def head_pair(nc, k, s, A, l, j):
    NB = 4
    NS = 3
    TURN, VALUES = 3, 5
    with (rearmed(nc, "pair_projected", "pair_squared", "pair_sums", "pair_rooted", "pair_floored", "pair_inverse",
                  "pair_spread", "pair_q_parts", "pair_k_parts", "pair_q_sum", "pair_k_sum", "pair_k_done",
                  "pair_v", "pair_v_done", "pair_q_scale", "win_weights", "win_scores", "win_masked", "win_bias",
                  "win_exp", "win_inverse", "win_scaled", "win_turned", "win_turned_copied", "win_values", "win_out",
                  "win_cleared", "win_weights_high") as
          (projected, squared, sums, rooted, floored, inverse, spread, q_parts, k_parts, q_sum, k_sum, k_done,
           v_ready, v_done, q_scaled, w_next, scores, masked, bias_done, exp_done, sum_inverse, scaled, turned, copied,
           values_done, out_done, cleared, w_high),
          nc.sbuf_tensor("pair_sq", [P, 2, 2, CHUNK], F32) as sq,
          nc.sbuf_tensor("pair_tmp", [P, 2, 4, CHUNK], F32) as tmp,
          nc.sbuf_tensor("pair_first_root", [P, 1], F32) as first_root,
          nc.sbuf_tensor("win_sm", [P, NB, 2, KEYS], F32) as sm,
          nc.sbuf_tensor("win_p", [P, NB, 2, 2 * P], F32) as pr,
          nc.sbuf_tensor("win_pt", [P, NB, 2, 2, P], F32) as pt,
          nc.sbuf_tensor("win_max", [P, TILES, 2], F32) as mx,
          nc.sbuf_tensor("win_nb", [P, TILES, 2], F32) as nb,
          nc.sbuf_tensor("win_rs", [P, TILES, 2], F32) as rs,
          nc.sbuf_tensor("win_ri", [P, TILES, 2], F32) as ri,
          nc.Block() as block):
        cols = [slice(c * CHUNK, (c + 1) * CHUNK) for c in range(CHUNKS)]
        tiles = [slice(4 * c, 4 * c + 4) for c in range(CHUNKS)]
        ORDER = (1, 0, 3, 2)
        sums_bank = k.psum[:, 5, 0:4 * TILES].rearrange("p (t w e) -> p t w e", w=2, e=2)
        spread_bank = k.psum[:, 4, :]

        def s_bank(i):
            return k.psum[:, i % NS, 0:2 * KEYS].rearrange("p (e n) -> p e n", e=2)

        def t_bank(i):
            return k.psum[:, NS + i % NS, :].rearrange("p (e a n) -> p e a n", e=2, a=2)

        def o_bank(i):
            return k.psum[:, 2 * NS + i // 4 % 2, i % 4 * P:(i % 4 + 1) * P]

        def near(i):
            return (1,) if i % SEQ_TILES == 0 else (0, 1)

        @block.sync
        def _(sp):
            sp.wait_ge(v_ready, CHUNKS)
            sp.dma_start(s.wj[:, :, :], A["win_wj"][l * PAIRS + (j + 1)]).then_inc(w_next, 16)
            sp.wait_ge(w_next, 16)

        @block.tensor
        def _(pe):
            def project(c):
                for n, i in enumerate(ORDER):
                    if c:
                        pe.wait_ge(q_parts if i < 2 else k_parts, 2 * (c - 1) + n % 2 + 1)
                    matmul_split(pe, k.psum[:, i, :], s.wj_high[:, i, :], s.wj_low[:, i, :], s.h_high[:, cols[c]],
                                 s.h_low[:, cols[c]]).then_inc(projected, 1)

            def norms(c):
                pe.wait_ge(squared, 2 * c + 2)
                if c:
                    pe.wait_ge(rooted, c)
                for t in range(4):
                    for w in range(2):
                        last = pe.matmul(sums_bank[:, 4 * c + t, w, :], sq[:, c % 2, w, t * P:(t + 1) * P],
                                         s.head_ones[:, 0:P:W_DIM], start=True, stop=True)
                last.then_inc(sums, 1)

            def project_values(c):
                if c >= 2:
                    pe.wait_ge(v_done, c - 1)
                for t in range(4):
                    i = 4 * c + t
                    last = pe.matmul(k.psum[:, 6 + c % 2, t * P:(t + 1) * P], s.h[:, i * P:(i + 1) * P],
                                     s.wj[:, 4, :], start=True, stop=True)
                last.then_inc(v_ready, 1)

            def spread_inverse(c):
                pe.wait_ge(inverse, c + 1)
                if c:
                    pe.wait_ge(k_done, 2 * c)
                for t in range(4):
                    for e in range(2):
                        last = pe.matmul(spread_bank[e * W_DIM:(e + 1) * W_DIM, t * P:(t + 1) * P],
                                         s.norm[:, 4 * c + t, 1, e:e + 1].broadcast_to([P, W_DIM]),
                                         k.ident[:, :], start=True, stop=True)
                last.then_inc(spread, 1)

            project(0)
            project_values(0)
            for c in range(CHUNKS):
                if c + 1 < CHUNKS:
                    project(c + 1)
                norms(c)
                if c + 1 < CHUNKS:
                    project_values(c + 1)
                spread_inverse(c)

            def score(i):
                if i % 4 == 0:
                    pe.wait_ge(q_sum, i // 4 + 1)
                    pe.wait_ge(k_done, 2 * (i // 4 + 1))
                if i >= NS:
                    pe.wait_ge(masked, 2 * (i - NS + 1))
                for e in range(2):
                    last = pe.matmul(s_bank(i)[:, e, :], s.q[:, i * P:(i + 1) * P],
                                     s.k_half[e][:, i * P:i * P + KEYS], start=True, stop=True)
                last.then_inc(scores, 1)

            def turn(i):
                pe.wait_ge(scaled, i + 1)
                if i >= NS:
                    pe.wait_ge(copied, i - NS + 1)
                for e in range(2):
                    for a in near(i):
                        last = pe.transpose(t_bank(i)[:, e, a, :], pr[:, i % NB, e, a * P:(a + 1) * P], k_ident)
                last.then_inc(turned, 1)

            def values(i):
                pe.wait_ge(copied, i + 1)
                if i % 4 == 0 and i >= 8:
                    pe.wait_ge(out_done, i // 4 - 1)
                for e in range(2):
                    for a in near(i):
                        last = pe.matmul(o_bank(i)[e * W_DIM:(e + 1) * W_DIM, :],
                                         s.v[:, i - 1 + a, e * W_DIM:(e + 1) * W_DIM], pt[:, i % NB, e, a, :],
                                         start=a == near(i)[0], stop=a == 1)
                last.then_inc(values_done, 1)

            k_ident = k.ident[:, :]
            pe.wait_ge(q_parts, 2 * CHUNKS)
            pe.wait_ge(k_parts, 2 * CHUNKS)
            for i in range(TILES + VALUES):
                if i < TILES:
                    score(i)
                if i == TURN:
                    pe.wait_ge(k_done, 2 * CHUNKS)
                    pe.wait_ge(rooted, CHUNKS)
                if TURN <= i < TILES + TURN:
                    turn(i - TURN)
                if i == VALUES:
                    pe.wait_ge(v_done, CHUNKS)
                if i >= VALUES:
                    values(i - VALUES)

        @block.scalar
        def _(act):
            def squares(c):
                if c >= 2:
                    act.wait_ge(sums, c - 1)
                for i in range(2):
                    act.wait_ge(projected, 4 * c + 2 * i + 2)
                    act.activation(sq[:, c % 2, i, :], k.psum[:, 2 * i, :], ACT.Square).then_inc(squared, 1)

            def root(c):
                act.wait_ge(sums, c + 1)
                act.activation(s.norm[:, tiles[c], :, :], sums_bank[:, tiles[c], :, :], ACT.Sqrt).then_inc(rooted, 1)

            def take_values(c):
                act.wait_ge(v_ready, c + 1)
                act.activation(s.v[:, tiles[c], :],
                               k.psum[:, 6 + c % 2, :].rearrange("p (t n) -> p t n", t=4), ACT.Copy)\
                   .then_inc(v_done, 1)

            act.activation(first_root[:, :], k.eps[:, :], ACT.Sqrt)
            squares(0)
            for c in range(CHUNKS):
                take_values(c)
                if c + 1 < CHUNKS:
                    squares(c + 1)
                root(c)

            def copy_turned(i):
                act.wait_ge(turned, i + 1)
                if i >= NB:
                    act.wait_ge(values_done, i - NB + 1)
                a = near(i)[0]
                act.activation(pt[:, i % NB, :, a:2, :], t_bank(i)[:, :, a:2, :], ACT.Copy).then_inc(copied, 1)

            for i in range(TILES + TURN):
                if i < TILES:
                    act.wait_ge(bias_done, i + 1)
                    if i == 0:
                        act.wait_ge(cleared, 1)
                    if i >= NB:
                        act.wait_ge(turned, i - NB + 1)
                    for e in range(2):
                        act.activation(pr[:, i % NB, e, WINDOW:2 * P], sm[:, i % NB, e, :], ACT.Exp,
                                       bias=nb[:, i, e:e + 1], scale=s.q_scale[:, 0, i, e:e + 1],
                                       accum_out=rs[:, i, e:e + 1]).then_inc(exp_done, 1)
                if i >= TURN:
                    copy_turned(i - TURN)

        @block.vector
        def _(dve):
            def parts(c, which):
                at = slice(c * CHUNK % SEQ, c * CHUNK % SEQ + CHUNK)
                if c >= 2:
                    if which == 0:
                        dve.wait_ge(q_sum, c - 1)
                    else:
                        dve.wait_ge(k_done, 2 * (c - 1))
                for n, i in list(enumerate(ORDER))[2 * which:2 * which + 2]:
                    dve.wait_ge(projected, 4 * c + n + 1)
                    if i % 2 == 0:
                        dve.wait_ge(squared, 2 * c + i // 2 + 1)
                    dve.scalar_tensor_tensor(tmp[:, c % 2, i, :], k.psum[:, i, :], s.cols[:, SCALES + i:SCALES + i + 1],
                                             s.table[:, i, at], ALU.mult, ALU.mult)\
                       .then_inc(q_parts if i < 2 else k_parts, 1)

            def invert(c):
                dve.wait_ge(rooted, c + 1)
                at = s.norm[:, tiles[c], :, :]
                dve.tensor_scalar(at, at, 1e-12, None, ALU.max).then_inc(floored, 1)
                dve.wait_ge(floored, c + 1)
                dve.reciprocal(at, at).then_inc(inverse, 1)

            def divide_k(c):
                dve.wait_ge(spread, c + 1)
                dve.wait_ge(k_sum, c + 1)
                for e in range(2):
                    rows = slice(e * W_DIM, (e + 1) * W_DIM)
                    dve.tensor_tensor(s.k_half[e][rows, WINDOW + c * CHUNK:WINDOW + (c + 1) * CHUNK],
                                      tmp[rows, c % 2, 2, :], spread_bank[rows, :], ALU.mult).then_inc(k_done, 1)

            parts(0, 0)
            parts(0, 1)
            for c in range(CHUNKS):
                if c + 1 < CHUNKS:
                    parts(c + 1, 0)
                invert(c)
                if c + 1 < CHUNKS:
                    parts(c + 1, 1)
                divide_k(c)
            dve.wait_ge(inverse, CHUNKS)
            for i, v in enumerate((QK_SCALE, -QK_SCALE)):
                dve.tensor_scalar(s.q_scale[:, i, :, :], s.norm[:, :, 0, :], v, None, ALU.mult).then_inc(q_scaled, 1)
            dve.wait_ge(q_scaled, 2)

            def mask(i):
                dve.wait_ge(scores, i + 1)
                if i >= NB:
                    dve.wait_ge(exp_done, 2 * (i - NB + 1))
                for e in range(2):
                    dve.tensor_tensor_reduce(sm[:, i % NB, e, :], s_bank(i)[:, e, :],
                                             s.band[:, int(i % SEQ_TILES == 0), :], 1.0, MASKED * 10,
                                             ALU.add, ALU.max, mx[:, i, e:e + 1]).then_inc(masked, 1)
                dve.wait_ge(masked, 2 * i + 2)
                dve.tensor_tensor(nb[:, i, :], mx[:, i, :], s.q_scale[:, 1, i, :], ALU.mult).then_inc(bias_done, 1)

            def invert(i):
                dve.wait_ge(exp_done, 2 * i + 2)
                dve.reciprocal(ri[:, i, :], rs[:, i, :]).then_inc(sum_inverse, 1)

            def take_out(n):
                dve.wait_ge(values_done, 4 * n + 4)
                dve.tensor_copy(s.o[:, j, n * CHUNK:(n + 1) * CHUNK], k.psum[:, 2 * NS + n % 2, :]).then_inc(out_done, 1)

            for i in range(TILES + 1):
                if i < TILES:
                    mask(i)
                if i:
                    invert(i - 1)
                if i >= 3 + VALUES and (i - 3 - VALUES) % 4 == 0:
                    take_out((i - 3 - VALUES) // 4)
            dve.wait_ge(w_next, 16)
            split_pair_weights(dve, s, w_high, 0)
            take_out(3)

        @block.gpsimd
        def _(pool):
            for c in range(CHUNKS):
                pool.wait_ge(q_parts, 2 * c + 2)
                pool.tensor_tensor(s.q[:, cols[c]], tmp[:, c % 2, 0, :], tmp[:, c % 2, 1, :], ALU.add)\
                    .then_inc(q_sum, 1)
                pool.wait_ge(k_parts, 2 * c + 2)
                pool.tensor_tensor(tmp[:, c % 2, 2, :], tmp[:, c % 2, 2, :], tmp[:, c % 2, 3, :], ALU.add)\
                    .then_inc(k_sum, 1)

            pool.memset(pr[:, :, :, 0:WINDOW], 0.0).then_inc(cleared, 1)
            for i in range(TILES):
                pool.wait_ge(sum_inverse, i + 1)
                if i == 0:
                    pool.wait_ge(cleared, 1)
                pool.tensor_tensor(pr[:, i % NB, :, WINDOW:2 * P], pr[:, i % NB, :, WINDOW:2 * P],
                                   ri[:, i, :].unsqueeze(2).broadcast_to([P, 2, KEYS]), ALU.mult).then_inc(scaled, 1)


def output_projection(nc, k, s, l):
    with rearmed(nc, "wo_ready", "wo_added", "w1_high") as (ready, added, high), nc.Block() as block:
        @block.tensor
        def _(pe):
            pe.wait_ge(s.weights_loaded, 16 * LAYER_WEIGHTS * (l + 1))
            for c in range(CHUNKS):
                for j in range(PAIRS):
                    last = pe.matmul(k.psum[:, c, :], s.wo[:, j, :], s.o[:, j, c * CHUNK:(c + 1) * CHUNK],
                                     start=j == 0, stop=j == PAIRS - 1)
                last.then_inc(ready, 1)

        @block.vector
        def _(dve):
            dve.wait_ge(s.weights_loaded, 16 * LAYER_WEIGHTS * (l + 1))
            high_part(dve, s.w1_high[:, :], s.w1[:, :]).then_inc(high, 1)
            dve.wait_ge(high, 1)
            low_part(dve, s.w1_low[:, :], s.w1[:, :], s.w1_high[:, :])
            for c in range(CHUNKS):
                at = slice(c * CHUNK, (c + 1) * CHUNK)
                dve.wait_ge(ready, c + 1)
                dve.tensor_tensor(s.y[:, at], s.y[:, at], k.psum[:, c, :], ALU.add).then_inc(added, 1)
            dve.wait_ge(added, CHUNKS)
            shift_tokens(dve, s)


def geglu(nc, k, s):
    NT = len(HID_TILES)
    with (rearmed(nc, "ffn_h_high", "ffn_h_split", "ffn_a", "ffn_g", "ffn_gelu", "ffn_gated", "ffn_out", "ffn_added") as
          (high, split, a_ready, g_ready, gelu_done, gated, out_ready, added),
          nc.sbuf_tensor("ffn_gelu_x", [P, 2, NT, CHUNK], F32) as gelu,
          nc.sbuf_tensor("ffn_hidden", [P, 2, NT, CHUNK], F32) as hid,
          nc.Block() as block):
        @block.tensor
        def _(pe):
            def up_product(c, i, m, first):
                w, at = slice(first + i * P, first + i * P + m), slice(c * CHUNK, (c + 1) * CHUNK)
                return matmul_split(pe, k.psum[0:m, i if first == 0 else 3 + i, :], s.w1_high[:, w], s.w1_low[:, w],
                                    s.h_high[:, at], s.h_low[:, at])

            def up(c):
                pe.wait_ge(split, c + 1)
                for i, m in enumerate(HID_TILES):
                    if c:
                        pe.wait_ge(gelu_done, NT * (c - 1) + i + 1)
                    up_product(c, i, m, HID).then_inc(g_ready, 1)
                for i, m in enumerate(HID_TILES):
                    if c:
                        pe.wait_ge(gated, NT * (c - 1) + i + 1)
                    up_product(c, i, m, 0).then_inc(a_ready, 1)

            def down(c):
                pe.wait_ge(gated, NT * (c + 1))
                if c >= 2:
                    pe.wait_ge(added, c - 1)
                for i, m in enumerate(HID_TILES):
                    last = pe.matmul(k.psum[:, 6 + c % 2, :], s.w2[0:m, i, :], hid[0:m, c % 2, i, :],
                                     start=i == 0, stop=i == NT - 1)
                last.then_inc(out_ready, 1)

            up(0)
            for c in range(CHUNKS):
                if c + 1 < CHUNKS:
                    up(c + 1)
                down(c)

        @block.scalar
        def _(act):
            for c in range(CHUNKS):
                for i, m in enumerate(HID_TILES):
                    act.wait_ge(g_ready, NT * c + i + 1)
                    if c >= 2:
                        act.wait_ge(gated, NT * (c - 2) + i + 1)
                    act.activation(gelu[0:m, c % 2, i, :], k.psum[0:m, 3 + i, :], ACT.Gelu,
                                   bias=s.cols[0:m, B1_G + i:B1_G + i + 1]).then_inc(gelu_done, 1)

        @block.vector
        def _(dve):
            def split_h(c):
                at = slice(c * CHUNK, (c + 1) * CHUNK)
                high_part(dve, s.h_high[:, at], s.h[:, at]).then_inc(high, 1)
                dve.wait_ge(high, c + 1)
                low_part(dve, s.h_low[:, at], s.h[:, at], s.h_high[:, at]).then_inc(split, 1)

            split_h(0)
            split_h(1)
            for c in range(CHUNKS + 1):
                if c + 2 < CHUNKS:
                    split_h(c + 2)
                if c < CHUNKS:
                    for i, m in enumerate(HID_TILES):
                        dve.wait_ge(a_ready, NT * c + i + 1)
                        dve.wait_ge(gelu_done, NT * c + i + 1)
                        if c >= 2:
                            dve.wait_ge(out_ready, c - 1)
                        dve.scalar_tensor_tensor(hid[0:m, c % 2, i, :], k.psum[0:m, i, :],
                                                 s.cols[0:m, B1_A + i:B1_A + i + 1], gelu[0:m, c % 2, i, :],
                                                 ALU.add, ALU.mult).then_inc(gated, 1)
                if c:
                    at = slice((c - 1) * CHUNK, c * CHUNK)
                    dve.wait_ge(out_ready, c)
                    dve.scalar_tensor_tensor(s.y[:, at], k.psum[:, 6 + (c - 1) % 2, :], s.cols[:, B2:B2 + 1],
                                             s.y[:, at], ALU.add, ALU.add).then_inc(added, 1)


def add_heads(nc, k, tag, h, once):
    loaded = sems(nc, *(f"{tag}_z_loaded{c}" for c in range(CHUNKS)))
    once_loaded, cleared, same_done, z_done, turned = sems(nc, *(f"{tag}_{n}" for n in (
        "once_loaded", "z_cleared", "z_compared", "z_guarded", "z_turned")))
    with (nc.sbuf_tensor(f"{tag}_z_raw", [P, TILES, DIM], F32) as raw,
          nc.sbuf_tensor(f"{tag}_z_same", [P, TILES, DIM], F32) as same,
          nc.sbuf_tensor(f"{tag}_z_tok", [P, TILES, DIM], F32) as z, nc.Block() as block):
        tiles = [slice(4 * c, 4 * c + 4) for c in range(CHUNKS)]

        @block.sync
        def _(sp):
            rows = k.z.rearrange("b h (n q) d -> (b h n) (q d)", q=DIM // HEAD_DIM)
            rows = rows.rearrange("(t p) c -> p t c", p=P)
            for c in range(CHUNKS):
                sp.dma_start(raw[:, tiles[c], :], rows[:, tiles[c], :]).then_inc(loaded[c], 16)
            sp.dma_start(*once).then_inc(once_loaded, 16)
            sp.wait_ge(once_loaded, 16)

        @block.tensor
        def _(pe):
            for c in range(CHUNKS):
                pe.wait_ge(z_done, c + 1)
                for t in range(4):
                    last = pe.transpose(k.psum[:, c, t * P:(t + 1) * P], z[:, 4 * c + t, :], k.ident[:, :])
                last.then_inc(turned, 1)

        @block.vector
        def _(dve):
            dve.memset(z[:, :, :], 0.0).then_inc(cleared, 1)
            for c in range(CHUNKS + 1):
                if c < CHUNKS:
                    dve.wait_ge(loaded[c], 16)
                    dve.tensor_tensor(same[:, tiles[c], :], raw[:, tiles[c], :], raw[:, tiles[c], :], ALU.is_equal)\
                       .then_inc(same_done, 1)
                    dve.wait_ge(same_done, c + 1)
                    dve.wait_ge(cleared, 1)
                    dve.copy_predicated(z[:, tiles[c], :], same[:, tiles[c], :].bitcast(mybir.dt.uint32),
                                        raw[:, tiles[c], :]).then_inc(z_done, 1)
                if c:
                    at = slice((c - 1) * CHUNK, c * CHUNK)
                    dve.wait_ge(turned, c)
                    dve.tensor_tensor(h[:, at], h[:, at], k.psum[:, c - 1, :], ALU.add)


def causal_block(nc, k, A, part):
    with ExitStack() as a:
        k.v_ch = a.enter_context(nc.sbuf_tensor("v_ch1", [P, TOK], F32))
        k.v_tok = a.enter_context(nc.sbuf_tensor("v_tok1", [P, SEQ_TILES, UNITS, 32], F32))
        k.att = a.enter_context(nc.sbuf_tensor("att1", [P, SEQ_TILES, UNITS, 32], F32))
        h = a.enter_context(nc.sbuf_tensor("h1", [P, TOK], F32))
        norm = a.enter_context(nc.sbuf_tensor("norm_cols", [P, 2], F32))
        layer_norm(nc, k, "ln2", k.x, h, part(1, 1), part(1, 0))
        with ExitStack() as ring:
            operands = OperandRing(nc, k, "att1", ring)
            project_heads(nc, k, "plain", h, A, False, operands)
            attention(nc, k, "att1", 1.0 / float(np.sqrt(SEQ)), True, operands)
        add_heads(nc, k, "z", h, (norm[:, :], A["norm_cols"]))
        layer_norm(nc, k, "ln3", h, h, lambda b: norm[:, 0:1], lambda b: norm[:, 1:2], residual=(k.x, part(1, 2)))


def experts(nc, k, A, part):
    with ExitStack() as ctx:
        def sb(name, shape, dt=F32):
            return ctx.enter_context(nc.sbuf_tensor(f"moe_{name}", shape, dt))

        W_PARTS = 3
        W_ROWS = W_PARTS * EXPERTS
        cur = sb("cur", [P, TOK])
        w1 = sb("w1", [P, EXPERTS, FF])
        w2 = sb("w2", [P, EXPERTS, FF_TILES, DIM])
        b1 = sb("b1", [P, EXPERTS, FF_TILES])
        b2 = sb("b2", [P, EXPERTS])
        wg = sb("wg", [P, ROUNDS, EXPERTS])
        bg = sb("bg", [P, ROUNDS, EXPERTS])
        select32 = sb("select32", [P, EXPERTS, P])
        select = sb("select", [P, EXPERTS, P], BF16)
        rows = sb("weight_rows", [P, 2, CHUNK], BF16)
        cur_high, cur_low = sb("cur_high", [P, TOK], F32R), sb("cur_low", [P, TOK], F32R)
        w1_high, w1_low = sb("w1_high", [P, EXPERTS, FF], F32R), sb("w1_low", [P, EXPERTS, FF], F32R)
        w2_high = sb("w2_high", [P, EXPERTS, FF_TILES, DIM], F32R)
        w2_low = sb("w2_low", [P, EXPERTS, FF_TILES, DIM], F32R)
        hidden = sb("hidden", [P, 2, FF_TILES, CHUNK])
        hidden_high = sb("hidden_high", [P, 2, FF_TILES, CHUNK], F32R)
        hidden_low = sb("hidden_low", [P, 2, FF_TILES, CHUNK], F32R)
        spread_w = sb("spread_weights", [P, 2, CHUNK])
        term = sb("term", [P, 2, CHUNK])
        wg_r = sb("wg_round", [P, EXPERTS])
        bg_r = sb("bg_round", [P, EXPERTS])
        logit = sb("logit", [P, TILES, EXPERTS])
        top = sb("top", [P, TILES])
        ex = sb("exp", [P, TILES, EXPERTS])
        rank = sb("rank", [P, TILES, EXPERTS])
        wins = sb("wins", [P, TILES, EXPERTS])
        weight = sb("weight", [P, TILES, EXPERTS])
        w_parts = sb("weight_parts", [P, TILES, W_PARTS, EXPERTS], BF16)
        total = sb("total", [P, TILES])
        cols = [slice(c * CHUNK, (c + 1) * CHUNK) for c in range(CHUNKS)]

        def wide(ap):
            return ap.broadcast_to([P, TILES, EXPERTS])

        loads = [(w1[:, :, :], A["moe_w1"]), (w2[:, :, :, :], A["moe_w2"]), (b1[:, :, :], A["moe_b1"]),
                 (b2[:, :], A["moe_b2"]), (wg[:, :, :], A["moe_wg"]), (bg[:, :, :], A["moe_bg"]),
                 (select32[:, :, :], A["moe_select"])]
        loaded, first_high, w2_high_done = sems(nc, "moe_loaded", "moe_first_high", "moe_w2_high")
        with nc.Block() as block:
            @block.sync
            def _(sp):
                for dst, src in loads:
                    sp.dma_start(dst, src).then_inc(loaded, 16)

            @block.gpsimd
            def _(pool):
                pool.memset(rows[:, :, :], 0.0)

        layer_norm(nc, k, "ln4", k.x, cur, part(1, 4), part(1, 3))
        with nc.Block() as block:
            @block.vector
            def _(dve):
                high_part(dve, cur_high[:, :], cur[:, :]).then_inc(first_high, 1)
                dve.wait_ge(loaded, 16 * len(loads))
                high_part(dve, w1_high[:, :, :], w1[:, :, :]).then_inc(first_high, 1)
                dve.wait_ge(first_high, 2)
                low_part(dve, cur_low[:, :], cur[:, :], cur_high[:, :])
                low_part(dve, w1_low[:, :, :], w1[:, :, :], w1_high[:, :, :])

            @block.gpsimd
            def _(pool):
                pool.wait_ge(loaded, 16 * len(loads))
                pool.tensor_copy(select[:, :, :], select32[:, :, :])
                pool.wait_ge(w2_high_done, 1)
                pool.tensor_tensor(w2_low[:, :, :, :], w2[:, :, :, :], w2_high[:, :, :, :].bitcast(F32), ALU.subtract)

            @block.scalar
            def _(act):
                act.wait_ge(loaded, 16 * len(loads))
                act.activation(w2_high[:, :, :, :], w2[:, :, :, :], ACT.Copy).then_inc(w2_high_done, 1)

        NSTEP = CHUNKS * EXPERTS
        BY_DVE = FF_TILES - 1
        with (nc.Fori(0, ROUNDS) as r,
              rearmed(nc, "moe_gate_weights", "moe_logits", "moe_shifted", "moe_exp", "moe_gate_chain", "moe_weights",
                      "moe_parts", "moe_weights_turned", "moe_rows", "moe_spread", "moe_spread_copied", "moe_up", "moe_gelu", "moe_down",
                      "moe_weighted", "moe_added", "moe_cur_high", "moe_cur_split", "moe_hidden_high",
                      "moe_hidden_low", "moe_hidden_low_last") as
              (gate_w, logits, shifted, exped, chain, weights, parts, turned, rows_done, spread, copied, up_done, gelu_done,
               down_done, weighted, added, cur_high_done, cur_split, high_done, low_done, low_last),
              nc.Block() as block):
            @block.tensor
            def _(pe):
                def up(n):
                    c, e = n // EXPERTS, n % EXPERTS
                    for f in range(FF_TILES):
                        if n:
                            pe.wait_ge(gelu_done, FF_TILES * (n - 1) + f + 1)
                        w = slice(f * P, (f + 1) * P)
                        matmul_split(pe, k.psum[:, f, :], w1_high[:, e, w], w1_low[:, e, w], cur_high[:, cols[c]],
                                     cur_low[:, cols[c]]).then_inc(up_done, 1)

                def down(n):
                    e = n % EXPERTS
                    if n >= 2:
                        pe.wait_ge(weighted, n - 1)
                    for f in range(FF_TILES):
                        if f < BY_DVE:
                            pe.wait_ge(low_done, BY_DVE * n + f + 1)
                        else:
                            pe.wait_ge(low_last, n + 1)
                        last = matmul_split(pe, k.psum[:, 4 + n % 2, :], w2_high[:, e, f, :], w2_low[:, e, f, :],
                                            hidden_high[:, n % 2, f, :], hidden_low[:, n % 2, f, :],
                                            start=f == 0, stop=f == FF_TILES - 1)
                    last.then_inc(down_done, 1)

                def turn_weights(c):
                    pe.wait_ge(parts, W_PARTS)
                    if c:
                        pe.wait_ge(rows_done, c)
                    for t in range(4):
                        last = pe.matmul(k.psum[0:W_ROWS, 6, t * P:(t + 1) * P],
                                         w_parts[:, 4 * c + t, :, :].rearrange("p a e -> p (a e)"),
                                         k.ident_bf[:, :], start=True, stop=True)
                    last.then_inc(turned, 1)

                def spread_weights(n):
                    c, e = n // EXPERTS, n % EXPERTS
                    if e == 0:
                        pe.wait_ge(rows_done, c + 1)
                    if n:
                        pe.wait_ge(copied, n)
                    pe.matmul(k.psum[:, 7, :], select[:, e, :], rows[:, c % 2, :], start=True, stop=True)\
                      .then_inc(spread, 1)

                up(0)
                pe.wait_ge(gate_w, 2)
                for t in range(TILES):
                    last = pe.matmul(k.psum[:, 6, t * EXPERTS:(t + 1) * EXPERTS], cur[:, t * P:(t + 1) * P],
                                     wg_r[:, :], start=True, stop=True)
                last.then_inc(logits, 1)
                for n in range(NSTEP):
                    if n != 1 and n + 1 < NSTEP:
                        up(n + 1)
                    if n % EXPERTS == 2 and n + 2 < NSTEP:
                        turn_weights(n // EXPERTS + 1)
                    if n:
                        spread_weights(n)
                    down(n)
                    if n == 0:
                        up(2)
                        turn_weights(0)
                        spread_weights(0)

            @block.scalar
            def _(act):
                def take_rows(c):
                    act.wait_ge(turned, c + 1)
                    if c >= 2:
                        act.wait_ge(spread, EXPERTS * (c - 1))
                    act.activation(rows[0:W_ROWS, c % 2, :], k.psum[0:W_ROWS, 6, :], ACT.Copy).then_inc(rows_done, 1)

                def copy_spread(n):
                    act.wait_ge(spread, n + 1)
                    if n >= 2:
                        act.wait_ge(weighted, n - 1)
                    act.activation(spread_w[:, n % 2, :], k.psum[:, 7, :], ACT.Copy).then_inc(copied, 1)

                for n in range(NSTEP):
                    e = n % EXPERTS
                    if n >= 2:
                        act.wait_ge(low_done, BY_DVE * (n - 1))
                        act.wait_ge(low_last, n - 1)
                    for f in range(FF_TILES):
                        act.wait_ge(up_done, FF_TILES * n + f + 1)
                        act.activation(hidden[:, n % 2, f, :], k.psum[:, f, :], ACT.Gelu_apprx_tanh,
                                       bias=b1[:, e, f:f + 1]).then_inc(gelu_done, 1)
                    if n == 0:
                        act.wait_ge(shifted, 1)
                        act.activation(ex[:, :, :], ex[:, :, :], ACT.Exp).then_inc(exped, 1)
                    if n == 1:
                        take_rows(0)
                    if n:
                        copy_spread(n - 1)
                    if e == 3 and n + 1 < NSTEP:
                        take_rows(n // EXPERTS + 1)
                copy_spread(NSTEP - 1)

            @block.gpsimd
            def _(pool):
                pool.tensor_copy(wg_r[:, :], wg[:, r, :]).then_inc(gate_w, 1)
                pool.tensor_copy(bg_r[:, :], bg[:, r, :]).then_inc(gate_w, 1)

                def add_term(n):
                    at = cols[n // EXPERTS]
                    pool.wait_ge(weighted, n + 1)
                    if n % EXPERTS:
                        pool.wait_ge(added, n)
                    pool.tensor_tensor(cur[:, at], cur[:, at], term[:, n % 2, :], ALU.add).then_inc(added, 1)

                for n in range(NSTEP + 1):
                    if n < NSTEP:
                        f = FF_TILES - 1
                        pool.wait_ge(high_done, FF_TILES * (n + 1))
                        pool.tensor_tensor(hidden_low[:, n % 2, f, :], hidden[:, n % 2, f, :],
                                           hidden_high[:, n % 2, f, :].bitcast(F32), ALU.subtract).then_inc(low_last, 1)
                    if n:
                        add_term(n - 1)

            @block.vector
            def _(dve):
                n = [0]

                def link(ins):
                    n[0] += 1
                    ins.then_inc(chain, 1)
                    dve.wait_ge(chain, n[0])

                def split_hidden(i):
                    if i >= 2:
                        dve.wait_ge(down_done, i - 1)
                    for f in range(FF_TILES):
                        dve.wait_ge(gelu_done, FF_TILES * i + f + 1)
                        high_part(dve, hidden_high[:, i % 2, f, :], hidden[:, i % 2, f, :]).then_inc(high_done, 1)
                        if f:
                            lower(i, f - 1)

                def lower(i, f):
                    dve.wait_ge(high_done, FF_TILES * i + f + 1)
                    low_part(dve, hidden_low[:, i % 2, f, :], hidden[:, i % 2, f, :], hidden_high[:, i % 2, f, :])\
                        .then_inc(low_done, 1)

                split_hidden(0)
                dve.wait_ge(logits, 1)
                dve.wait_ge(gate_w, 2)
                link(dve.tensor_tensor(logit[:, :, :],
                                       k.psum[:, 6, 0:TILES * EXPERTS].rearrange("p (t e) -> p t e", e=EXPERTS),
                                       bg_r[:, :].unsqueeze(1).broadcast_to([P, TILES, EXPERTS]), ALU.add))
                link(dve.tensor_reduce(top[:, :], logit[:, :, :], AX.X, ALU.max))
                dve.tensor_tensor(ex[:, :, :], logit[:, :, :], wide(top[:, :].unsqueeze(2)), ALU.subtract)\
                   .then_inc(shifted, 1)
                for e in range(EXPERTS):
                    dve.memset(rank[:, :, e:e + 1], float(EXPERTS - 1 - e)).then_inc(chain, 1)
                    n[0] += 1
                for d in range(1, EXPERTS):
                    m = EXPERTS - d
                    link(dve.tensor_tensor(wins[:, :, 0:m], logit[:, :, 0:m], logit[:, :, d:EXPERTS], ALU.is_ge))
                    link(dve.tensor_tensor(rank[:, :, d:EXPERTS], rank[:, :, d:EXPERTS], wins[:, :, 0:m], ALU.add))
                    link(dve.tensor_tensor(rank[:, :, 0:m], rank[:, :, 0:m], wins[:, :, 0:m], ALU.subtract))
                link(dve.tensor_scalar(rank[:, :, :], rank[:, :, :], 2.0, None, ALU.is_lt))
                dve.wait_ge(exped, 1)
                link(dve.tensor_tensor(ex[:, :, :], ex[:, :, :], rank[:, :, :], ALU.mult))
                link(dve.tensor_reduce(total[:, :], ex[:, :, :], AX.X, ALU.add))
                link(dve.reciprocal(total[:, :], total[:, :]))
                link(dve.tensor_tensor(weight[:, :, :], ex[:, :, :], wide(total[:, :].unsqueeze(2)), ALU.mult))
                for a in range(W_PARTS):
                    dve.tensor_copy(w_parts[:, :, a, :], weight[:, :, :]).then_inc(parts, 1)
                    if a + 1 < W_PARTS:
                        dve.wait_ge(parts, a + 1)
                        link(dve.tensor_tensor(weight[:, :, :], weight[:, :, :], w_parts[:, :, a, :], ALU.subtract))

                def weigh(i):
                    dve.wait_ge(down_done, i + 1)
                    dve.wait_ge(copied, i + 1)
                    if i >= 2:
                        dve.wait_ge(added, i - 1)
                    dve.scalar_tensor_tensor(term[:, i % 2, :], k.psum[:, 4 + i % 2, :],
                                             b2[:, i % EXPERTS:i % EXPERTS + 1], spread_w[:, i % 2, :],
                                             ALU.add, ALU.mult).then_inc(weighted, 1)

                def split_cur(c):
                    dve.wait_ge(added, EXPERTS * (c + 1))
                    high_part(dve, cur_high[:, cols[c]], cur[:, cols[c]]).then_inc(cur_high_done, 1)
                    dve.wait_ge(cur_high_done, c + 1)
                    low_part(dve, cur_low[:, cols[c]], cur[:, cols[c]], cur_high[:, cols[c]]).then_inc(cur_split, 1)

                for i in range(NSTEP):
                    if i + 1 < NSTEP:
                        split_hidden(i + 1)
                    weigh(i)
                    if i % EXPERTS == 2 and i > EXPERTS:
                        split_cur(i // EXPERTS - 1)
                split_cur(CHUNKS - 1)

        with nc.Block() as block:
            @block.vector
            def _(dve):
                for c in range(CHUNKS):
                    dve.scalar_tensor_tensor(k.x[:, cols[c]], cur[:, cols[c]], part(1, 5)(c * CHUNK // SEQ),
                                             k.x[:, cols[c]], ALU.mult, ALU.add)


def build(nc, A, out, stages="ABCD"):
    k = Core()
    k.A = A
    with ExitStack() as ctx:
        def sb(name, shape, dt=F32):
            return ctx.enter_context(nc.sbuf_tensor(name, shape, dt))

        k.x = sb("x_ch", [P, TOK])
        k.ident = sb("ident", [P, P])
        k.ident_bf = sb("ident_bf", [P, P], BF16)
        k.ones_mean = sb("ones_mean_sb", [P, P])
        k.c = sb("c_cols", [P, 2 * BATCH])
        k.eps = sb("eps", [P, 1])
        k.mod = sb("mod", [P, 2, 6, BATCH])
        k.psum = ctx.enter_context(nc.psum_tensor("psum", [P, 8, 512], F32))
        k.parts = nc.dram_tensor("qk_parts", (2, 3, BATCH, GROUPS, HEAD_DIM, GROUP, SEQ), BF16).ap()
        k.z = nc.dram_tensor("z_heads", (BATCH, HEADS, SEQ, HEAD_DIM), F32).ap()
        prologue(nc, k, A)
        m = k.mod

        def part(l, i):
            return lambda b: m[:, l, i, b:b + 1]

        if "A" in stages:
            with scope(nc), ExitStack() as a:
                k.v_ch = a.enter_context(nc.sbuf_tensor("v_ch0", [P, TOK], F32))
                k.v_tok = a.enter_context(nc.sbuf_tensor("v_tok0", [P, SEQ_TILES, UNITS, 32], F32))
                k.att = a.enter_context(nc.sbuf_tensor("att0", [P, SEQ_TILES, UNITS, 32], F32))
                lepe = Lepe(nc, k, A, a)
                with ExitStack() as ring:
                    operands = OperandRing(nc, k, "att0", ring)
                    with nc.sbuf_tensor("h0", [P, TOK], F32) as h:
                        layer_norm(nc, k, "ln0", k.x, h, part(0, 1), part(0, 0))
                        project_heads(nc, k, "rot", h, A, True, operands)
                    attention(nc, k, "att0", 1.0 / float(np.sqrt(HEAD_DIM)), False, operands, lepe.convolve)
                residual_attention(nc, k, "res0", lepe)
        if "B" in stages:
            with scope(nc):
                windowed_layers(nc, k, A, part)
        if "C" in stages:
            with scope(nc):
                causal_block(nc, k, A, part)
        if "D" in stages:
            with scope(nc):
                experts(nc, k, A, part)
        (stored,) = sems(nc, "x_stored")
        with nc.Block() as block:
            @block.sync
            def _(sp):
                sp.dma_start(out, k.x[:, :]).then_inc(stored, 16)
                sp.wait_ge(stored, 16)


def lay_out(inputs):
    i = {n: np.asarray(a) for n, a in inputs.items()}
    f = np.ascontiguousarray
    A = dict(shape_constants())
    A["x"] = f(i["L0_attn_x"].reshape(TOK, DIM).T)
    A["c"] = f(np.concatenate([i["L0_c"], i["L1_c"]]).T)
    A["wmod0"], A["wmod1"] = i["L0_wmod"], i["L1_wmod"]
    def by_channel(t):
        qk = t[..., :2 * DIM].reshape(t.shape[:-1] + (2, GROUPS, GROUP, HEAD_DIM)).swapaxes(-1, -2)
        return np.concatenate([qk.reshape(t.shape[:-1] + (2 * DIM,)), t[..., 2 * DIM:]], -1)

    A["rot_w"] = f(by_channel(i["L0_attn_w_qkv"].T))
    A["rot_b"] = f(by_channel(i["L0_attn_b_qkv"]).reshape(3, DIM).T)
    A["lepe"] = f(np.concatenate([i["L0_attn_w_lepe"][:, 0, :], i["L0_attn_b_lepe"][:, None]], 1))
    A["plain_w"] = f(by_channel(np.concatenate([i[f"L1_attn_W{n}"].T for n in "qkv"], 1)))
    A["plain_b"] = f(by_channel(np.concatenate([i[f"L1_attn_b{n}"] for n in "qkv"])).reshape(3, DIM).T)
    A["norm_cols"] = f(np.stack([i["L1_attn_gamma"], i["L1_attn_beta"]], 1))
    A["moe_w1"] = f(i["L1_ffn_W1"].transpose(1, 0, 2))
    A["moe_w2"] = f(i["L1_ffn_W2"].reshape(EXPERTS, FF_TILES, P, DIM).transpose(2, 0, 1, 3))
    A["moe_b1"] = f(i["L1_ffn_b1"].reshape(EXPERTS, FF_TILES, P).transpose(2, 0, 1))
    A["moe_b2"] = f(i["L1_ffn_b2"].T)
    A["moe_wg"] = f(i["L1_ffn_Wg"].transpose(1, 0, 2))
    A["moe_bg"] = f(np.broadcast_to(i["L1_ffn_bg"][None], (P, ROUNDS, EXPERTS)))
    rot = (np.arange(W_DIM) + W_DIM // 2) % W_DIM
    wqkv = i["L0_ffn_wqkv"].reshape(DEPTH, DIM, 3, PAIRS, 2, W_DIM)
    turned = wqkv[..., rot]
    five = np.stack([wqkv[:, :, 0], turned[:, :, 0], wqkv[:, :, 1], turned[:, :, 1], wqkv[:, :, 2]], 2)
    five = five.reshape(DEPTH, DIM, 5, PAIRS, P).transpose(0, 3, 1, 2, 4).reshape(DEPTH * PAIRS, DIM, 5, P)
    A["win_wj"] = f(np.concatenate([five, five[-1:]]))
    A["win_wo"] = f(i["L0_ffn_wo"].reshape(DEPTH, PAIRS, P, DIM).transpose(0, 2, 1, 3))
    A["win_w1"] = f(i["L0_ffn_w1"])
    w2 = np.pad(i["L0_ffn_w2"], ((0, 0), (0, 3 * P - HID), (0, 0)))
    A["win_w2"] = f(w2.reshape(DEPTH, 3, P, DIM).transpose(0, 2, 1, 3))
    cols = np.zeros((DEPTH, P, COLS), np.float32)
    for n, name in enumerate(("L0_ffn_q_scale", "L0_ffn_k_scale")):
        cols[:, :, SCALES + 2 * n] = np.tile(i[name], (1, 2))
        cols[:, :, SCALES + 2 * n + 1] = np.tile(i[name][:, rot], (1, 2))
    cols[:, :, LN_G], cols[:, :, LN_B], cols[:, :, B2] = i["L0_ffn_ln_g"], i["L0_ffn_ln_b"], i["L0_ffn_b2"]
    for n, m in enumerate(HID_TILES):
        cols[:, :m, B1_A + n] = i["L0_ffn_b1"][:, n * P:n * P + m]
        cols[:, :m, B1_G + n] = i["L0_ffn_b1"][:, HID + n * P:HID + n * P + m]
    A["win_cols"] = cols
    return A


def kernel(**inputs):
    import concourse.bacc as bacc
    from concourse.bass_utils import run_bass_kernel_spmd

    nc = bacc.Bacc("TRN2", target_bir_lowering=False, num_devices=1)
    arrays = {f"in_{n}": a for n, a in lay_out(inputs).items()}
    A = {n[3:]: nc.dram_tensor(n, a.shape, mybir.dt.from_np(a.dtype), kind="ExternalInput").ap()
         for n, a in arrays.items()}
    out = nc.dram_tensor("out_x", (DIM, TOK), F32, kind="ExternalOutput").ap()
    build(nc, A, out)
    run = run_bass_kernel_spmd(nc, [arrays], core_ids=[0])
    return np.ascontiguousarray(run.results[0]["out_x"].T).reshape(BATCH, SEQ, DIM)
```
